# Optimizing a Trainium2 kernel written in Bass

```python
import numpy as np
import jax
import jax.numpy as jnp

def _softmax(x, axis=-1):
    return jax.nn.softmax(x, axis=axis)

def _gelu(x):
    return jax.nn.gelu(x, approximate=True)

def _silu(x):
    return jax.nn.silu(x)

def _sigmoid(x):
    return jax.nn.sigmoid(x)

def _layernorm(x, axis=-1, eps=1e-05):
    m = jnp.mean(x, axis=axis, keepdims=True)
    v = jnp.var(x, axis=axis, keepdims=True)
    return (x - m) / jnp.sqrt(v + eps)

def _scatter_add(tgt, idx, src, axis=0):
    return tgt.at[idx].add(src)

def _segment_sum(src, seg, n):
    return jax.ops.segment_sum(src, seg, n)
kernel_name = 'mk_vit_tower_cls_d1_tok_img768_r4_fa77b8'

def setup_inputs(seed: int=0):
    np.random.seed(seed)
    _w = jnp.asarray

    def _rec_inputs():
        import jax
        import jax.numpy as jnp
        _rk = jax.random.key(seed)
        x = -0.00016672 + 0.999947 * jax.random.normal(jax.random.fold_in(_rk, 1), (64, 64, 64, 3), jnp.float32)
        cls_tok = 0.02 * jax.random.normal(jax.random.fold_in(_rk, 5), (1, 1, 192), jnp.float32)
        return (x, cls_tok)
    x, cls_tok = _rec_inputs()

    def _L0_tok_setup():
        import jax, jax.numpy as jnp
        import numpy as np
        PATCH = 16
        EMBED = 192
        key = jax.random.key(seed)
        k1, k2 = jax.random.split(key)
        images = jax.random.normal(k1, (64, 96, 96, 3), dtype=jnp.float32)
        patch_dim = PATCH * PATCH * 3
        W = jax.random.normal(k2, (patch_dim, EMBED), dtype=jnp.float32) * patch_dim ** (-0.5)
        b = jnp.zeros((EMBED,), dtype=jnp.float32)
        return {'images': images, 'W': W, 'b': b}
    _L0_tok_all = _L0_tok_setup()
    _L0_tok_in = {k: v for k, v in _L0_tok_all.items() if k in ('W', 'b')}
    del _L0_tok_all

    def _L0_attn_setup():
        import jax, jax.numpy as jnp
        import numpy as np
        NUM_HEADS = 12
        BITS_W = 8
        BITS_A = 8
        BITS_S = 4
        EPS = 1.1920928955078125e-07

        def fq_weight(w):
            qmin, qmax = (-2 ** (BITS_W - 1), 2 ** (BITS_W - 1) - 1)
            mn = jnp.minimum(w.min(axis=1, keepdims=True), 0.0)
            mx = jnp.maximum(w.max(axis=1, keepdims=True), 0.0)
            scale = jnp.maximum((mx - mn) / float(qmax - qmin), EPS)
            zp = qmin - jnp.round(mn / scale)
            wq = jnp.clip(jnp.round(w / scale) + zp, qmin, qmax)
            return (wq - zp) * scale

        def fq_act(x):
            qmin, qmax = (-2 ** (BITS_A - 1), 2 ** (BITS_A - 1) - 1)
            mn = jnp.minimum(x.min(), 0.0)
            mx = jnp.maximum(x.max(), 0.0)
            scale = jnp.maximum((mx - mn) / float(qmax - qmin), EPS)
            zp = qmin - jnp.round(mn / scale)
            xq = jnp.clip(jnp.round(x / scale) + zp, qmin, qmax)
            return ((xq - zp) * scale, scale)

        def int_log_softmax(x, scale):
            x_int = x / scale
            x_int = x_int - x_int.max(axis=-1, keepdims=True)
            x0, n = (-0.6931, 30)
            x0_int = jnp.floor(x0 / scale)
            x_int = jnp.maximum(x_int, n * x0_int)
            q = jnp.floor(x_int / x0_int)
            r = x_int - x0_int * q
            c0 = 0.35815147
            b_int = jnp.floor(0.96963238 / c0 / scale)
            c_int = jnp.floor(1.0 / c0 / (scale * scale))
            z = r * (r + b_int) + c_int
            exp_int = jnp.clip(jnp.floor(z * jnp.exp2(n - q)), 0.0, None)
            exp_sum = exp_int.sum(axis=-1, keepdims=True)
            sm = jnp.round(exp_sum / exp_int)
            big = jnp.floor(jnp.log2(sm))
            big = jnp.where(sm - jnp.exp2(big) >= jnp.exp2(big - 1.0), big + 1.0, big)
            mask = big >= float(2 ** BITS_S)
            qlog = jnp.clip(big, 0.0, float(2 ** BITS_S - 1))
            return jnp.where(mask, 0.0, jnp.exp2(-qlog))
        key = jax.random.key(seed)
        ks = jax.random.split(key, 5)
        B, N, C = (16, 577, 192)
        return {'x': jax.random.normal(ks[0], (B, N, C), jnp.float32), 'w_qkv': jax.random.normal(ks[1], (3 * C, C), jnp.float32) * 0.02, 'b_qkv': jax.random.normal(ks[2], (3 * C,), jnp.float32) * 0.02, 'w_proj': jax.random.normal(ks[3], (C, C), jnp.float32) * 0.02, 'b_proj': jax.random.normal(ks[4], (C,), jnp.float32) * 0.02}
    _L0_attn_all = _L0_attn_setup()
    _L0_attn_in = {k: v for k, v in _L0_attn_all.items() if k in ('w_qkv', 'b_qkv', 'w_proj', 'b_proj')}
    del _L0_attn_all

    def _L0_ffn_setup():
        import jax, jax.numpy as jnp
        import numpy as np
        B, S, D, F, E = (4, 512, 192, 768, 8)
        key = jax.random.key(seed)
        ks = jax.random.split(key, 5)
        return {'x': jax.random.normal(ks[0], (B, S, D), dtype=jnp.float32), 'Ws': jax.random.normal(ks[1], (D, E), dtype=jnp.float32) * 0.02, 'bs': jnp.zeros((E,), dtype=jnp.float32), 'W1': jax.random.normal(ks[2], (E, D, F), dtype=jnp.float32) * 0.02, 'b1': jnp.zeros((E, F), dtype=jnp.float32), 'W2': jax.random.normal(ks[3], (E, F, D), dtype=jnp.float32) * 0.02, 'b2': jnp.zeros((E, D), dtype=jnp.float32)}
    _L0_ffn_all = _L0_ffn_setup()
    _L0_ffn_in = {k: v for k, v in _L0_ffn_all.items() if k in ('Ws', 'bs', 'W1', 'b1', 'W2', 'b2')}
    del _L0_ffn_all
    return {'x': x, 'cls_tok': cls_tok, 'L0_tok_W': _L0_tok_in['W'], 'L0_tok_b': _L0_tok_in['b'], 'L0_attn_w_qkv': _L0_attn_in['w_qkv'], 'L0_attn_b_qkv': _L0_attn_in['b_qkv'], 'L0_attn_w_proj': _L0_attn_in['w_proj'], 'L0_attn_b_proj': _L0_attn_in['b_proj'], 'L0_ffn_Ws': _L0_ffn_in['Ws'], 'L0_ffn_bs': _L0_ffn_in['bs'], 'L0_ffn_W1': _L0_ffn_in['W1'], 'L0_ffn_b1': _L0_ffn_in['b1'], 'L0_ffn_W2': _L0_ffn_in['W2'], 'L0_ffn_b2': _L0_ffn_in['b2']}

def reference(x, cls_tok, L0_tok_W, L0_tok_b, L0_attn_w_qkv, L0_attn_b_qkv, L0_attn_w_proj, L0_attn_b_proj, L0_ffn_Ws, L0_ffn_bs, L0_ffn_W1, L0_ffn_b1, L0_ffn_W2, L0_ffn_b2):
    import jax
    import jax.numpy as jnp

    def _L0_tok_ref(images, W, b):
        import jax, jax.numpy as jnp
        import numpy as np
        PATCH = 16
        EMBED = 192
        B, H, Wd, C = images.shape
        p = PATCH
        hp, wp = (H // p, Wd // p)
        x = images.reshape(B, hp, p, wp, p, C)
        x = x.transpose(0, 1, 3, 2, 4, 5)
        x = x.reshape(B, hp * wp, p * p * C)
        return jnp.einsum('bnd,de->bne', x, W) + b

    def _L0_attn_ref(x, w_qkv, b_qkv, w_proj, b_proj):
        import jax, jax.numpy as jnp
        import numpy as np
        NUM_HEADS = 12
        BITS_W = 8
        BITS_A = 8
        BITS_S = 4
        EPS = 1.1920928955078125e-07

        def fq_weight(w):
            qmin, qmax = (-2 ** (BITS_W - 1), 2 ** (BITS_W - 1) - 1)
            mn = jnp.minimum(w.min(axis=1, keepdims=True), 0.0)
            mx = jnp.maximum(w.max(axis=1, keepdims=True), 0.0)
            scale = jnp.maximum((mx - mn) / float(qmax - qmin), EPS)
            zp = qmin - jnp.round(mn / scale)
            wq = jnp.clip(jnp.round(w / scale) + zp, qmin, qmax)
            return (wq - zp) * scale

        def fq_act(x):
            qmin, qmax = (-2 ** (BITS_A - 1), 2 ** (BITS_A - 1) - 1)
            mn = jnp.minimum(x.min(), 0.0)
            mx = jnp.maximum(x.max(), 0.0)
            scale = jnp.maximum((mx - mn) / float(qmax - qmin), EPS)
            zp = qmin - jnp.round(mn / scale)
            xq = jnp.clip(jnp.round(x / scale) + zp, qmin, qmax)
            return ((xq - zp) * scale, scale)

        def int_log_softmax(x, scale):
            x_int = x / scale
            x_int = x_int - x_int.max(axis=-1, keepdims=True)
            x0, n = (-0.6931, 30)
            x0_int = jnp.floor(x0 / scale)
            x_int = jnp.maximum(x_int, n * x0_int)
            q = jnp.floor(x_int / x0_int)
            r = x_int - x0_int * q
            c0 = 0.35815147
            b_int = jnp.floor(0.96963238 / c0 / scale)
            c_int = jnp.floor(1.0 / c0 / (scale * scale))
            z = r * (r + b_int) + c_int
            exp_int = jnp.clip(jnp.floor(z * jnp.exp2(n - q)), 0.0, None)
            exp_sum = exp_int.sum(axis=-1, keepdims=True)
            sm = jnp.round(exp_sum / exp_int)
            big = jnp.floor(jnp.log2(sm))
            big = jnp.where(sm - jnp.exp2(big) >= jnp.exp2(big - 1.0), big + 1.0, big)
            mask = big >= float(2 ** BITS_S)
            qlog = jnp.clip(big, 0.0, float(2 ** BITS_S - 1))
            return jnp.where(mask, 0.0, jnp.exp2(-qlog))
        B, N, C = x.shape
        H = NUM_HEADS
        hd = C // H
        attn_scale = hd ** (-0.5)
        y = x @ fq_weight(w_qkv).T + b_qkv
        y, _ = fq_act(y)
        qkv = y.reshape(B, N, 3, H, hd).transpose(2, 0, 3, 1, 4)
        q, k, v = (qkv[0], qkv[1], qkv[2])
        attn = jnp.einsum('bhnd,bhmd->bhnm', q, k) * attn_scale
        attn, s_attn = fq_act(attn)
        attn = int_log_softmax(attn, s_attn)
        o = jnp.einsum('bhnm,bhmd->bhnd', attn, v)
        o = o.transpose(0, 2, 1, 3).reshape(B, N, C)
        o, _ = fq_act(o)
        o = o @ fq_weight(w_proj).T + b_proj
        o, _ = fq_act(o)
        return o

    def _L0_ffn_ref(x, Ws, bs, W1, b1, W2, b2):
        import jax, jax.numpy as jnp
        import numpy as np
        B, S, D, F, E = (4, 512, 192, 768, 8)
        b, s, d = x.shape
        xt = x.reshape(-1, d)
        logits = xt @ Ws + bs
        probs = jax.nn.softmax(logits, axis=-1)
        routes = jnp.argmax(probs, axis=-1)
        prob_max = jnp.max(probs, axis=-1)
        h = jax.nn.gelu(jnp.einsum('td,edf->etf', xt, W1) + b1[:, None, :], approximate=False)
        y = jnp.einsum('etf,efd->etd', h, W2) + b2[:, None, :]
        out = jnp.take_along_axis(y, routes[None, :, None], axis=0)[0]
        out = out * prob_max[:, None]
        return out.reshape(b, s, d)
    h = _L0_tok_ref(x, L0_tok_W, L0_tok_b)
    h = jnp.concatenate([jnp.broadcast_to(cls_tok, (h.shape[0], 1, h.shape[2])), h], axis=1)
    h = h + _L0_attn_ref(_layernorm(h, axis=-1), L0_attn_w_qkv, L0_attn_b_qkv, L0_attn_w_proj, L0_attn_b_proj)
    h = h + _L0_ffn_ref(_layernorm(h, axis=-1), L0_ffn_Ws, L0_ffn_bs, L0_ffn_W1, L0_ffn_b1, L0_ffn_W2, L0_ffn_b2)
    return h

_drawn_inputs = setup_inputs


def setup_inputs(seed=0):
    import zlib

    import numpy as np

    out = dict(_drawn_inputs(seed))
    spreads = {'L0_tok_b': (0.0, 0.1),
     'L0_ffn_bs': (0.0, 0.549),
     'L0_ffn_b1': (0.0, 0.8),
     'L0_ffn_b2': (0.0, 0.414)}
    factors = {'cls_tok': 6.364,
     'L0_attn_b_qkv': 8.0,
     'L0_attn_b_proj': 2.786,
     'L0_ffn_W1': 3.624,
     'L0_ffn_W2': 3.358}
    for name, (base, spread) in spreads.items():
        noise = np.random.default_rng([zlib.crc32(name.encode()), seed]).standard_normal(out[name].shape)
        drawn = base * np.exp(spread * noise) if base else spread * noise
        out[name] = jnp.asarray(drawn.astype(out[name].dtype))
    for name, factor in factors.items():
        out[name] = (out[name] * factor).astype(out[name].dtype)
    return out
```

```python
from contextlib import ExitStack

import numpy as np

import concourse.bass as bass
from concourse import mybir

ALU = mybir.AluOpType
ACT = mybir.ActivationFunctionType
AX = mybir.AxisListType
F32 = mybir.dt.float32
BF16 = mybir.dt.bfloat16
I32 = mybir.dt.int32
U32 = mybir.dt.uint32
RMAX = bass.bass_isa.ReduceOp.max

MAGIC = 12582912.0
QEPS = 1.1920928955078125e-07
LN_EPS = 1e-5
INV_255 = float(np.float32(1.0) / np.float32(255.0))
FOUR_THIRDS = float(np.float32(4.0) / np.float32(3.0))
EXP_MASK = 0x7F800000


def tally(sem):
    count = [0]

    def mark(instruction):
        instruction.then_inc(sem, 1)
        count[0] += 1
        return count[0]

    return mark


def vit_tower(nc, x, cls_tok, tok_w, tok_b, w_qkv, b_qkv, w_proj, b_proj, ws, bs, w1, b1, w2, b2, out):
    B, IMG, _, CH = x.shape
    PATCH = 16
    SIDE = IMG // PATCH
    SEG = PATCH * CH
    C = tok_w.shape[1]
    HALF = C // 2
    HEADS, HD = 12, 16
    HG = HEADS // 2
    N = SIDE * SIDE + 1
    T = B * N
    NT = 9
    KC = PATCH * SEG // HALF
    E = ws.shape[1]
    F = w1.shape[2]
    FC = F // 128
    FH = F // 2
    GI = 7
    R = GI * N
    NG = -(-B // GI)
    M = HG * N
    L = NG * 2 * HG
    SLOT_TILES = (T + E * 127) // 128
    SLOTS = SLOT_TILES * 128
    COL_P, COL_ROW, COL_MEAN, COL_RSTD = C, C + 1, C + 2, C + 3
    PAYW = C + 4
    NO_ROW = 4 * T

    with ExitStack() as ctx:
        def sb(name, shape, dt=F32):
            return ctx.enter_context(nc.sbuf_tensor(name, shape, dt))

        def sem(name):
            return ctx.enter_context(nc.semaphore(name))

        slots = nc.dram_tensor("slots", (SLOTS, PAYW), F32, kind="Internal").ap()

        w1_sb = sb("w1_sb", [128, E, 2, F])
        w2_sb = sb("w2_sb", [128, E, FC, C])
        pay = sb("pay", [128, NT, PAYW])
        w_t = sb("w_t", [HALF, 2, 4 * C], BF16)
        ident = sb("ident", [128, 128])
        identb = sb("identb", [128, 128], BF16)
        small = sb("small", [128, 160])
        smalli = sb("smalli", [128, 40], I32)

        RA, RB, RC, RD = 6 * T, 7936, 6 * T, B * HALF
        area_a = sb("area_a", [128, RA + RB])
        area_c = sb("area_c", [128, RC])
        area_d = sb("area_d", [128, RD])

        def part(area, start, shape, dt=F32):
            n = int(np.prod(shape))
            words = n if dt != BF16 else -(-n // 2)
            v = area[:, start:start + words]
            if dt != F32:
                v = v.bitcast(dt)[:, 0:n]
            if len(shape) > 1:
                names = " ".join(f"d{i}" for i in range(len(shape)))
                v = v.rearrange(f"p ({names}) -> p {names}", **{f"d{i}": s for i, s in enumerate(shape) if i})
            return v

        x_sb = part(area_a, 0, [2, PATCH, SIDE, SEG])
        x_c = part(area_c, 0, [8, PATCH * SEG])
        x_t = [part(area_a, RA + 1024 * i, [KC, 128]) for i in range(2)]
        y_sb = part(area_a, 0, [6, T])
        xn = part(area_a, 0, [NT, C])
        residue = [part(area_a, NT * C + 512 * i, [512]) for i in range(2)]
        qmask = part(area_a, RA, [2, B, R], BF16)
        w_row = part(area_d, 0, [8, C])
        w_int = part(area_d, 8 * C, [8, C], BF16)
        w_v = part(area_d, 12 * C, [8, C])
        tokw_sb = part(area_d, 20 * C, [KC, C])
        x_part = part(area_c, 0, [3, 2, T], BF16)
        kv_t = part(area_d, 0, [4, T], BF16)
        k_exp = part(area_c, 0, [2, B, HG, N], BF16)
        v_exp_t = k_exp
        v_exp = part(area_d, 0, [2, B, HALF], BF16)
        SW = L * N
        soft = [part(area_a, SW * i, [L, N]) for i in range(6)]
        soft_i = [part(area_a, SW * i, [L, N], I32) for i in range(6)]
        probs = part(area_a, SW * 6, [NG * 2, M], BF16)
        probs_t = part(area_a, SW * 6 + SW // 2, [NG * 2, R], BF16)
        o_q = part(area_c, 0, [2, T], BF16)
        o_v = part(area_a, 0, [2, T])
        proj = part(area_a, 2 * T, [NT, C])
        proj_v = part(area_a, 2 * T + NT * C, [NT, C])
        xn2 = part(area_a, 0, [NT, C])
        xn2_t = part(area_a, NT * C, [2, NT, 128])
        xg = part(area_a, 0, [SLOT_TILES, PAYW])
        o = SLOT_TILES * PAYW
        xg_n = [part(area_a, o + C * i, [C]) for i in range(2)]
        o += 2 * C
        xg_t = [part(area_a, o + 256 * i, [2, 128]) for i in range(2)]
        o += 512
        h_sb = [part(area_a, o + F * i, [F]) for i in range(2)]
        o += 2 * F
        h_t = [part(area_a, o + F * i, [FC, 128]) for i in range(2)]
        o += 2 * F
        y_out = [part(area_a, o + C * i, [C]) for i in range(2)]
        o += 2 * C
        assert o <= RA + RB
        b2_pad = part(area_c, 2048, [E, C])
        fill = part(area_c, 2048 + E * C, [PAYW])
        head_mask = small[:, 0:6]
        o = 6

        def cols(n):
            nonlocal o
            v = small[:, o:o + n]
            o += n
            return v

        w_max, w_min, w_scale, w_inv, w_him = (cols(8) for _ in range(5))
        bq_col = cols(6)
        magic_c = cols(1)
        stat = cols(2 * 6)
        gin = cols(2)
        gout = cols(2)
        q_y, q_a, q_o, q_p = ([cols(1) for _ in range(4)] for _ in range(4))
        a_mul = cols(1)
        pol = cols(3)
        pol_t, pol_f, pol_g = cols(3), cols(3), cols(3)
        x0_30, x0_inv, q_bias, x0_pos = cols(1), cols(1), cols(1), cols(1)
        assert o <= 160
        rows = sb("rows", [128, 3, C])
        bs_row = sb("bs_row", [128, E])
        ws_sb = sb("ws_sb", [HALF, 2, E])
        row_max = sb("row_max", [128, L])
        row_sum = sb("row_sum", [128, L])
        bn = sb("bn", [128, NT, 6])
        mv = sb("mv", [128, NT, 2])
        rstd = sb("rstd", [128, NT])
        pow_e = sb("pow_e", [128, NT])
        lg, ex, hot, rk = (part(area_a, 8000 + NT * E * i, [NT, E]) for i in range(4))
        hot_b = part(area_a, 8000 + NT * E * 4, [NT, E], BF16)
        te = part(area_a, 8000 + NT * E * 5, [SLOT_TILES, E])
        e_idx = sb("e_idx", [128, NT, E])
        tri = sb("tri", [128, 128], BF16)
        ones_b = sb("ones_b", [128, 128], BF16)
        n9 = [sb(f"n9_{i}", [128, NT]) for i in range(3)]
        e8 = [sb(f"e8_{i}", [128, E]) for i in range(4)]
        dest = sb("dest", [128, NT], U32)
        te_idx = sb("te_idx", [128, SLOT_TILES])
        tile_expert = sb("tile_expert", [128, SLOT_TILES], I32)

        ps = ctx.enter_context(nc.psum_tensor("ps", [128, 8, 512], F32))

        def bank_b(b):
            return ps[:, b, :].bitcast(BF16)

        x_in = [sem(f"x_in{i}") for i in range(2)]
        w_in, tokw_in, small_in, w1_in, w2_in, b2_in = (sem(n) for n in ("w_in", "tokw_in", "small_in", "w1_in", "w2_in", "b2_in"))
        consts = sem("consts")
        vec, act_s, pool_s = sem("vec"), sem("act_s"), sem("pool_s")
        w_int_ready, w_t_psum, w_t_ready, w_scales_psum, diag_ready = (sem(n) for n in (
            "w_int_ready", "w_t_psum", "w_t_ready", "w_scales_psum", "diag_ready"))
        x_packed = sem("x_packed")
        xt_psum, xt_ready_v, xt_ready_a, embed_psum, embed_done = (sem(n) for n in (
            "xt_psum", "xt_ready_v", "xt_ready_a", "embed_psum", "embed_done"))
        var_ready, rstd_ready, xn_ready, xnt_psum, hi_done, res_done, mid_done, lo_done = (sem(n) for n in (
            "var_ready", "rstd_ready", "xn_ready", "xnt_psum", "hi_done", "res_done", "mid_done", "lo_done"))
        y_psum, y_ready = sem("y_psum"), sem("y_ready")
        stat_ready, all_max = sem("stat_ready"), sem("all_max")
        bound_in, bound_done, rounded = sem("bound_in"), sem("bound_done"), sem("rounded")
        qmask_zero, qmask_ready, k_exp_ready = sem("qmask_zero"), sem("qmask_ready"), sem("k_exp_ready")
        v_ready, s_psum, v_exp_t_ready, v_psum, v_exp_ready = (sem(n) for n in (
            "v_ready", "s_psum", "v_exp_t_ready", "v_psum", "v_exp_ready"))
        attn_scaled, xi_ready, q_ready, e_ready, y0_ready, p_ready, pt_psum, pt_ready, av_psum = (sem(n) for n in (
            "attn_scaled", "xi_ready", "q_ready", "e_ready", "y0_ready", "p_ready", "pt_psum", "pt_ready", "av_psum"))
        oq_ready, proj_psum, proj_ready, xn2_ready, xn2_psum, xn2t_v, xn2t_a, lg_psum = (sem(n) for n in (
            "oq_ready", "proj_psum", "proj_ready", "xn2_ready", "xn2_psum", "xn2t_v", "xn2t_a", "lg_psum"))
        lg_max, ex_ready, hot_ready, rank_psum, dest_ready, table_ready = (sem(n) for n in (
            "lg_max", "ex_ready", "hot_ready", "rank_psum", "dest_ready", "table_ready"))
        filled, scattered, slots_in0, slots_in1 = (sem(n) for n in ("filled", "scattered", "slots_in0", "slots_in1"))
        xg_ready, xgt_psum, xgt_ready, g1_psum, h_ready, ht_psum, ht_ready, g2_psum, y_done, stored, stored1 = (sem(n) for n in (
            "xg_ready", "xgt_psum", "xgt_ready", "g1_psum", "h_ready", "ht_psum", "ht_ready", "g2_psum", "y_done", "stored", "stored1"))

        block = ctx.enter_context(nc.Block())

        XG = [(range(0, 4), 0), (range(0, 4), 1), (range(8, 9), None), (range(4, 8), 0), (range(4, 8), 1)]
        PIECES = [(0, 512), (512, 1024), (1024, T)]
        VB = 10
        AVI = 22
        AVP = [(0, 22), (22, 44), (44, B)]
        CONSTS = 19
        P_FILL = 3
        W_TBANK = 6

        def xn2_out(copy, i):
            bank = (5, 6, 7, 5, 6)[i]
            m = min(4, 18 - 4 * i) // 2
            w = 128 if i < 4 else B
            src = ps[0:HALF, bank, 0:m * 256].rearrange("p (j k t) -> p j k t", k=2, t=128)[:, :, :, 0:w]
            dst = xn2_t[0:HALF, :, 2 * i:2 * i + m, 0:w].rearrange("p k j t -> p j k t")
            if m == 1:
                return copy(dst[:, 0], src[:, 0])
            return copy(dst, src)

        @block.sync
        def _(sp):
            xr = x.rearrange("(t b) (h r) w c -> t (b h) (r w c)", t=2, r=PATCH)
            for t in range(2):
                sp.dma_start(area_a[:, t * PATCH * IMG * CH:(t + 1) * PATCH * IMG * CH], xr[t]).then_inc(x_in[t], 16)
            sp.dma_start(w1_sb[0:HALF, :, 0, :], w1[:, 0:HALF, :].rearrange("e d f -> d e f")).then_inc(w1_in, 16)
            sp.dma_start(w1_sb[0:HALF, :, 1, :], w1[:, HALF:C, :].rearrange("e d f -> d e f")).then_inc(w1_in, 16)
            sp.dma_start(w1_sb[HALF:HALF + 1, :, 0, :], b1.unsqueeze(0)).then_inc(w1_in, 16)
            for c in range(FC):
                sp.dma_start(w2_sb[:, :, c, :], w2[:, c * 128:(c + 1) * 128, :].rearrange("e p d -> p e d")).then_inc(w2_in, 16)
            sp.wait_ge(pool_s, P_FILL)
            sp.dma_start(slots.rearrange("(t p) c -> p t c", p=128),
                         fill.unsqueeze(1).to_broadcast([128, SLOT_TILES, PAYW])).then_inc(filled, 16)
            sp.dma_start(b2_pad[HALF:HALF + 1], b2.unsqueeze(0)).then_inc(b2_in, 16)
            sp.wait_ge(scattered, 16 * NT)
            sl = slots.rearrange("(t p) c -> p t c", p=128)
            sp.dma_start(xg[:, 0:2, :], sl[:, 0:2, :]).then_inc(slots_in0, 16)
            sp.dma_start(xg[:, 2:SLOT_TILES, :], sl[:, 2:SLOT_TILES, :]).then_inc(slots_in1, 16)

        @block.gpsimd
        def _(pool):
            mark = tally(consts)
            mark(pool.memset(ident[:, :], 0.0))
            mark(pool.memset(identb[:, :], 0.0))
            mark(pool.memset(head_mask, 1.0))
            mark(pool.memset(tri[:, :], 1.0))
            mark(pool.memset(ones_b[:, :], 1.0))
            mark(pool.memset(magic_c, MAGIC))
            mark(pool.memset(pow_e[:, :], -0.5))
            mark(pool.memset(gin, 0.0))
            n = mark(pool.memset(rows[:, 2, :], 1.0))
            pool.wait_ge(consts, n)
            mark(pool.affine_select(out=ident[:, :], in_=ident[:, :], compare_op=ALU.not_equal, fill=1.0,
                                    base=0, pattern=[[-1, 128]], channel_multiplier=1))
            mark(pool.affine_select(out=identb[:, :], in_=identb[:, :], compare_op=ALU.not_equal, fill=1.0,
                                    base=0, pattern=[[-1, 128]], channel_multiplier=1))
            mark(pool.affine_select(out=tri[:, :], in_=tri[:, :], compare_op=ALU.is_gt, fill=0.0,
                                    base=0, pattern=[[1, 128]], channel_multiplier=-1))
            n = mark(pool.affine_select(out=head_mask, in_=head_mask, compare_op=ALU.is_ge, fill=0.0,
                                        base=0, pattern=[[-HD, HG]], channel_multiplier=1))
            pool.wait_ge(consts, n)
            mark(pool.affine_select(out=head_mask, in_=head_mask, compare_op=ALU.is_ge, fill=0.0,
                                    base=HD - 1, pattern=[[HD, HG]], channel_multiplier=-1))
            mark(pool.iota(e_idx[:, :, :], [[0, NT], [1, E]], base=0, channel_multiplier=0,
                           allow_small_or_imprecise_dtypes=True))
            mark(pool.iota(te_idx[:, :], [[1, SLOT_TILES]], base=0, channel_multiplier=0,
                           allow_small_or_imprecise_dtypes=True))
            mark(pool.iota(smalli[:, 0:1], [[0, 1]], base=0, channel_multiplier=1))
            mark(pool.iota(smalli[:, 1:1 + NT - 1], [[N * B // 2, 2], [1, SIDE]], base=1, channel_multiplier=SIDE))
            assert mark(pool.iota(smalli[:, NT:NT + 1], [[0, 1]], base=0, channel_multiplier=N)) == CONSTS

            for j in range(8):
                if j % SIDE == 0:
                    pool.wait_ge(x_in[j // SIDE], 16)
                pool.tensor_copy(x_c[:, j, :].rearrange("p (r s) -> p r s", s=SEG),
                                 x_sb[:, j // SIDE, :, j % SIDE, :]).then_inc(x_packed, 1)

            pool.wait_ge(var_ready, 1)
            pool.tensor_tensor(rstd[:, :], mv[:, :, 1], pow_e[:, :], ALU.pow).then_inc(rstd_ready, 1)
            pool.wait_ge(embed_psum, 8)
            pool.memset(part(area_a, RA, [RB]), 0.0).then_inc(qmask_zero, 1)
            for i in range(3):
                pool.wait_ge(stat_ready, i + 1)
                pool.partition_all_reduce(gout, gin, 128, RMAX).then_inc(all_max, 1)
            pool.wait_ge(v_psum, 14)
            pool.memset(b2_pad, 0.0).then_inc(pool_s, 1)
            pool.memset(fill, 0.0).then_inc(pool_s, 1)
            pool.wait_ge(pool_s, 2)
            pool.memset(fill[:, COL_ROW:COL_ROW + 1].bitcast(I32), NO_ROW).then_inc(pool_s, 1)
            pool.wait_ge(stat_ready, 4)
            pool.partition_all_reduce(gout, gin, 128, RMAX).then_inc(all_max, 1)
            pool.wait_ge(var_ready, 2)
            pool.tensor_tensor(pay[:, :, COL_RSTD], rstd[:, :], pow_e[:, :], ALU.pow).then_inc(rstd_ready, 1)
            pool.wait_ge(dest_ready, 1)
            pool.wait_ge(filled, 16)
            for j in range(NT):
                n = 128 if j < NT - 1 else B
                pool.indirect_dma_start(out=slots, out_offset=bass.IndirectOffsetOnAxis(ap=dest[0:n, j:j + 1], axis=0),
                                        in_=pay[0:n, j, :], in_offset=None, bounds_check=SLOTS - 1,
                                        oob_is_err=False).then_inc(scattered, 16)
            out_rows = out.rearrange("b n c -> (b n) c")

            def store(t, k):
                pool.wait_ge(y_done, t + 1)
                row = xg[:, bass.ds(t, 1), COL_ROW].bitcast(U32) if not isinstance(t, int) else \
                    xg[:, t, COL_ROW:COL_ROW + 1].bitcast(U32)
                pool.indirect_dma_start(out=out_rows, out_offset=bass.IndirectOffsetOnAxis(ap=row, axis=0),
                                        in_=y_out[k], in_offset=None, bounds_check=T - 1,
                                        oob_is_err=False).then_inc((stored, stored1)[k], 16)

            for t in range(SLOT_TILES):
                store(t, t % 2)
            pool.wait_ge(stored, 16 * SLOT_TILES // 2)
            pool.wait_ge(stored1, 16 * SLOT_TILES // 2)

        @block.tensor
        def _(pe):
            pe.wait_ge(consts, CONSTS)

            pe.wait_ge(w_int_ready, 8)
            for k in range(2):
                for c in range(8):
                    mm = pe.transpose(bank_b(W_TBANK + k)[0:HALF, c * HALF:(c + 1) * HALF],
                                      w_int[0:HALF, c, k * HALF:(k + 1) * HALF], identb[0:HALF, 0:HALF])
                mm.then_inc(w_t_psum, 1)
            pe.wait_ge(diag_ready, 2)
            pe.wait_ge(w_t_ready, 1)
            for g in range(2):
                mm = pe.matmul(ps[:, W_TBANK, g * HALF:(g + 1) * HALF], rows[0:HALF, 2, 0:128],
                               w_v[0:HALF, g, 0:HALF], start=True, stop=True)
            mm.then_inc(w_scales_psum, 1)

            def turn_patches(j):
                pe.wait_ge(x_packed, j + 1)
                if j >= 2:
                    pe.wait_ge(xt_ready_v, j - 1)
                    pe.wait_ge(xt_ready_a, j - 1)
                for k in range(KC):
                    mm = pe.transpose(ps[0:HALF, 2 * (j % 2) + k // 4, (k % 4) * 128:(k % 4 + 1) * 128],
                                      x_c[:, j, k * HALF:(k + 1) * HALF], ident[:, :])
                mm.then_inc(xt_psum, 1)

            def embed(j):
                pe.wait_ge(xt_ready_v, j + 1)
                pe.wait_ge(xt_ready_a, j + 1)
                if j == 0:
                    pe.wait_ge(tokw_in, 16)
                if j >= 2:
                    pe.wait_ge(embed_done, j - 1)
                for k in range(KC):
                    mm = pe.matmul(ps[:, 4 + j % 2, 0:C], x_t[j % 2][0:HALF, k, :], tokw_sb[0:HALF, k, :],
                                   start=k == 0, stop=k == KC - 1)
                mm.then_inc(embed_psum, 1)

            turn_patches(0)
            for j in range(8):
                if j < 7:
                    turn_patches(j + 1)
                embed(j)

            pe.wait_ge(xn_ready, NT)
            pe.wait_ge(w_t_ready, 3)
            for i, (tiles, half) in enumerate(XG):
                if i >= 2:
                    pe.wait_ge(res_done, i - 1)
                n = 0
                for k in ([half] if half is not None else [0, 1]):
                    for j in tiles:
                        w = 128 if j < NT - 1 else B
                        mm = pe.transpose(ps[0:HALF, 6 + i % 2, n:n + w], xn[0:w, j, k * HALF:(k + 1) * HALF],
                                          ident[0:w, 0:w])
                        n += w
                mm.then_inc(xnt_psum, 1)

            for c in range(6):
                for s, (a, b) in enumerate(PIECES):
                    if c == 0:
                        pe.wait_ge(lo_done, 3 if s == 0 else 5)
                        if s == 2:
                            pe.wait_ge(embed_done, 8)
                    if c >= 2:
                        pe.wait_ge(y_ready, 3 * (c - 2) + s + 1)
                    for n, (k, q) in enumerate([(k, q) for q in range(3) for k in range(2)]):
                        mm = pe.matmul(ps[0:HALF, (c % 2) * 3 + s, 0:b - a], w_t[:, k, c * HALF:(c + 1) * HALF],
                                       x_part[0:HALF, q, k, a:b], start=n == 0, stop=n == 5)
                    mm.then_inc(y_psum, 1)

            pe.wait_ge(qmask_ready, 1)
            pe.wait_ge(k_exp_ready, 1)
            for G in range(NG):
                for g in range(2):
                    images = range(GI * G, min(GI * G + GI, B))
                    for b in images:
                        mm = pe.matmul(ps[0:R, G // 2, (G % 2) * 2 * M + g * M:(G % 2) * 2 * M + (g + 1) * M],
                                       qmask[0:HALF, g, b, :], k_exp[0:HALF, g, b, :, :],
                                       start=b == images[0], stop=b == images[-1])
            mm.then_inc(s_psum, 1)

            n = 0
            for g in range(2):
                pe.wait_ge(v_exp_t_ready, g + 1)
                for b0 in range(0, B, VB):
                    if n >= 3:
                        pe.wait_ge(v_exp_ready, n - 2)
                    for b in range(b0, min(b0 + VB, B)):
                        mm = pe.transpose(bank_b(5 + n % 3)[0:M, (b - b0) * HALF:(b - b0 + 1) * HALF],
                                          v_exp_t[0:HALF, g, b, :, :], identb[0:HALF, 0:HALF])
                    mm.then_inc(v_psum, 1)
                    n += 1
            NV = n

            pe.wait_ge(v_exp_ready, NV)
            for i in range(2 * NG):
                if i == 0:
                    pe.wait_ge(p_ready, 1)
                if i == NG:
                    pe.wait_ge(p_ready, 2)
                mm = pe.transpose(bank_b(5 + i // 8)[0:M, (i % 8) * 128:(i % 8) * 128 + R],
                                  probs[0:R, i, :], identb[0:R, 0:R])
                if i % 8 == 7 or i == 2 * NG - 1:
                    mm.then_inc(pt_psum, 1)
            pe.wait_ge(pt_ready, 3)
            for g in range(2):
                for b in range(B):
                    mm = pe.matmul(ps[0:HALF, 3 * g + b // AVI, (b % AVI) * N:(b % AVI + 1) * N],
                                   v_exp[0:M, g, b, :], probs_t[0:M, 2 * (b // GI) + g, (b % GI) * N:(b % GI + 1) * N],
                                   start=True, stop=True)
                mm.then_inc(av_psum, 1)

            pe.wait_ge(oq_ready, 1)
            for j in range(NT):
                w = 128 if j < NT - 1 else B
                for g in range(2):
                    mm = pe.matmul(ps[0:w, j // 2, (j % 2) * C:(j % 2 + 1) * C], o_q[0:HALF, g, j * 128:j * 128 + w],
                                   w_t[:, g, 3 * C:4 * C], start=g == 0, stop=g == 1)
            mm.then_inc(proj_psum, 1)

            pe.wait_ge(xn2_ready, NT)
            for i in range(5):
                bank = (5, 6, 7, 5, 6)[i]
                if i >= 3:
                    pe.wait_ge((xn2t_v, xn2t_a)[(i - 3) % 2], (i - 3) // 2 + 1)
                for n in range(4 * i, min(4 * i + 4, 18)):
                    j, k = n // 2, n % 2
                    w = 128 if j < NT - 1 else B
                    mm = pe.transpose(ps[0:HALF, bank, (n % 4) * 128:(n % 4) * 128 + w],
                                      xn2[0:w, j, k * HALF:(k + 1) * HALF], ident[0:w, 0:w])
                mm.then_inc(xn2_psum, 1)
            pe.wait_ge(xn2t_v, 3)
            pe.wait_ge(xn2t_a, 2)
            for j in range(NT):
                w = 128 if j < NT - 1 else B
                for k in range(2):
                    mm = pe.matmul(ps[0:w, 7, j * E:(j + 1) * E], xn2_t[0:HALF, k, j, 0:w], ws_sb[:, k, :],
                                   start=k == 0, stop=k == 1)
            mm.then_inc(lg_psum, 1)
            pe.wait_ge(hot_ready, 1)
            pe.matmul(ps[:, 0, 0:NT * E], tri[:, :], hot_b[:, :, :], start=True, stop=False, skip_group_check=True)
            for j in range(NT - 1):
                pe.matmul(ps[:, 0, (j + 1) * E:NT * E], ones_b[:, :],
                          hot_b[:, j:j + 1, :].to_broadcast([128, NT - 1 - j, E]), start=False, stop=j == NT - 2,
                          skip_group_check=True)
            for j in range(NT):
                mm = pe.matmul(ps[:, 1, 0:E], ones_b[:, :], hot_b[:, j, :], start=j == 0, stop=j == NT - 1)
            mm.then_inc(rank_psum, 1)

            pe.wait_ge(table_ready, 1)
            pe.wait_ge(w1_in, 48)
            pe.wait_ge(w2_in, 16 * FC)
            pe.wait_ge(b2_in, 16)

            def turn_tokens(t, k):
                pe.wait_ge(xg_ready, t + 1)
                if not isinstance(t, int) or t >= 1:
                    pe.wait_ge(xgt_ready, t)
                for c in range(2):
                    mm = pe.transpose(ps[0:HALF, 7, c * 128:(c + 1) * 128], xg_n[k][:, c * HALF:(c + 1) * HALF],
                                      ident[:, :])
                mm.then_inc(xgt_psum, 1)

            def expert_of(t):
                return pe.value_load(tile_expert[0:1, bass.ds(t, 1)], min_val=0, max_val=E - 1)

            def first_product(t, k):
                e = expert_of(t)
                pe.wait_ge(xgt_ready, t + 1)
                if not isinstance(t, int) or t >= 2:
                    pe.wait_ge(h_ready, t - 1)
                for half in range(2):
                    for c in range(2):
                        p = HALF + 1 if c == 0 else HALF
                        mm = pe.matmul(ps[:, 2 * k + half, 0:FH], xg_t[k][0:p, c, :],
                                       w1_sb[0:p, bass.ds(e, 1), c, half * FH:(half + 1) * FH],
                                       start=c == 0, stop=c == 1)
                mm.then_inc(g1_psum, 1)

            def turn_hidden(t, k):
                pe.wait_ge(h_ready, t + 1)
                if not isinstance(t, int) or t >= 1:
                    pe.wait_ge(ht_ready, t)
                for f in range(FC):
                    mm = pe.transpose(ps[:, 4 + f // 3, (f % 3) * 128:(f % 3 + 1) * 128],
                                      h_sb[k][:, f * 128:(f + 1) * 128], ident[:, :])
                mm.then_inc(ht_psum, 1)

            def second_product(t, k):
                e = expert_of(t)
                pe.wait_ge(ht_ready, t + 1)
                if not isinstance(t, int) or t >= 1:
                    pe.wait_ge(y_done, t)
                pe.matmul(ps[:, 6, 0:C], xg_t[k][0:HALF + 1, 0, :], b2_pad[0:HALF + 1, bass.ds(e, 1), :],
                          start=True, stop=False)
                for f in range(FC):
                    mm = pe.matmul(ps[:, 6, 0:C], h_t[k][:, f, :], w2_sb[:, bass.ds(e, 1), f, :],
                                   start=False, stop=f == FC - 1)
                mm.then_inc(g2_psum, 1)

            turn_tokens(0, 0)
            first_product(0, 0)
            turn_tokens(1, 1)

            def step(t, k, more=2):
                turn_hidden(t, k)
                if more >= 1:
                    first_product(t + 1, 1 - k)
                second_product(t, k)
                if more >= 2:
                    turn_tokens(t + 2, k)

            step(0, 0)
            step(1, 1)
            with pe.Fori(2, SLOT_TILES - 2, 2) as t:
                step(t, 0)
                step(t + 1, 1)
            step(SLOT_TILES - 2, 0, 1)
            step(SLOT_TILES - 1, 1, 0)

        @block.vector
        def _(v):
            mark = tally(vec)

            def then(instruction):
                v.wait_ge(vec, mark(instruction))

            mark(v.memset(pay[B:128, NT - 1, :], 0.0))
            v.wait_ge(w_in, 32)
            wr = w_row[0:HALF]
            h96 = slice(0, HALF)
            mark(v.tensor_reduce(w_max[h96], wr, AX.X, ALU.max))
            then(v.tensor_reduce(w_min[h96], wr, AX.X, ALU.min))
            mark(v.tensor_scalar(w_max[h96], w_max[h96], 0.0, None, ALU.max))
            then(v.tensor_scalar(w_min[h96], w_min[h96], 0.0, None, ALU.min))
            then(v.tensor_tensor(w_scale[h96], w_max[h96], w_min[h96], ALU.subtract))
            then(v.tensor_scalar(w_scale[h96], w_scale[h96], INV_255, QEPS, ALU.mult, ALU.max))
            then(v.reciprocal(w_inv[h96], w_scale[h96]))
            then(v.tensor_tensor(w_him[h96], w_min[h96], w_inv[h96], ALU.mult))
            then(v.tensor_scalar(w_him[h96], w_him[h96], MAGIC, 255.0, ALU.add, ALU.add))
            for c in range(8):
                n = mark(v.tensor_scalar(w_v[h96, c], wr[:, c], w_inv[h96, c:c + 1], MAGIC, ALU.mult, ALU.add))
            v.wait_ge(vec, n)
            for c in range(8):
                v.tensor_scalar(w_int[h96, c], w_v[h96, c], w_him[h96, c:c + 1], MAGIC, ALU.min,
                                ALU.subtract).then_inc(w_int_ready, 1)
            v.wait_ge(consts, CONSTS)
            v.wait_ge(w_int_ready, 8)
            for g in range(2):
                v.tensor_scalar(w_v[h96, g, 0:HALF], ident[h96, 0:HALF], w_scale[h96, 6 + g:7 + g], None,
                                ALU.mult).then_inc(diag_ready, 1)
            for k in range(2):
                v.wait_ge(w_t_psum, k + 1)
                v.tensor_copy(w_t[:, k, :], bank_b(W_TBANK + k)[h96, 0:8 * HALF]).then_inc(w_t_ready, 1)
            v.wait_ge(w_scales_psum, 1)
            v.tensor_copy(rows[:, 2, :], ps[:, W_TBANK, 0:C]).then_inc(w_t_ready, 1)

            then(v.tensor_scalar(smalli[:, 20:21], smalli[:, 0:1], 2, None, ALU.arith_shift_right))
            then(v.tensor_copy(n9[0][:, 0:1], smalli[:, 20:21]))
            mark(v.tensor_scalar(pay[:, 0:NT - 1, COL_ROW].bitcast(I32), smalli[:, 1:NT], n9[0][:, 0:1], None, ALU.add))
            mark(v.tensor_copy(pay[0:B, NT - 1, COL_ROW:COL_ROW + 1].bitcast(I32), smalli[0:B, NT:NT + 1]))

            v.wait_ge(small_in, 16 * 6)

            def patches_out(j):
                v.wait_ge(xt_psum, j + 1)
                if j >= 2:
                    v.wait_ge(embed_psum, j - 1)
                v.tensor_copy(x_t[j % 2][h96, 0:4, :], ps[h96, 2 * (j % 2), :]).then_inc(xt_ready_v, 1)

            patches_out(0)
            for j in range(8):
                if j < 7:
                    patches_out(j + 1)
                v.wait_ge(embed_psum, j + 1)
                v.tensor_tensor(pay[:, j, 0:C], ps[:, 4 + j % 2, 0:C], rows[:, 0, :], ALU.add).then_inc(embed_done, 1)
                v.wait_ge(embed_done, j + 1)
                mark(v.bn_stats(bn[:, j, :], pay[:, j, 0:C]))
            n = mark(v.bn_stats(bn[:, 8, :], pay[:, 8, 0:C]))
            v.wait_ge(vec, n)
            for j in range(NT):
                n = mark(v.bn_aggr(mv[:, j, :], bn[:, j, :]))
            v.wait_ge(vec, n)
            v.tensor_scalar(mv[:, :, 1], mv[:, :, 1], LN_EPS, None, ALU.add).then_inc(var_ready, 1)
            v.wait_ge(rstd_ready, 1)
            for j in range(NT):
                v.tensor_scalar(xn[:, j, :], pay[:, j, 0:C], mv[:, j, 0:1], rstd[:, j:j + 1], ALU.subtract,
                                ALU.mult).then_inc(xn_ready, 1)

            def token_view(q, k, i):
                tiles, half = XG[i]
                if half is None:
                    return x_part[h96, q].rearrange("p k (b n) -> p k b n", n=N)[:, :, :, 0]
                t = tiles[0] // SIDE
                return x_part[h96, q, half, t * T // 2:(t + 1) * T // 2].rearrange(
                    "p (b n) -> p b n", n=N)[:, :, 1:N].rearrange("p b (h w) -> p w b h", w=SIDE)

            def split(i):
                tiles, half = XG[i]
                n = 512 if half is not None else 2 * B
                shape = dict(w=SIDE, b=B // 2) if half is not None else dict(w=2)
                pat = "p (w b h) -> p w b h" if half is not None else "p (w b) -> p w b"
                return n, (lambda ap: ap[h96, 0:n].rearrange(pat, **shape))

            def residue_of(i):
                n, view = split(i)
                v.wait_ge(hi_done, i + 1)
                if i >= 2:
                    v.wait_ge(lo_done, i - 1)
                v.tensor_tensor(view(residue[i % 2]), view(ps[:, 6 + i % 2, :]), token_view(0, None, i),
                                ALU.subtract).then_inc(res_done, 1)

            def lowest(i):
                n, view = split(i)
                v.wait_ge(mid_done, i + 1)
                v.tensor_tensor(token_view(2, None, i), view(residue[i % 2]), token_view(1, None, i),
                                ALU.subtract).then_inc(lo_done, 1)

            residue_of(0)
            for i in range(5):
                if i < 4:
                    residue_of(i + 1)
                lowest(i)

            for c in range(6):
                v.wait_ge(y_ready, 3 * c + 3)
                mark(v.tensor_reduce(stat[h96, c:c + 1], y_sb[h96, c, :], AX.X, ALU.max))
                n = mark(v.tensor_reduce(stat[h96, 6 + c:7 + c], y_sb[h96, c, :], AX.X, ALU.min))
            v.wait_ge(vec, n)

            def extremes(p, count, which, stat_max=None, stat_min=None):
                mark(v.tensor_reduce(gin[p, 0:1], stat_max, AX.X, ALU.max))
                then(v.tensor_reduce(gin[p, 1:2], stat_min, AX.X, ALU.min))
                mark(v.tensor_scalar(gin[p, 0:1], gin[p, 0:1], 0.0, None, ALU.max))
                v.tensor_scalar(gin[p, 1:2], gin[p, 1:2], -1.0, 0.0, ALU.mult, ALU.max).then_inc(stat_ready, 1)
                v.wait_ge(all_max, which)

            def scales(q, mul=None):
                then(v.tensor_tensor(q[0], gout[:, 0:1], gout[:, 1:2], ALU.add))
                if mul is not None:
                    then(v.tensor_scalar(q[0], q[0], mul, None, ALU.mult))
                then(v.tensor_scalar(q[0], q[0], INV_255, QEPS, ALU.mult, ALU.max))
                then(v.reciprocal(q[1], q[0]))
                if mul is not None:
                    then(v.tensor_scalar(q[1], q[1], mul, None, ALU.mult))
                v.tensor_scalar(q[3], gout[:, 1:2], -1.0, None, ALU.mult).then_inc(bound_in, 1)

            def upper(q, which):
                v.wait_ge(bound_done, which)
                then(v.tensor_scalar(q[2], q[2], 255.0, None, ALU.add))

            extremes(h96, 6, 1, stat[h96, 0:6], stat[h96, 6:12])
            scales(q_y)
            upper(q_y, 1)
            v.wait_ge(rounded, 2)
            v.wait_ge(qmask_zero, 1)
            for i in range(GI):
                mark(v.tensor_scalar(
                    qmask[h96, :, 0:GI * (NG - 1), :].rearrange("p g (G i) r -> p g G i r", i=GI)[:, :, :, i, i * N:(i + 1) * N],
                    y_sb[h96, 0:2, 0:R * (NG - 1)].rearrange("p g (G r) -> p g G r", r=R)[:, :, :, i * N:(i + 1) * N],
                    q_y[2][h96], MAGIC, ALU.min, ALU.subtract))
            v.tensor_scalar(qmask[h96, :, B - 1, 0:N], y_sb[h96, 0:2, T - N:T], q_y[2][h96], MAGIC, ALU.min,
                            ALU.subtract).then_inc(qmask_ready, 1)
            v.wait_ge(rounded, 4)
            then(v.tensor_scalar(kv_t[h96, 0:2, :], y_sb[h96, 2:4, :], q_y[2][h96], MAGIC, ALU.min, ALU.subtract))
            kb = kv_t[h96, 0:2, :].rearrange("p g (b n) -> p (g b) n", n=N)
            kx = k_exp[h96].rearrange("p g b h n -> p (g b) h n")
            for h in range(HG):
                ins = v.tensor_scalar(kx[:, :, h, :], kb, head_mask[h96, h:h + 1], None, ALU.mult)
                if h == HG - 1:
                    ins.then_inc(k_exp_ready, 1)
                else:
                    mark(ins)
            v.wait_ge(rounded, 6)
            v.tensor_scalar(kv_t[h96, 2:4, :], y_sb[h96, 4:6, :], q_y[2][h96], MAGIC, ALU.min,
                            ALU.subtract).then_inc(v_ready, 1)

            then(v.tensor_scalar(a_mul, q_y[0], q_y[0], HD ** -0.5, ALU.mult, ALU.mult))
            then(v.memset(gin, 0.0))
            v.wait_ge(s_psum, 1)
            sv = ps[0:R, 0:5, 0:4 * M].rearrange("p b (l m) -> p b l m", m=N)
            rm = row_max[0:R].rearrange("p (b l) -> p b l", b=5)
            mark(v.tensor_reduce(rm, sv, AX.X, ALU.max))
            then(v.tensor_reduce(stat[0:R, 0:5], ps[0:R, 0:5, 0:4 * M], AX.X, ALU.min))
            extremes(slice(0, R), 0, 2, row_max[0:R], stat[0:R, 0:5])
            scales(q_a, a_mul)
            c0 = np.float32(0.35815147)
            then(v.reciprocal(x0_pos, q_a[0]))
            mark(v.tensor_scalar(pol[:, 0:1], x0_pos, float(np.float32(-0.6931)), None, ALU.mult))
            mark(v.tensor_scalar(pol[:, 1:2], x0_pos, float(np.float32(0.96963238) / c0), None, ALU.mult))
            then(v.tensor_scalar(pol[:, 2:3], x0_pos, x0_pos, float(np.float32(1.0) / c0), ALU.mult, ALU.mult))
            then(v.tensor_scalar(pol_t, pol, 16777216.0, None, ALU.min))
            then(v.tensor_copy(smalli[:, 24:27], pol_t))
            then(v.tensor_copy(pol_f, smalli[:, 24:27]))
            then(v.tensor_tensor(pol_g, pol_f, pol_t, ALU.is_gt))
            then(v.tensor_tensor(pol_f, pol_f, pol_g, ALU.subtract))
            mark(v.tensor_scalar(pol_g, pol, 8388608.0, None, ALU.is_ge))
            then(v.tensor_tensor(pol_t, pol, pol_f, ALU.subtract))
            then(v.tensor_tensor(pol_t, pol_t, pol_g, ALU.mult))
            then(v.tensor_tensor(pol, pol_f, pol_t, ALU.add))
            mark(v.tensor_scalar(x0_30, pol[:, 0:1], 30.0, None, ALU.mult))
            mark(v.tensor_scalar(x0_pos, pol[:, 0:1], -1.0, None, ALU.mult))
            then(v.reciprocal(x0_inv, pol[:, 0:1]))
            then(v.tensor_scalar(q_bias, x0_inv, -0.5, -0.5, ALU.mult, ALU.add))
            upper(q_a, 2)

            v.wait_ge(attn_scaled, 1)
            then(v.tensor_scalar(row_max[0:R], row_max[0:R], q_a[2][0:R], None, ALU.min))
            LH = L // 2
            V_, XI, QI, W_, E_, Y0 = soft
            VI, _, QQ, WI, _, _ = soft_i

            def half(ap, i):
                return ap[0:R, i * LH:(i + 1) * LH, :]

            def bc(ap, i):
                return ap[0:R, i * LH:(i + 1) * LH].unsqueeze(2).to_broadcast([R, LH, N])

            for i in range(2):
                v.wait_ge(attn_scaled, i + 2)
                then(v.scalar_tensor_tensor(out=half(V_, i), in0=half(V_, i), scalar=q_a[2][0:R], in1=bc(row_max, i),
                                            op0=ALU.min, op1=ALU.subtract))
                v.tensor_scalar(half(XI, i), half(V_, i), x0_30[0:R], None, ALU.max).then_inc(xi_ready, 1)
            for i in range(2):
                v.wait_ge(q_ready, i + 1)
                mark(v.tensor_scalar(half(VI, i), half(QQ, i), -8388608.0, 157.0 * 8388608.0, ALU.mult, ALU.add))
                then(v.scalar_tensor_tensor(out=half(XI, i), in0=half(QQ, i), scalar=x0_pos[0:R], in1=half(XI, i),
                                            op0=ALU.mult, op1=ALU.add))
                then(v.scalar_tensor_tensor(out=half(W_, i), in0=half(XI, i), scalar=pol[0:R, 1:2], in1=half(XI, i),
                                            op0=ALU.add, op1=ALU.mult))
                then(v.scalar_tensor_tensor(out=half(E_, i), in0=half(W_, i), scalar=pol[0:R, 2:3], in1=half(V_, i),
                                            op0=ALU.add, op1=ALU.mult))
                v.tensor_scalar(half(E_, i), half(E_, i), 1.0, None, ALU.max).then_inc(e_ready, 1)
                v.wait_ge(e_ready, i + 1)
                n = mark(v.tensor_reduce(row_sum[0:R, i * LH:(i + 1) * LH], half(E_, i), AX.X, ALU.add))
            v.wait_ge(vec, n)
            then(v.tensor_scalar(row_sum[0:R], row_sum[0:R], -1.0, None, ALU.mult))
            for i in range(2):
                v.wait_ge(y0_ready, i + 1)
                then(v.tensor_tensor(half(W_, i), half(E_, i), half(Y0, i), ALU.mult))
                then(v.scalar_tensor_tensor(out=half(W_, i), in0=half(W_, i), scalar=2.0, in1=half(Y0, i),
                                            op0=ALU.subtract, op1=ALU.mult))
                then(v.tensor_tensor(half(W_, i), half(W_, i), bc(row_sum, i), ALU.mult))
                then(v.tensor_scalar(half(W_, i), half(W_, i), 1048576.0, MAGIC, ALU.min, ALU.add))
                then(v.tensor_scalar(half(W_, i), half(W_, i), MAGIC, FOUR_THIRDS, ALU.subtract, ALU.mult))
                then(v.tensor_scalar(half(WI, i), half(WI, i), EXP_MASK, EXP_MASK, ALU.bitwise_and, ALU.bitwise_xor))
                v.scalar_tensor_tensor(out=probs[0:R, i * NG:(i + 1) * NG].rearrange("p a (h m) -> p (a h) m", m=N),
                                       in0=half(W_, i), scalar=2.0 ** -14, in1=half(W_, i),
                                       op0=ALU.is_ge, op1=ALU.mult).then_inc(p_ready, 1)
            for n in range(3):
                v.wait_ge(pt_psum, n + 1)
                m = min(8, 2 * NG - 8 * n)
                v.tensor_copy(probs_t[0:M, 8 * n:8 * n + m, :],
                              bank_b(5 + n)[0:M, :].rearrange("p (a r) -> p a r", r=128)[:, 0:m, 0:R]).then_inc(pt_ready, 1)

            then(v.tensor_scalar(a_mul, q_y[0], 0.5, None, ALU.mult))
            then(v.memset(gin, 0.0))
            for g in range(2):
                v.wait_ge(av_psum, g + 1)
                for s, (a, b) in enumerate(AVP):
                    i = 3 * g + s
                    mark(v.tensor_reduce(stat[h96, i:i + 1], ps[h96, i, 0:(b - a) * N], AX.X, ALU.max))
                    n = mark(v.tensor_reduce(stat[h96, 6 + i:7 + i], ps[h96, i, 0:(b - a) * N], AX.X, ALU.min))
            v.wait_ge(vec, n)
            extremes(h96, 6, 3, stat[h96, 0:6], stat[h96, 6:12])
            scales(q_o, a_mul)
            upper(q_o, 3)
            mark(v.tensor_scalar(rows[:, 2, :], rows[:, 2, :], q_o[0], None, ALU.mult))
            v.wait_ge(rounded, 8)
            for g in range(2):
                for t in range(2):
                    mark(v.tensor_scalar(
                        o_q[h96, g, 512 * t:512 * t + 512].rearrange("p (w b h) -> p w b h", w=SIDE, b=B // 2),
                        o_v[h96, g, t * T // 2:(t + 1) * T // 2].rearrange("p (b n) -> p b n", n=N)[:, :, 1:N].rearrange(
                            "p b (h w) -> p w b h", w=SIDE), q_o[2][h96], MAGIC, ALU.min, ALU.subtract))
            mark(v.tensor_scalar(o_q[h96, :, 1024:T], o_v[h96].rearrange("p g (b n) -> p g b n", n=N)[:, :, :, 0],
                                 q_o[2][h96], MAGIC, ALU.min, ALU.subtract))
            v.memset(gin, 0.0).then_inc(oq_ready, 1)

            then(v.memset(proj[64:128, NT - 1, :], 0.0))
            v.wait_ge(proj_psum, 1)
            for i in range(5):
                p, m = (128, 2) if i < 4 else (B, 1)
                n = mark(v.tensor_tensor(proj[0:p, 2 * i:2 * i + m, :], ps[0:p, i, 0:m * C].rearrange("p (a c) -> p a c", c=C),
                                     rows[0:p, 2:3, :].to_broadcast([p, m, C]), ALU.mult))
            v.wait_ge(vec, n)
            mark(v.tensor_tensor(proj[:, 0:NT - 1, :], proj[:, 0:NT - 1, :],
                                 rows[:, 1:2, :].to_broadcast([128, NT - 1, C]), ALU.add))
            v.tensor_tensor(proj[0:B, NT - 1, :], proj[0:B, NT - 1, :], rows[0:B, 1, :], ALU.add).then_inc(proj_ready, 1)
            v.wait_ge(proj_ready, 1)
            mark(v.tensor_reduce(stat[:, 0:1], proj.rearrange("p a c -> p (a c)"), AX.X, ALU.max))
            then(v.tensor_reduce(stat[:, 1:2], proj.rearrange("p a c -> p (a c)"), AX.X, ALU.min))
            extremes(slice(0, 128), 1, 4, stat[:, 0:1], stat[:, 1:2])
            scales(q_p)
            upper(q_p, 4)
            v.wait_ge(rounded, 9)
            then(v.tensor_scalar(proj_v, proj_v, q_p[2], MAGIC, ALU.min, ALU.subtract))
            mark(v.scalar_tensor_tensor(out=pay[:, 0:NT - 1, 0:C], in0=proj_v[:, 0:NT - 1, :], scalar=q_p[0],
                                        in1=pay[:, 0:NT - 1, 0:C], op0=ALU.mult, op1=ALU.add))
            then(v.scalar_tensor_tensor(out=pay[0:B, NT - 1, 0:C], in0=proj_v[0:B, NT - 1, :], scalar=q_p[0][0:B],
                                        in1=pay[0:B, NT - 1, 0:C], op0=ALU.mult, op1=ALU.add))
            for j in range(NT):
                n = mark(v.bn_stats(bn[:, j, :], pay[:, j, 0:C]))
            v.wait_ge(vec, n)
            for j in range(NT):
                n = mark(v.bn_aggr(pay[:, j, COL_MEAN:COL_MEAN + 2], bn[:, j, :]))
            v.wait_ge(vec, n)
            v.tensor_scalar(rstd[:, :], pay[:, :, COL_RSTD], LN_EPS, None, ALU.add).then_inc(var_ready, 1)
            v.wait_ge(rstd_ready, 2)
            for j in range(NT):
                v.tensor_scalar(xn2[:, j, :], pay[:, j, 0:C], pay[:, j, COL_MEAN:COL_MEAN + 1],
                                pay[:, j, COL_RSTD:COL_RSTD + 1], ALU.subtract, ALU.mult).then_inc(xn2_ready, 1)
            for i in range(0, 5, 2):
                v.wait_ge(xn2_psum, i + 1)
                xn2_out(v.tensor_copy, i).then_inc(xn2t_v, 1)

            def all_tiles(f):
                mark(f(slice(0, 128), slice(0, NT - 1)))
                return f(slice(0, B), slice(NT - 1, NT))

            v.wait_ge(lg_psum, 1)
            lgp = ps[:, 7, 0:NT * E].rearrange("p (j e) -> p j e", e=E)
            then(v.memset(lg[:, NT - 1, :], 0.0))
            then(all_tiles(lambda p, t: v.tensor_tensor(
                lg[p, t, :], lgp[p, t, :], bs_row[p].unsqueeze(1).to_broadcast([p.stop, t.stop - t.start, E]), ALU.add)))
            then(v.tensor_reduce(n9[0][:, :], lg[:, :, :], AX.X, ALU.max))

            def per_tile(ap):
                return ap.unsqueeze(2).to_broadcast([128, NT, E])

            v.tensor_tensor(ex[:, :, :], lg[:, :, :], per_tile(n9[0][:, :]), ALU.subtract).then_inc(lg_max, 1)
            then(v.tensor_tensor(hot[:, :, :], lg[:, :, :], per_tile(n9[0][:, :]), ALU.is_lt))
            then(v.scalar_tensor_tensor(out=hot[:, :, :], in0=hot[:, :, :], scalar=float(E), in1=e_idx[:, :, :],
                                        op0=ALU.mult, op1=ALU.add))
            then(v.tensor_reduce(n9[1][:, :], hot[:, :, :], AX.X, ALU.min))
            then(v.tensor_tensor(hot[:, :, :], e_idx[:, :, :], per_tile(n9[1][:, :]), ALU.is_equal))
            then(v.memset(hot[64:128, NT - 1, :], 0.0))
            v.tensor_copy(hot_b[:, :, :], hot[:, :, :]).then_inc(hot_ready, 1)
            v.wait_ge(ex_ready, 1)
            then(v.tensor_reduce(n9[2][:, :], ex[:, :, :], AX.X, ALU.add))
            then(v.reciprocal(pay[:, :, COL_P], n9[2][:, :]))
            v.wait_ge(rank_psum, 1)
            tiles, ends, tmp, starts = e8
            then(v.tensor_scalar(tiles[:, :], ps[:, 1, 0:E], 1.0 / 128, 127.0 / 128 - 0.5 + 1.0 / 256, ALU.mult, ALU.add))
            then(v.tensor_scalar(tiles[:, :], tiles[:, :], MAGIC, MAGIC, ALU.add, ALU.subtract))
            src = tiles
            for i, sh in enumerate((1, 2, 4)):
                dst = (ends, tmp, ends)[i]
                mark(v.tensor_copy(dst[:, 0:sh], src[:, 0:sh]))
                then(v.tensor_tensor(dst[:, sh:E], src[:, sh:E], src[:, 0:E - sh], ALU.add))
                src = dst
            then(v.tensor_tensor(starts[:, :], ends[:, :], tiles[:, :], ALU.subtract))
            then(v.tensor_tensor(te[:, :, :], ends[:, :].unsqueeze(1).to_broadcast([128, SLOT_TILES, E]),
                                 te_idx[:, :].unsqueeze(2).to_broadcast([128, SLOT_TILES, E]), ALU.is_le))
            then(v.tensor_reduce(te_idx[:, :], te[:, :, :], AX.X, ALU.add))
            v.tensor_scalar(tile_expert[:, :], te_idx[:, :], float(E - 1), None, ALU.min).then_inc(table_ready, 1)
            then(v.scalar_tensor_tensor(out=rk[:, :, :], in0=starts[:, :].unsqueeze(1).to_broadcast([128, NT, E]),
                                        scalar=128.0, in1=ps[:, 0, 0:NT * E].rearrange("p (j e) -> p j e", e=E),
                                        op0=ALU.mult, op1=ALU.add))
            then(v.tensor_tensor(rk[:, :, :], rk[:, :, :], hot[:, :, :], ALU.mult))
            then(v.tensor_reduce(n9[1][:, :], rk[:, :, :], AX.X, ALU.add))
            v.tensor_copy(dest[:, :], n9[1][:, :]).then_inc(dest_ready, 1)

            for k in range(2):
                mark(v.memset(xg_t[k][HALF:HALF + 1, 0, :], 1.0))

            def normalise(t, k):
                if not isinstance(t, int) or t >= 2:
                    v.wait_ge(xgt_psum, t - 1)
                row = lambda a, b: xg[:, bass.ds(t, 1), a:b] if not isinstance(t, int) else xg[:, t, a:b]
                mean = row(COL_MEAN, COL_MEAN + 1)
                rs = row(COL_RSTD, COL_RSTD + 1)
                v.tensor_scalar(xg_n[k], row(0, C), mean, rs, ALU.subtract, ALU.mult).then_inc(xg_ready, 1)

            def hidden_out(t, k):
                v.wait_ge(ht_psum, t + 1)
                if not isinstance(t, int) or t >= 2:
                    v.wait_ge(g2_psum, t - 1)
                v.tensor_copy(h_t[k].rearrange("p (a f) r -> p a (f r)", a=2), ps[:, 4:6, 0:FH]).then_inc(ht_ready, 1)

            def finish(t, k):
                v.wait_ge(g2_psum, t + 1)
                if not isinstance(t, int) or t >= 2:
                    v.wait_ge((stored, stored1)[k], STORE_VALUE(t, k))
                prob = xg[:, bass.ds(t, 1), COL_P:COL_P + 1] if not isinstance(t, int) else xg[:, t, COL_P:COL_P + 1]
                h = xg[:, bass.ds(t, 1), 0:C] if not isinstance(t, int) else xg[:, t, 0:C]
                v.scalar_tensor_tensor(out=y_out[k], in0=ps[:, 6, 0:C], scalar=prob, in1=h,
                                       op0=ALU.mult, op1=ALU.add).then_inc(y_done, 1)

            def STORE_VALUE(t, k):
                return 8 * (t - k)

            v.wait_ge(slots_in0, 16)
            normalise(0, 0)
            normalise(1, 1)
            v.wait_ge(slots_in1, 16)

            def step(t, k, more=True):
                if more:
                    normalise(t + 2, k)
                hidden_out(t, k)
                finish(t, k)

            for t in range(SLOT_TILES):
                step(t, t % 2, t < SLOT_TILES - 2)

        @block.scalar
        def _(act):
            mark = tally(act_s)
            h96 = slice(0, HALF)
            act.dma_start(w_row[h96, 0:6, :], w_qkv.rearrange("(c p) d -> p c d", p=HALF)).then_inc(w_in, 16)
            act.dma_start(w_row[h96, 6:8, :], w_proj.rearrange("(c p) d -> p c d", p=HALF)).then_inc(w_in, 16)
            act.dma_start(tokw_sb[h96], tok_w.rearrange("(c p) d -> p c d", p=HALF)).then_inc(tokw_in, 16)
            act.dma_start(bq_col[h96], b_qkv.rearrange("(c p) -> p c", p=HALF), allow_slow_non_contiguous=True).then_inc(small_in, 16)
            act.dma_start(rows[:, 0, :], tok_b.partition_broadcast(128)).then_inc(small_in, 16)
            act.dma_start(rows[:, 1, :], b_proj.partition_broadcast(128)).then_inc(small_in, 16)
            act.dma_start(bs_row[:, :], bs.partition_broadcast(128)).then_inc(small_in, 16)
            act.dma_start(ws_sb[:, :, :], ws.rearrange("(k p) e -> p k e", p=HALF)).then_inc(small_in, 16)
            act.dma_start(pay[0:B, NT - 1, 0:C], cls_tok.rearrange("a b c -> (a b c)").partition_broadcast(B)).then_inc(small_in, 16)

            for j in range(8):
                act.wait_ge(xt_psum, j + 1)
                if j >= 2:
                    act.wait_ge(embed_psum, j - 1)
                act.copy(x_t[j % 2][h96, 4:8, :], ps[h96, 2 * (j % 2) + 1, :]).then_inc(xt_ready_a, 1)

            def token_view(q, i):
                tiles, half = XG[i]
                if half is None:
                    return x_part[h96, q].rearrange("p k (b n) -> p k b n", n=N)[:, :, :, 0]
                t = tiles[0] // SIDE
                return x_part[h96, q, half, t * T // 2:(t + 1) * T // 2].rearrange(
                    "p (b n) -> p b n", n=N)[:, :, 1:N].rearrange("p b (h w) -> p w b h", w=SIDE)

            def grouped(ap, i):
                if XG[i][1] is None:
                    return ap[h96, 0:2 * B].rearrange("p (w b) -> p w b", w=2)
                return ap[h96, 0:512].rearrange("p (w b h) -> p w b h", w=SIDE, b=B // 2)

            def highest(i):
                act.wait_ge(xnt_psum, i + 1)
                act.copy(token_view(0, i), grouped(ps[:, 6 + i % 2, :], i)).then_inc(hi_done, 1)

            highest(0)
            for i in range(5):
                if i < 4:
                    highest(i + 1)
                act.wait_ge(res_done, i + 1)
                act.copy(token_view(1, i), grouped(residue[i % 2], i)).then_inc(mid_done, 1)

            act.wait_ge(small_in, 16 * 6)
            act.wait_ge(lo_done, 5)
            for c in range(6):
                for s, (a, b) in enumerate(PIECES):
                    act.wait_ge(y_psum, 3 * c + s + 1)
                    act.activation(y_sb[h96, c, a:b], ps[h96, (c % 2) * 3 + s, 0:b - a], ACT.Identity,
                                   bias=bq_col[h96, c:c + 1], scale=w_scale[h96, c:c + 1]).then_inc(y_ready, 1)

            def bound(q, which):
                act.wait_ge(bound_in, which)
                act.activation(q[2], q[3], ACT.Identity, bias=magic_c, scale=q[1]).then_inc(bound_done, 1)

            bound(q_y, 1)
            act.wait_ge(y_ready, 18)
            for c in range(6):
                act.activation(y_sb[h96, c, :], y_sb[h96, c, :], ACT.Identity, bias=magic_c[h96],
                               scale=q_y[1][h96]).then_inc(rounded, 1)

            act.wait_ge(v_ready, 1)
            act.wait_ge(s_psum, 1)
            for g in range(2):
                vb = kv_t[h96, 2 + g, :].rearrange("p (b n) -> p b n", n=N)
                for h in range(HG):
                    ins = act.activation(v_exp_t[h96, g, :, h, :], vb, ACT.Copy, scale=head_mask[h96, h:h + 1])
                    if h < HG - 1:
                        mark(ins)
                    else:
                        ins.then_inc(v_exp_t_ready, 1)
            act.wait_ge(v_exp_t_ready, 2)
            bound(q_a, 2)

            act.activation(row_max[0:R], row_max[0:R], ACT.Identity, bias=magic_c[0:R],
                           scale=q_a[1][0:R]).then_inc(attn_scaled, 1)
            LH = L // 2
            V_, XI, QI, W_, E_, Y0 = soft
            QQ = soft_i[2]
            sv = ps[0:R, 0:5, 0:4 * M].rearrange("p b (l m) -> p b l m", m=N)
            v3 = V_[0:R].rearrange("p (b l) m -> p b l m", b=5)
            act.activation(v3[:, 0:2], sv[:, 0:2], ACT.Identity, bias=magic_c[0:R], scale=q_a[1][0:R])
            act.activation(v3[:, 2], sv[:, 2], ACT.Identity, bias=magic_c[0:R],
                           scale=q_a[1][0:R]).then_inc(attn_scaled, 1)
            act.activation(v3[:, 3:5], sv[:, 3:5], ACT.Identity, bias=magic_c[0:R],
                           scale=q_a[1][0:R]).then_inc(attn_scaled, 1)

            def v_out(n):
                g, b0 = n // 7, (n % 7) * VB
                m = min(VB, B - b0)
                act.wait_ge(v_psum, n + 1)
                act.copy(v_exp[0:M, g, b0:b0 + m, :],
                         bank_b(5 + n % 3)[0:M, 0:m * HALF].rearrange("p (b c) -> p b c", c=HALF)).then_inc(v_exp_ready, 1)

            for i in range(2):
                for n in range(2 * i, 2 * i + 2):
                    v_out(n)
                act.wait_ge(xi_ready, i + 1)
                act.activation(QQ[0:R, i * LH:(i + 1) * LH], XI[0:R, i * LH:(i + 1) * LH], ACT.Identity,
                               bias=q_bias[0:R], scale=x0_inv[0:R]).then_inc(q_ready, 1)
            for i in range(2):
                for n in range(4 + 5 * i, 9 + 5 * i):
                    v_out(n)
                act.wait_ge(e_ready, i + 1)
                act.wait_ge(act_s, mark(act.activation(Y0[0:R, i * LH:(i + 1) * LH], E_[0:R, i * LH:(i + 1) * LH], ACT.Ln)))
                act.activation(Y0[0:R, i * LH:(i + 1) * LH], Y0[0:R, i * LH:(i + 1) * LH], ACT.Exp,
                               scale=-1.0).then_inc(y0_ready, 1)
            bound(q_o, 3)
            act.wait_ge(av_psum, 2)
            for g in range(2):
                act.activation(o_v[h96, g, 0:2 * AVI * N].rearrange("p (s t) -> p s t", s=2),
                               ps[h96, 3 * g:3 * g + 2, 0:AVI * N], ACT.Identity, bias=magic_c[h96], scale=q_o[1][h96])
                act.activation(o_v[h96, g, 2 * AVI * N:T], ps[h96, 3 * g + 2, 0:T - 2 * AVI * N], ACT.Identity,
                               bias=magic_c[h96], scale=q_o[1][h96]).then_inc(rounded, 1)

            bound(q_p, 4)
            act.wait_ge(proj_ready, 1)
            act.activation(proj_v, proj, ACT.Identity, bias=magic_c, scale=q_p[1]).then_inc(rounded, 1)

            for i in range(1, 5, 2):
                act.wait_ge(xn2_psum, i + 1)
                xn2_out(act.copy, i).then_inc(xn2t_a, 1)
            act.wait_ge(lg_max, 1)
            act.activation(ex[:, :, :], ex[:, :, :], ACT.Exp).then_inc(ex_ready, 1)

            def tokens_out(t, k):
                act.wait_ge(xgt_psum, t + 1)
                act.copy(xg_t[k][h96].rearrange("p c t -> p (c t)"), ps[h96, 7, 0:256]).then_inc(xgt_ready, 1)

            def gelu(t, k):
                act.wait_ge(g1_psum, t + 1)
                if not isinstance(t, int) or t >= 2:
                    act.wait_ge(ht_psum, t - 1)
                act.activation(h_sb[k].rearrange("p (a f) -> p a f", a=2), ps[:, 2 * k:2 * k + 2, 0:FH],
                               ACT.Gelu).then_inc(h_ready, 1)

            tokens_out(0, 0)
            gelu(0, 0)
            tokens_out(1, 1)

            for t in range(SLOT_TILES):
                if t < SLOT_TILES - 1:
                    gelu(t + 1, (t + 1) % 2)
                if t < SLOT_TILES - 2:
                    tokens_out(t + 2, t % 2)


_INS = ['x', 'cls_tok', 'L0_tok_W', 'L0_tok_b', 'L0_attn_w_qkv', 'L0_attn_b_qkv', 'L0_attn_w_proj', 'L0_attn_b_proj',
        'L0_ffn_Ws', 'L0_ffn_bs', 'L0_ffn_W1', 'L0_ffn_b1', 'L0_ffn_W2', 'L0_ffn_b2']
_OUTS = [((64, 17, 192), 'float32')]


def kernel(**inputs):
    import numpy as _np
    import concourse.bacc as _bacc
    from concourse import mybir as _mybir
    from concourse.bass_utils import run_bass_kernel_spmd as _run

    nc = _bacc.Bacc("TRN2", target_bir_lowering=False, num_devices=1)
    arrays, args = {}, []
    for name in _INS:
        a = _np.ascontiguousarray(inputs[name])
        arrays[f"in_{name}_dram"] = a
        args.append(nc.dram_tensor(f"in_{name}_dram", a.shape, _mybir.dt.from_np(a.dtype), kind="ExternalInput").ap())
    for i, (shape, dtype) in enumerate(_OUTS):
        dt = _mybir.dt.from_np(_np.dtype(dtype))
        args.append(nc.dram_tensor(f"out_{i}_dram", shape, dt, kind="ExternalOutput").ap())
    vit_tower(nc, *args)
    r = _run(nc, [arrays], core_ids=[0])
    return r.results[0]["out_0_dram"]
```

```python
from contextlib import ExitStack

import numpy as np

import concourse.bass as bass
from concourse import mybir

ALU = mybir.AluOpType
ACT = mybir.ActivationFunctionType
AX = mybir.AxisListType
F32 = mybir.dt.float32
BF16 = mybir.dt.bfloat16
I32 = mybir.dt.int32
U32 = mybir.dt.uint32
RMAX = bass.bass_isa.ReduceOp.max

MAGIC = 12582912.0
QEPS = 1.1920928955078125e-07
LN_EPS = 1e-5
INV_255 = float(np.float32(1.0) / np.float32(255.0))
FOUR_THIRDS = float(np.float32(4.0) / np.float32(3.0))
EXP_MASK = 0x7F800000


def tally(sem):
    count = [0]

    def mark(instruction):
        instruction.then_inc(sem, 1)
        count[0] += 1
        return count[0]

    return mark, lambda: count[0]


def vit_tower(nc, x, cls_tok, tok_w, tok_b, w_qkv, b_qkv, w_proj, b_proj, ws, bs, w1, b1, w2, b2, out):
    B, IMG, _, CH = x.shape
    PATCH = 16
    SIDE = IMG // PATCH
    SEG = PATCH * CH
    C = tok_w.shape[1]
    HALF = C // 2
    HEADS, HD = 12, 16
    HG = HEADS // 2
    N = SIDE * SIDE + 1
    T = B * N
    NT = 9
    KC = PATCH * SEG // HALF
    E = ws.shape[1]
    F = w1.shape[2]
    FC = F // 128
    FH = F // 2
    GI = 7
    R = GI * N
    NG = -(-B // GI)
    M = HG * N
    L = NG * 2 * HG
    SLOT_TILES = (T + E * 127) // 128
    SLOTS = SLOT_TILES * 128
    COL_P, COL_ROW, COL_MEAN, COL_RSTD = C, C + 1, C + 2, C + 3
    PAYW = C + 4
    NO_ROW = 4 * T

    with ExitStack() as ctx:
        def sb(name, shape, dt=F32):
            return ctx.enter_context(nc.sbuf_tensor(name, shape, dt))

        def sem(name):
            return ctx.enter_context(nc.semaphore(name))

        slots = nc.dram_tensor("slots", (SLOTS, PAYW), F32, kind="Internal").ap()

        w1_sb = sb("w1_sb", [128, E, 2, F])
        w2_sb = sb("w2_sb", [128, E, FC, C])
        pay = sb("pay", [128, NT, PAYW])
        w_t = sb("w_t", [HALF, 2, 4 * C], BF16)
        ident = sb("ident", [128, 128])
        identb = sb("identb", [128, 128], BF16)
        small = sb("small", [128, 200])
        smalli = sb("smalli", [128, 40], I32)

        RA, RB, RC, RD = 6 * T, 7936, 6 * T, B * HALF
        area_a = sb("area_a", [128, RA + RB])
        area_c = sb("area_c", [128, RC])
        area_d = sb("area_d", [128, RD])

        def part(area, start, shape, dt=F32):
            n = int(np.prod(shape))
            words = n if dt != BF16 else -(-n // 2)
            v = area[:, start:start + words]
            if dt != F32:
                v = v.bitcast(dt)[:, 0:n]
            if len(shape) > 1:
                names = " ".join(f"d{i}" for i in range(len(shape)))
                v = v.rearrange(f"p ({names}) -> p {names}", **{f"d{i}": s for i, s in enumerate(shape) if i})
            return v

        x_sb = part(area_a, 0, [2, PATCH, SIDE, SEG])
        x_c = part(area_c, 0, [8, PATCH * SEG])
        x_t = [part(area_a, RA + 1024 * i, [KC, 128]) for i in range(2)]
        y_sb = part(area_a, 0, [6, T])
        xn = part(area_d, 0, [NT, C])
        residue = [part(area_d, NT * C + 512 * i, [512]) for i in range(2)]
        qmask = part(area_a, RA, [2, B, R], BF16)
        w_row = part(area_d, 0, [8, C])
        w_int = part(area_d, 8 * C, [8, C], BF16)
        w_v = part(area_d, 12 * C, [8, C])
        tokw_sb = part(area_d, 20 * C, [KC, C])
        b_row = part(area_d, 28 * C, [HALF])
        x_part = part(area_c, 0, [3, 2, T], BF16)
        kv_t = part(area_d, 0, [4, T], BF16)
        k_exp = part(area_c, 0, [2, B, HG, N], BF16)
        v_exp_t = part(area_a, 0, [2, B, HG, N], BF16)
        v_exp = part(area_d, 0, [2, B, HALF], BF16)
        SW = L * N
        assert SW * 3 <= RC and SW <= B * M // 2 * 40 // 64
        soft, soft_i = ([part(area_c if i < 3 else area_a, SW * (i % 3), [L, N], dt) for i in range(4)]
                        for dt in (F32, I32))
        probs = part(area_a, RA, [NG * 2, M], BF16)
        probs_t = part(area_a, RA + SW // 2, [NG * 2, R], BF16)
        o_q = part(area_c, 0, [2, T], BF16)
        o_v = part(area_a, 0, [2, T])
        proj = part(area_a, 2 * T, [NT, C])
        proj_v = part(area_a, 2 * T + NT * C, [NT, C])
        xn2 = part(area_a, 0, [NT, C])
        xn2_t = part(area_a, NT * C, [2, NT, 128])
        xg = part(area_a, 0, [SLOT_TILES, PAYW])
        o = SLOT_TILES * PAYW
        xg_n = [part(area_a, o + C * i, [C]) for i in range(2)]
        o += 2 * C
        xg_t = [part(area_a, o + 256 * i, [2, 128]) for i in range(2)]
        o += 512
        w1_tile = [part(area_a, o + 2 * F * i, [2, F]) for i in range(2)]
        o += 4 * F
        h_t = [part(area_a, o + F * i, [FC, 128]) for i in range(2)]
        o += 2 * F
        y_b = [part(area_a, o + C * i, [C]) for i in range(2)]
        o += 2 * C
        y_out = [part(area_a, o + C * i, [C]) for i in range(2)]
        o += 2 * C
        assert o <= RA + RB
        b2_rows = part(area_c, 2048, [E, C])
        fill = part(area_c, 2048 + E * C, [PAYW])
        head_mask = small[:, 0:6]
        o = 6

        def cols(n):
            nonlocal o
            v = small[:, o:o + n]
            o += n
            return v

        w_max, w_min, w_scale, w_inv, w_him = (cols(8) for _ in range(5))
        bq_col = cols(6)
        magic_c = cols(1)
        exp_c = cols(1)
        stat = cols(2 * 19).rearrange("p (s c) -> p s c", s=2)
        gin = cols(2)
        gout = cols(2)
        q_y, q_a, q_o, q_p = ([cols(1) for _ in range(4)] for _ in range(4))
        a_mul = cols(1)
        pol = cols(3)
        pol_t, pol_f, pol_g = cols(3), cols(3), cols(3)
        x0_30, x0_inv, q_bias, x0_pos = cols(1), cols(1), cols(1), cols(1)
        assert o <= 200
        rows = sb("rows", [128, 3, C])
        bs_row = sb("bs_row", [128, E])
        ws_sb = sb("ws_sb", [HALF, 2, E])
        row_max = sb("row_max", [128, L])
        row_sum = sb("row_sum", [128, L])
        bn = sb("bn", [128, NT, 6])
        mv = sb("mv", [128, NT, 2])
        rstd = sb("rstd", [128, NT])
        pow_e = sb("pow_e", [128, NT])
        lg, ex, hot, rk = (part(area_a, 8000 + NT * E * i, [NT, E]) for i in range(4))
        hot_b = part(area_a, 8000 + NT * E * 4, [NT, E], BF16)
        te = part(area_a, 8000 + NT * E * 5, [SLOT_TILES, E])
        e_idx = sb("e_idx", [128, NT, E])
        tri = sb("tri", [128, 128], BF16)
        ones_b = sb("ones_b", [128, 128], BF16)
        n9 = [sb(f"n9_{i}", [128, NT]) for i in range(3)]
        e8 = [sb(f"e8_{i}", [128, E]) for i in range(4)]
        dest = sb("dest", [128, NT], U32)
        te_idx = sb("te_idx", [128, SLOT_TILES])
        tile_expert = sb("tile_expert", [128, SLOT_TILES], I32)

        ps = ctx.enter_context(nc.psum_tensor("ps", [128, 8, 512], F32))

        def bank_b(b):
            return ps[:, b, :].bitcast(BF16)

        x_in = [sem(f"x_in{i}") for i in range(2)]
        w_in, tokw_in, small_in, w1_in, w2_in, b2_in = (sem(n) for n in ("w_in", "tokw_in", "small_in", "w1_in", "w2_in", "b2_in"))
        consts = sem("consts")
        vec, act_s, pool_s = sem("vec"), sem("act_s"), sem("pool_s")
        w_int_ready, w_t_psum, w_t_ready, w_scales_psum, diag_ready = (sem(n) for n in (
            "w_int_ready", "w_t_psum", "w_t_ready", "w_scales_psum", "diag_ready"))
        packed_v, packed_a, bq_in, bq_ready = (sem(n) for n in ("packed_v", "packed_a", "bq_in", "bq_ready"))
        xt_psum, xt_ready_v, xt_ready_a, embed_psum, embed_done = (sem(n) for n in (
            "xt_psum", "xt_ready_v", "xt_ready_a", "embed_psum", "embed_done"))
        var_ready, rstd_ready, xn_ready, xnt_psum, hi_done, res_done, mid_done, lo_done = (sem(n) for n in (
            "var_ready", "rstd_ready", "xn_ready", "xnt_psum", "hi_done", "res_done", "mid_done", "lo_done"))
        y_psum, y_ready = sem("y_psum"), sem("y_ready")
        stat_ready, all_max = sem("stat_ready"), sem("all_max")
        bound_in, bound_done, rounded = sem("bound_in"), sem("bound_done"), sem("rounded")
        qmask_zero, qmask_ready, k_exp_ready = sem("qmask_zero"), sem("qmask_ready"), sem("k_exp_ready")
        v_ready, s_psum, v_exp_t_ready, v_psum, v_exp_ready = (sem(n) for n in (
            "v_ready", "s_psum", "v_exp_t_ready", "v_psum", "v_exp_ready"))
        attn_scaled, xi_ready, q_ready, e_ready, y0_ready, power_ready, p_ready, pt_psum, pt_ready_v, pt_ready_a, av_psum = (sem(n) for n in (
            "attn_scaled", "xi_ready", "q_ready", "e_ready", "y0_ready", "power_ready", "p_ready", "pt_psum", "pt_ready_v", "pt_ready_a", "av_psum"))
        oq_ready, proj_psum, xn2_ready, xn2_psum, xn2t_v, xn2t_a, lg_psum = (sem(n) for n in (
            "oq_ready", "proj_psum", "xn2_ready", "xn2_psum", "xn2t_v", "xn2t_a", "lg_psum"))
        lg_max, ex_ready, hot_ready, rank_psum, dest_ready, table_ready = (sem(n) for n in (
            "lg_max", "ex_ready", "hot_ready", "rank_psum", "dest_ready", "table_ready"))
        filled, scattered, slots_in0, slots_in1 = (sem(n) for n in ("filled", "scattered", "slots_in0", "slots_in1"))
        xg_ready, xgt_psum, xgt_ready, w1_tile_ready, g1_psum, h_ready, g2_psum, y_b_done, y_done, stored, stored1 = (sem(n) for n in (
            "xg_ready", "xgt_psum", "xgt_ready", "w1_tile_ready", "g1_psum", "h_ready", "g2_psum", "y_b_done", "y_done", "stored", "stored1"))

        block = ctx.enter_context(nc.Block())

        XG = [(range(0, 4), 0), (range(0, 4), 1), (range(8, 9), None), (range(4, 8), 0), (range(4, 8), 1)]
        XG_A = 3
        PIECES = [(0, 512), (1024, T), (512, 1024)]

        def y_bank(c, s):
            a, b = PIECES[s]
            return (c, 0) if s != 1 else (6, c * (b - a))
        LN1_TILES = [0, 1, 2, 3, 8, 4, 5, 6, 7]
        LN1_COLS = [(0, 5), (5, 9)]
        VB = 10
        AVI = 16
        PT_BANK = (5, 6, 6, 7)

        def av_bank(g, b):
            return b // (B // 2) * 4 + 2 * g + b % (B // 2) // AVI

        CONSTS = 20
        P_FILL = 2
        W_TBANK = 6

        def xn2_out(copy, i):
            bank = (5, 6, 7, 5, 6)[i]
            m = min(4, 18 - 4 * i) // 2
            w = 128 if i < 4 else B
            src = ps[0:HALF, bank, 0:m * 256].rearrange("p (j k t) -> p j k t", k=2, t=128)[:, :, :, 0:w]
            dst = xn2_t[0:HALF, :, 2 * i:2 * i + m, 0:w].rearrange("p k j t -> p j k t")
            if m == 1:
                return copy(dst[:, 0], src[:, 0])
            return copy(dst, src)

        def probs_out(copy, n):
            return copy(probs_t[0:M, 5 * n:5 * n + 5, :],
                        bank_b(PT_BANK[n])[0:M, 0:5 * 128].rearrange("p (a r) -> p a r", r=128)[:, :, 0:R])

        def spread(engine, blocks, rows_t, g, heads, done, mark):
            for h in heads:
                ins = engine.tensor_scalar(blocks[0:HALF, g, :, h, :], rows_t.rearrange("p (b n) -> p b n", n=N),
                                           head_mask[0:HALF, h:h + 1], None, ALU.mult)
                if h == heads[-1]:
                    ins.then_inc(done, 1)
                else:
                    mark(ins)

        @block.sync
        def _(sp):
            xr = x.rearrange("(t b) (h r) w c -> t (b h) (r w c)", t=2, r=PATCH)
            for t in range(2):
                sp.dma_start(area_a[:, t * PATCH * IMG * CH:(t + 1) * PATCH * IMG * CH], xr[t]).then_inc(x_in[t], 16)
            for t in range(2):
                sp.wait_ge(x_in[t], 16)
            sp.wait_ge(tokw_in, 16)
            sp.wait_ge(w_in, 32)
            sp.dma_start(w1_sb[0:HALF, :, 0, :], w1[:, 0:HALF, :].rearrange("e d f -> d e f")).then_inc(w1_in, 16)
            sp.dma_start(w1_sb[0:HALF, :, 1, :], w1[:, HALF:C, :].rearrange("e d f -> d e f")).then_inc(w1_in, 16)
            sp.dma_start(w1_sb[HALF:HALF + 1, :, 0, :], b1.unsqueeze(0)).then_inc(w1_in, 16)
            for c in range(FC):
                sp.dma_start(w2_sb[:, :, c, :], w2[:, c * 128:(c + 1) * 128, :].rearrange("e p d -> p e d")).then_inc(w2_in, 16)
            sp.wait_ge(pool_s, P_FILL)
            sp.dma_start(slots.rearrange("(t p) c -> p t c", p=128),
                         fill.unsqueeze(1).to_broadcast([128, SLOT_TILES, PAYW])).then_inc(filled, 16)
            sp.dma_start(b2_rows.rearrange("p e c -> p (e c)"),
                         b2.rearrange("e c -> (e c)").partition_broadcast(128)).then_inc(b2_in, 16)
            sp.wait_ge(scattered, 16 * NT)
            sl = slots.rearrange("(t p) c -> p t c", p=128)
            sp.dma_start(xg[:, 0:2, :], sl[:, 0:2, :]).then_inc(slots_in0, 16)
            sp.dma_start(xg[:, 2:SLOT_TILES, :], sl[:, 2:SLOT_TILES, :]).then_inc(slots_in1, 16)

        @block.gpsimd
        def _(pool):
            mark, _ = tally(consts)
            mark(pool.memset(ident[:, :], 0.0))
            mark(pool.memset(identb[:, :], 0.0))
            mark(pool.memset(head_mask, 1.0))
            mark(pool.memset(tri[:, :], 1.0))
            mark(pool.memset(ones_b[:, :], 1.0))
            mark(pool.memset(magic_c, MAGIC))
            mark(pool.memset(exp_c, 157.0 * 2.0 ** 23))
            mark(pool.memset(pow_e[:, :], -0.5))
            mark(pool.memset(gin, 0.0))
            n = mark(pool.memset(rows[:, 2, :], 1.0))
            pool.wait_ge(consts, n)
            mark(pool.affine_select(out=ident[:, :], in_=ident[:, :], compare_op=ALU.not_equal, fill=1.0,
                                    base=0, pattern=[[-1, 128]], channel_multiplier=1))
            mark(pool.affine_select(out=identb[:, :], in_=identb[:, :], compare_op=ALU.not_equal, fill=1.0,
                                    base=0, pattern=[[-1, 128]], channel_multiplier=1))
            mark(pool.affine_select(out=tri[:, :], in_=tri[:, :], compare_op=ALU.is_gt, fill=0.0,
                                    base=0, pattern=[[1, 128]], channel_multiplier=-1))
            n = mark(pool.affine_select(out=head_mask, in_=head_mask, compare_op=ALU.is_ge, fill=0.0,
                                        base=0, pattern=[[-HD, HG]], channel_multiplier=1))
            pool.wait_ge(consts, n)
            mark(pool.affine_select(out=head_mask, in_=head_mask, compare_op=ALU.is_ge, fill=0.0,
                                    base=HD - 1, pattern=[[HD, HG]], channel_multiplier=-1))
            mark(pool.iota(e_idx[:, :, :], [[0, NT], [1, E]], base=0, channel_multiplier=0,
                           allow_small_or_imprecise_dtypes=True))
            mark(pool.iota(te_idx[:, :], [[1, SLOT_TILES]], base=0, channel_multiplier=0,
                           allow_small_or_imprecise_dtypes=True))
            mark(pool.iota(smalli[:, 0:1], [[0, 1]], base=0, channel_multiplier=1))
            mark(pool.iota(smalli[:, 1:1 + NT - 1], [[N * B // 2, 2], [1, SIDE]], base=1, channel_multiplier=SIDE))
            assert mark(pool.iota(smalli[:, NT:NT + 1], [[0, 1]], base=0, channel_multiplier=N)) == CONSTS

            for i, (a, b) in enumerate(LN1_COLS):
                pool.wait_ge(var_ready, i + 1)
                pool.tensor_tensor(rstd[:, a:b], mv[:, a:b, 1], pow_e[:, a:b], ALU.pow).then_inc(rstd_ready, 1)
            pool.wait_ge(embed_psum, 8)
            pool.memset(part(area_a, RA, [RB]), 0.0).then_inc(qmask_zero, 1)
            for i in range(3):
                pool.wait_ge(stat_ready, i + 1)
                pool.partition_all_reduce(gout, gin, 128, RMAX).then_inc(all_max, 1)
            pool.wait_ge(p_ready, 2)
            pool.memset(fill, 0.0).then_inc(pool_s, 1)
            pool.wait_ge(pool_s, 1)
            pool.memset(fill[:, COL_ROW:COL_ROW + 1].bitcast(I32), NO_ROW).then_inc(pool_s, 1)
            pool.wait_ge(stat_ready, 4)
            pool.partition_all_reduce(gout, gin, 128, RMAX).then_inc(all_max, 1)
            pool.wait_ge(var_ready, 3)
            pool.tensor_tensor(pay[:, :, COL_RSTD], rstd[:, :], pow_e[:, :], ALU.pow).then_inc(rstd_ready, 1)
            pool.wait_ge(dest_ready, 1)
            pool.wait_ge(filled, 16)
            for j in range(NT):
                n = 128 if j < NT - 1 else B
                pool.indirect_dma_start(out=slots, out_offset=bass.IndirectOffsetOnAxis(ap=dest[0:n, j:j + 1], axis=0),
                                        in_=pay[0:n, j, :], in_offset=None, bounds_check=SLOTS - 1,
                                        oob_is_err=False).then_inc(scattered, 16)
            out_rows = out.rearrange("b n c -> (b n) c")

            def store(t, k):
                pool.wait_ge(y_done, t + 1)
                row = xg[:, t, COL_ROW:COL_ROW + 1].bitcast(U32)
                pool.indirect_dma_start(out=out_rows, out_offset=bass.IndirectOffsetOnAxis(ap=row, axis=0),
                                        in_=y_out[k], in_offset=None, bounds_check=T - 1,
                                        oob_is_err=False).then_inc((stored, stored1)[k], 16)

            for t in range(SLOT_TILES):
                store(t, t % 2)
            pool.wait_ge(stored, 16 * SLOT_TILES // 2)
            pool.wait_ge(stored1, 16 * SLOT_TILES // 2)

        @block.tensor
        def _(pe):
            pe.wait_ge(consts, CONSTS)

            def turn_weights(k):
                pe.wait_ge(w_int_ready, 8)
                for c in range(8):
                    mm = pe.transpose(bank_b(W_TBANK + k)[0:HALF, c * HALF:(c + 1) * HALF],
                                      w_int[0:HALF, c, k * HALF:(k + 1) * HALF], identb[0:HALF, 0:HALF])
                mm.then_inc(w_t_psum, 1)

            def turn_vectors():
                pe.wait_ge(diag_ready, 2)
                pe.wait_ge(w_t_ready, 1)
                pe.wait_ge(bq_in, 16)
                for g in range(2):
                    pe.matmul(ps[:, W_TBANK, g * HALF:(g + 1) * HALF], rows[0:HALF, 2, 0:128],
                              w_v[0:HALF, g, 0:HALF], start=True, stop=True)
                pe.transpose(ps[0:HALF, W_TBANK, C:C + 6], b_row[0:6, :], ident[0:6, 0:6]).then_inc(w_scales_psum, 1)

            def turn_patches(j):
                pe.wait_ge((packed_v, packed_a)[j % 2], j // 2 + 1)
                if j >= 2:
                    pe.wait_ge(xt_ready_v, j - 1)
                    pe.wait_ge(xt_ready_a, j - 1)
                for k in range(KC):
                    mm = pe.transpose(ps[0:HALF, 2 * (j % 2) + k // 4, (k % 4) * 128:(k % 4 + 1) * 128],
                                      x_c[:, j, k * HALF:(k + 1) * HALF], ident[:, :])
                mm.then_inc(xt_psum, 1)

            def embed(j):
                pe.wait_ge(xt_ready_v, j + 1)
                pe.wait_ge(xt_ready_a, j + 1)
                if j == 0:
                    pe.wait_ge(tokw_in, 16)
                if j >= 2:
                    pe.wait_ge(embed_done, j - 1)
                for k in range(KC):
                    mm = pe.matmul(ps[:, 4 + j % 2, 0:C], x_t[j % 2][0:HALF, k, :], tokw_sb[0:HALF, k, :],
                                   start=k == 0, stop=k == KC - 1)
                mm.then_inc(embed_psum, 1)

            def turn_normalised(i):
                tiles, half = XG[i]
                pe.wait_ge(xn_ready, 5 if i < XG_A else NT)
                if i < 2:
                    pe.wait_ge(w_t_ready, 3)
                    pe.wait_ge(bq_ready, 1)
                else:
                    pe.wait_ge(res_done, i - 1)
                n = 0
                for k in ([half] if half is not None else [0, 1]):
                    for j in tiles:
                        w = 128 if j < NT - 1 else B
                        mm = pe.transpose(ps[0:HALF, 6 + i % 2, n:n + w], xn[0:w, j, k * HALF:(k + 1) * HALF],
                                          ident[0:w, 0:w])
                        n += w
                mm.then_inc(xnt_psum, 1)

            turn_patches(0)
            turn_patches(1)
            embed(0)
            turn_patches(2)
            embed(1)
            turn_patches(3)
            embed(2)
            turn_patches(4)
            embed(3)
            turn_weights(0)
            turn_weights(1)
            turn_patches(5)
            embed(4)
            turn_vectors()
            turn_patches(6)
            embed(5)
            turn_normalised(0)
            turn_normalised(1)
            turn_patches(7)
            embed(6)
            turn_normalised(2)
            embed(7)

            def y_of(s, c):
                a, b = PIECES[s]
                bank, col = y_bank(c, s)
                if s == 0 and c >= 4:
                    pe.wait_ge(embed_done, c + 3)
                if s == 2:
                    pe.wait_ge(y_ready, c + 1)
                for n, (k, q) in enumerate([(k, q) for q in range(3) for k in range(2)]):
                    mm = pe.matmul(ps[0:HALF, bank, col:col + b - a], w_t[:, k, c * HALF:(c + 1) * HALF],
                                   x_part[0:HALF, q, k, a:b], start=n == 0, stop=n == 5)
                mm.then_inc(y_psum, 1)

            pe.wait_ge(lo_done, XG_A)
            for c in range(3):
                y_of(0, c)
            turn_normalised(3)
            turn_normalised(4)
            for c in range(3, 6):
                y_of(0, c)
            pe.wait_ge(lo_done, 5)
            for s in (1, 2):
                for c in range(6):
                    y_of(s, c)

            for g in range(2):
                pe.wait_ge(qmask_ready, g + 1)
                pe.wait_ge(k_exp_ready, g + 1)
                for G in range(NG):
                    images = range(GI * G, min(GI * G + GI, B))
                    for b in images:
                        mm = pe.matmul(ps[0:R, G // 2, (G % 2) * 2 * M + g * M:(G % 2) * 2 * M + (g + 1) * M],
                                       qmask[0:HALF, g, b, :], k_exp[0:HALF, g, b, :, :],
                                       start=b == images[0], stop=b == images[-1])
                    if g == 1 and G % 2 == 1:
                        mm.then_inc(s_psum, 1)

            n = 0
            pe.wait_ge(v_exp_t_ready, 2)
            for g in range(2):
                for b0 in range(0, B, VB):
                    if n >= 3:
                        pe.wait_ge(v_exp_ready, n - 2)
                    for b in range(b0, min(b0 + VB, B)):
                        mm = pe.transpose(bank_b(5 + n % 3)[0:M, (b - b0) * HALF:(b - b0 + 1) * HALF],
                                          v_exp_t[0:HALF, g, b, :, :], identb[0:HALF, 0:HALF])
                    mm.then_inc(v_psum, 1)
                    n += 1
            NV = n

            def turn_probs(n):
                for i in range(5 * n, 5 * n + 5):
                    mm = pe.transpose(bank_b(PT_BANK[n])[0:M, (i % 5) * 128:(i % 5) * 128 + R],
                                      probs[0:R, i, :], identb[0:R, 0:R])
                mm.then_inc(pt_psum, 1)

            def attend(g, images):
                for b in images:
                    mm = pe.matmul(ps[0:HALF, av_bank(g, b), (b % AVI) * N:(b % AVI + 1) * N],
                                   v_exp[0:M, g, b, :], probs_t[0:M, 2 * (b // GI) + g, (b % GI) * N:(b % GI + 1) * N],
                                   start=True, stop=True)
                return mm

            pe.wait_ge(v_exp_ready, NV)
            pe.wait_ge(p_ready, 1)
            turn_probs(0)
            turn_probs(1)
            pe.wait_ge(pt_ready_a, 2)
            for g in range(2):
                attend(g, range(0, B // 2)).then_inc(av_psum, 1)
            pe.wait_ge(p_ready, 2)
            turn_probs(2)
            turn_probs(3)
            pe.wait_ge(pt_ready_a, 3)
            pe.wait_ge(pt_ready_v, 1)
            for g in range(2):
                attend(g, range(B // 2, B)).then_inc(av_psum, 1)

            for j in range(NT):
                if j % SIDE == 0:
                    pe.wait_ge(oq_ready, (2, 4, 5)[j // SIDE])
                w = 128 if j < NT - 1 else B
                for g in range(2):
                    mm = pe.matmul(ps[0:w, j // 2, (j % 2) * C:(j % 2 + 1) * C], o_q[0:HALF, g, j * 128:j * 128 + w],
                                   w_t[:, g, 3 * C:4 * C], start=g == 0, stop=g == 1)
                if j % 2 == 1 or j == NT - 1:
                    mm.then_inc(proj_psum, 1)

            pe.wait_ge(xn2_ready, NT)
            for i in range(5):
                bank = (5, 6, 7, 5, 6)[i]
                if i >= 3:
                    pe.wait_ge((xn2t_v, xn2t_a)[(i - 3) % 2], (i - 3) // 2 + 1)
                for n in range(4 * i, min(4 * i + 4, 18)):
                    j, k = n // 2, n % 2
                    w = 128 if j < NT - 1 else B
                    mm = pe.transpose(ps[0:HALF, bank, (n % 4) * 128:(n % 4) * 128 + w],
                                      xn2[0:w, j, k * HALF:(k + 1) * HALF], ident[0:w, 0:w])
                mm.then_inc(xn2_psum, 1)
            pe.wait_ge(xn2t_v, 3)
            pe.wait_ge(xn2t_a, 2)
            for j in range(NT):
                w = 128 if j < NT - 1 else B
                for k in range(2):
                    mm = pe.matmul(ps[0:w, 7, j * E:(j + 1) * E], xn2_t[0:HALF, k, j, 0:w], ws_sb[:, k, :],
                                   start=k == 0, stop=k == 1)
            mm.then_inc(lg_psum, 1)
            pe.wait_ge(hot_ready, 1)
            pe.matmul(ps[:, 0, 0:NT * E], tri[:, :], hot_b[:, :, :], start=True, stop=False, skip_group_check=True)
            for j in range(NT - 1):
                pe.matmul(ps[:, 0, (j + 1) * E:NT * E], ones_b[:, :],
                          hot_b[:, j:j + 1, :].to_broadcast([128, NT - 1 - j, E]), start=False, stop=j == NT - 2,
                          skip_group_check=True)
            for j in range(NT):
                mm = pe.matmul(ps[:, 1, 0:E], ones_b[:, :], hot_b[:, j, :], start=j == 0, stop=j == NT - 1)
            mm.then_inc(rank_psum, 1)

            pe.wait_ge(table_ready, 1)
            pe.wait_ge(w2_in, 16 * FC)

            def turn_tokens(t, k):
                pe.wait_ge(xg_ready, t + 1)
                if not isinstance(t, int) or t >= 1:
                    pe.wait_ge(xgt_ready, t)
                for c in range(2):
                    mm = pe.transpose(ps[0:HALF, 7, c * 128:(c + 1) * 128], xg_n[k][:, c * HALF:(c + 1) * HALF],
                                      ident[:, :])
                mm.then_inc(xgt_psum, 1)

            def first_product(t, k):
                pe.wait_ge(xgt_ready, t + 1)
                pe.wait_ge(w1_tile_ready, 2 * t + 2)
                if not isinstance(t, int) or t >= 2:
                    pe.wait_ge(h_ready, t - 1)
                for f in range(FC):
                    for c in range(2):
                        p = HALF + 1 if c == 0 else HALF
                        mm = pe.matmul(ps[:, 2 * k + f // 3, (f % 3) * 128:(f % 3 + 1) * 128],
                                       w1_tile[k][0:p, c, f * 128:(f + 1) * 128], xg_t[k][0:p, c, :],
                                       start=c == 0, stop=c == 1)
                mm.then_inc(g1_psum, 1)

            def second_product(t, k):
                e = pe.value_load(tile_expert[0:1, bass.ds(t, 1)], min_val=0, max_val=E - 1)
                pe.wait_ge(h_ready, t + 1)
                if not isinstance(t, int) or t >= 2:
                    pe.wait_ge(y_done, t - 1)
                for f in range(FC):
                    mm = pe.matmul(ps[:, 4 + k, 0:C], h_t[k][:, f, :], w2_sb[:, bass.ds(e, 1), f, :],
                                   start=f == 0, stop=f == FC - 1)
                mm.then_inc(g2_psum, 1)

            turn_tokens(0, 0)
            turn_tokens(1, 1)
            first_product(0, 0)

            def step(t, k, more=2):
                if more >= 2:
                    turn_tokens(t + 2, k)
                if more >= 1:
                    first_product(t + 1, 1 - k)
                second_product(t, k)

            step(0, 0)
            step(1, 1)
            with pe.Fori(2, SLOT_TILES - 2, 2) as t:
                step(t, 0)
                step(t + 1, 1)
            step(SLOT_TILES - 2, 0, 1)
            step(SLOT_TILES - 1, 1, 0)

        @block.vector
        def _(v):
            mark, marked = tally(vec)

            def then(instruction):
                v.wait_ge(vec, mark(instruction))

            mark(v.memset(pay[B:128, NT - 1, :], 0.0))
            mark(v.memset(stat[:, :, :], 0.0))
            wr = w_row[0:HALF]
            h96 = slice(0, HALF)

            def pack(j):
                v.wait_ge(x_in[j // SIDE], 16)
                v.tensor_copy(x_c[:, j, :].rearrange("p (r s) -> p r s", s=SEG),
                              x_sb[:, j // SIDE, :, j % SIDE, :]).then_inc(packed_v, 1)

            def patches_out(j):
                v.wait_ge(xt_psum, j + 1)
                if j >= 2:
                    v.wait_ge(embed_psum, j - 1)
                v.tensor_copy(x_t[j % 2][h96, 0:4, :], ps[h96, 2 * (j % 2), :]).then_inc(xt_ready_v, 1)

            def embedded(j):
                v.wait_ge(embed_psum, j + 1)
                v.tensor_tensor(pay[:, j, 0:C], ps[:, 4 + j % 2, 0:C], rows[:, 0, :], ALU.add).then_inc(embed_done, 1)
                v.wait_ge(embed_done, j + 1)
                mark(v.bn_stats(bn[:, LN1_TILES.index(j), :], pay[:, j, 0:C]))

            def weight_scales():
                mark(v.tensor_scalar(w_max[h96], w_max[h96], 0.0, None, ALU.max))
                then(v.tensor_scalar(w_min[h96], w_min[h96], 0.0, None, ALU.min))
                then(v.tensor_tensor(w_scale[h96], w_max[h96], w_min[h96], ALU.subtract))
                then(v.tensor_scalar(w_scale[h96], w_scale[h96], INV_255, QEPS, ALU.mult, ALU.max))
                then(v.reciprocal(w_inv[h96], w_scale[h96]))
                then(v.tensor_tensor(w_him[h96], w_min[h96], w_inv[h96], ALU.mult))
                then(v.tensor_scalar(w_him[h96], w_him[h96], MAGIC, 255.0, ALU.add, ALU.add))

            def weight_rounded(chunks):
                for c in chunks:
                    mark(v.tensor_scalar(w_v[h96, c], wr[:, c], w_inv[h96, c:c + 1], MAGIC, ALU.mult, ALU.add))

            def weight_integers(chunks, n):
                v.wait_ge(vec, n)
                for c in chunks:
                    v.tensor_scalar(w_int[h96, c], w_v[h96, c], w_him[h96, c:c + 1], MAGIC, ALU.min,
                                    ALU.subtract).then_inc(w_int_ready, 1)

            def weights_out(k):
                v.wait_ge(w_t_psum, k + 1)
                v.tensor_copy(w_t[:, k, :], bank_b(W_TBANK + k)[h96, 0:8 * HALF]).then_inc(w_t_ready, 1)

            def normalise_part(i):
                a, b = LN1_COLS[i]
                for n in range(a, b):
                    last = mark(v.bn_aggr(mv[:, n, :], bn[:, n, :]))
                v.wait_ge(vec, last)
                v.tensor_scalar(mv[:, a:b, 1], mv[:, a:b, 1], LN_EPS, None, ALU.add).then_inc(var_ready, 1)
                v.wait_ge(rstd_ready, i + 1)
                for n in range(a, b):
                    j = LN1_TILES[n]
                    v.tensor_scalar(xn[:, j, :], pay[:, j, 0:C], mv[:, n, 0:1], rstd[:, n:n + 1], ALU.subtract,
                                    ALU.mult).then_inc(xn_ready, 1)

            pack(0)
            pack(2)
            patches_out(0)
            v.wait_ge(w_in, 32)
            mark(v.tensor_reduce(w_max[h96], wr, AX.X, ALU.max))
            patches_out(1)
            then(v.tensor_reduce(w_min[h96], wr, AX.X, ALU.min))
            v.wait_ge(small_in, 16 * 5)
            embedded(0)
            pack(4)
            patches_out(2)
            weight_scales()
            embedded(1)
            pack(6)
            patches_out(3)
            weight_rounded(range(8))
            rounded_at = marked()
            embedded(2)
            patches_out(4)
            weight_integers(range(8), rounded_at)
            embedded(3)
            v.wait_ge(consts, CONSTS)
            v.wait_ge(w_int_ready, 8)
            for g in range(2):
                v.tensor_scalar(w_v[h96, g, 0:HALF], ident[h96, 0:HALF], w_scale[h96, 6 + g:7 + g], None,
                                ALU.mult).then_inc(diag_ready, 1)
            weights_out(0)
            weights_out(1)
            patches_out(5)
            last = mark(v.bn_stats(bn[:, 4, :], pay[:, 8, 0:C]))
            v.wait_ge(vec, last)
            normalise_part(0)
            embedded(4)
            v.wait_ge(w_scales_psum, 1)
            v.tensor_copy(rows[:, 2, :], ps[:, W_TBANK, 0:C]).then_inc(w_t_ready, 1)
            v.tensor_copy(bq_col[h96], ps[h96, W_TBANK, C:C + 6]).then_inc(bq_ready, 1)
            patches_out(6)

            def token_view(q, k, i):
                tiles, half = XG[i]
                if half is None:
                    return x_part[h96, q].rearrange("p k (b n) -> p k b n", n=N)[:, :, :, 0]
                t = tiles[0] // SIDE
                return x_part[h96, q, half, t * T // 2:(t + 1) * T // 2].rearrange(
                    "p (b n) -> p b n", n=N)[:, :, 1:N].rearrange("p b (h w) -> p w b h", w=SIDE)

            def split(i):
                tiles, half = XG[i]
                n = 512 if half is not None else 2 * B
                shape = dict(w=SIDE, b=B // 2) if half is not None else dict(w=2)
                pat = "p (w b h) -> p w b h" if half is not None else "p (w b) -> p w b"
                return n, (lambda ap: ap[h96, 0:n].rearrange(pat, **shape))

            def residue_of(i):
                n, view = split(i)
                v.wait_ge(hi_done, i + 1)
                if i >= 2:
                    v.wait_ge(lo_done, i - 1)
                v.tensor_tensor(view(residue[i % 2]), view(ps[:, 6 + i % 2, :]), token_view(0, None, i),
                                ALU.subtract).then_inc(res_done, 1)

            def lowest(i):
                n, view = split(i)
                v.wait_ge(mid_done, i + 1)
                v.tensor_tensor(token_view(2, None, i), view(residue[i % 2]), token_view(1, None, i),
                                ALU.subtract).then_inc(lo_done, 1)

            embedded(5)
            residue_of(0)
            patches_out(7)
            residue_of(1)
            lowest(0)
            lowest(1)
            embedded(6)
            residue_of(2)
            lowest(2)
            then(v.tensor_scalar(smalli[:, 20:21], smalli[:, 0:1], 2, None, ALU.arith_shift_right))
            then(v.tensor_copy(n9[0][:, 0:1], smalli[:, 20:21]))
            mark(v.tensor_scalar(pay[:, 0:NT - 1, COL_ROW].bitcast(I32), smalli[:, 1:NT], n9[0][:, 0:1], None, ALU.add))
            mark(v.tensor_copy(pay[0:B, NT - 1, COL_ROW:COL_ROW + 1].bitcast(I32), smalli[0:B, NT:NT + 1]))
            embedded(7)
            v.wait_ge(vec, marked())
            normalise_part(1)
            residue_of(3)
            residue_of(4)
            lowest(3)
            lowest(4)

            def extremes_of(p, i, values, n=1):
                mark(v.tensor_reduce(stat[p, 0, 1 + i:1 + i + n], values, AX.X, ALU.max))
                mark(v.tensor_reduce(stat[p, 1, 1 + i:1 + i + n], values, AX.X, ALU.min, negate=True))

            for s, (a, b) in enumerate(PIECES):
                if s == 1:
                    v.wait_ge(y_ready, 12)
                    extremes_of(h96, 6, y_sb[h96, :, a:b], 6)
                    continue
                for c in range(6):
                    v.wait_ge(y_ready, 6 * s + c + 1)
                    extremes_of(h96, 6 * s + c, y_sb[h96, c, a:b])

            def over_all(count, which):
                v.wait_ge(vec, marked())
                v.tensor_reduce(gin, stat[:, :, 0:count + 1], AX.X, ALU.max).then_inc(stat_ready, 1)
                v.wait_ge(all_max, which)

            def scales(q, mul=1.0):
                mark(v.tensor_scalar(q[3], gout[:, 1:2], -1.0, None, ALU.mult))
                then(v.tensor_scalar(q[0], gout[:, 0:1], gout[:, 1:2], mul, ALU.add, ALU.mult))
                then(v.tensor_scalar(q[0], q[0], INV_255, QEPS, ALU.mult, ALU.max))
                if isinstance(mul, float):
                    v.reciprocal(q[1], q[0]).then_inc(bound_in, 1)
                else:
                    then(v.reciprocal(q[1], q[0]))
                    v.tensor_scalar(q[1], q[1], mul, None, ALU.mult).then_inc(bound_in, 1)

            def upper(q, which):
                v.wait_ge(bound_done, which)
                then(v.tensor_scalar(q[2], q[2], 255.0, None, ALU.add))

            over_all(18, 1)
            scales(q_y)
            upper(q_y, 1)
            then(v.tensor_scalar(a_mul, q_y[0], q_y[0], HD ** -0.5, ALU.mult, ALU.mult))
            then(v.memset(stat[:, :, :], 0.0))
            v.wait_ge(qmask_zero, 1)
            for g in range(2):
                v.wait_ge(rounded, 2 * g + 1)
                for i in range(GI):
                    mark(v.tensor_scalar(
                        qmask[h96, g, 0:GI * (NG - 1), :].rearrange("p (G i) r -> p G i r", i=GI)[:, :, i, i * N:(i + 1) * N],
                        y_sb[h96, g, 0:R * (NG - 1)].rearrange("p (G r) -> p G r", r=R)[:, :, i * N:(i + 1) * N],
                        q_y[2][h96], MAGIC, ALU.min, ALU.subtract))
                v.tensor_scalar(qmask[h96, g, B - 1, 0:N], y_sb[h96, g, T - N:T], q_y[2][h96], MAGIC, ALU.min,
                                ALU.subtract).then_inc(qmask_ready, 1)
                v.wait_ge(rounded, 2 * g + 2)
                then(v.tensor_scalar(kv_t[h96, g, :], y_sb[h96, 2 + g, :], q_y[2][h96], MAGIC, ALU.min, ALU.subtract))
                spread(v, k_exp, kv_t[h96, g, :], g, range(HG), k_exp_ready, mark)
            v.wait_ge(rounded, 6)
            v.tensor_scalar(kv_t[h96, 2:4, :], y_sb[h96, 4:6, :], q_y[2][h96], MAGIC, ALU.min,
                            ALU.subtract).then_inc(v_ready, 1)
            v.wait_ge(v_ready, 1)
            spread(v, v_exp_t, kv_t[h96, 2, :], 0, range(HG), v_exp_t_ready, mark)

            rm = row_max[0:R].rearrange("p (b l) -> p b l", b=5)
            for i in range(5):
                v.wait_ge(s_psum, i + 1)
                n = mark(v.tensor_reduce(rm[:, i], ps[0:R, i, 0:4 * M].rearrange("p (l m) -> p l m", m=N), AX.X, ALU.max))
                mark(v.tensor_reduce(stat[0:R, 1, 1 + i:2 + i], ps[0:R, i, 0:4 * M], AX.X, ALU.min, negate=True))
            v.wait_ge(vec, n)
            mark(v.tensor_reduce(stat[0:R, 0, 1:2], row_max[0:R], AX.X, ALU.max))
            over_all(5, 2)
            scales(q_a, a_mul)
            c0 = np.float32(0.35815147)
            then(v.reciprocal(x0_pos, q_a[0]))
            mark(v.tensor_scalar(pol[:, 0:1], x0_pos, float(np.float32(-0.6931)), None, ALU.mult))
            mark(v.tensor_scalar(pol[:, 1:2], x0_pos, float(np.float32(0.96963238) / c0), None, ALU.mult))
            then(v.tensor_scalar(pol[:, 2:3], x0_pos, x0_pos, float(np.float32(1.0) / c0), ALU.mult, ALU.mult))
            then(v.tensor_scalar(pol_t, pol, 16777216.0, None, ALU.min))
            then(v.tensor_copy(smalli[:, 24:27], pol_t))
            then(v.tensor_copy(pol_f, smalli[:, 24:27]))
            then(v.tensor_tensor(pol_g, pol_f, pol_t, ALU.is_gt))
            then(v.tensor_tensor(pol_f, pol_f, pol_g, ALU.subtract))
            mark(v.tensor_scalar(pol_g, pol, 8388608.0, None, ALU.is_ge))
            then(v.tensor_tensor(pol_t, pol, pol_f, ALU.subtract))
            then(v.tensor_tensor(pol_t, pol_t, pol_g, ALU.mult))
            then(v.tensor_tensor(pol, pol_f, pol_t, ALU.add))
            mark(v.tensor_scalar(x0_30, pol[:, 0:1], 30.0, None, ALU.mult))
            mark(v.tensor_scalar(x0_pos, pol[:, 0:1], -1.0, None, ALU.mult))
            then(v.reciprocal(x0_inv, pol[:, 0:1]))
            then(v.tensor_scalar(q_bias, x0_inv, -0.5, -0.5, ALU.mult, ALU.add))
            upper(q_a, 2)
            v.wait_ge(attn_scaled, 1)
            then(v.tensor_scalar(row_max[0:R], row_max[0:R], q_a[2][0:R], None, ALU.min))
            LH = L // 2
            V_, XI, _, W_ = soft
            VI, _, QQ, WI = soft_i
            _, E_, Y0, _ = soft

            def half(ap, i):
                return ap[0:R, i * LH:(i + 1) * LH, :]

            def bc(ap, i):
                return ap[0:R, i * LH:(i + 1) * LH].unsqueeze(2).to_broadcast([R, LH, N])

            for i in range(2):
                v.wait_ge(attn_scaled, i + 2)
                then(v.scalar_tensor_tensor(out=half(V_, i), in0=half(V_, i), scalar=q_a[2][0:R], in1=bc(row_max, i),
                                            op0=ALU.min, op1=ALU.subtract))
                v.tensor_scalar(half(XI, i), half(V_, i), x0_30[0:R], None, ALU.max).then_inc(xi_ready, 1)
            for i in range(2):
                v.wait_ge(q_ready, i + 1)
                then(v.scalar_tensor_tensor(out=half(XI, i), in0=half(QQ, i), scalar=x0_pos[0:R], in1=half(XI, i),
                                            op0=ALU.mult, op1=ALU.add))
                if i == 0:
                    v.wait_ge(v_psum, 40 // VB)
                then(v.scalar_tensor_tensor(out=half(W_, i), in0=half(XI, i), scalar=pol[0:R, 1:2], in1=half(XI, i),
                                            op0=ALU.add, op1=ALU.mult))
                v.wait_ge(power_ready, i + 1)
                v.scalar_tensor_tensor(out=half(E_, i), in0=half(W_, i), scalar=pol[0:R, 2:3], in1=half(V_, i),
                                       op0=ALU.add, op1=ALU.mult).then_inc(e_ready, 1)
                v.wait_ge(e_ready, i + 1)
                n = mark(v.tensor_reduce(row_sum[0:R, i * LH:(i + 1) * LH], half(E_, i), AX.X, ALU.add))
            v.wait_ge(vec, n)
            then(v.tensor_scalar(row_sum[0:R], row_sum[0:R], -1.0, None, ALU.mult))
            for i in range(2):
                v.wait_ge(y0_ready, i + 1)
                then(v.tensor_tensor(half(W_, i), half(E_, i), half(Y0, i), ALU.mult))
                then(v.scalar_tensor_tensor(out=half(W_, i), in0=half(W_, i), scalar=2.0, in1=half(Y0, i),
                                            op0=ALU.subtract, op1=ALU.mult))
                then(v.tensor_tensor(half(W_, i), half(W_, i), bc(row_sum, i), ALU.mult))
                then(v.tensor_scalar(half(W_, i), half(W_, i), 1048576.0, MAGIC, ALU.min, ALU.add))
                then(v.tensor_scalar(half(W_, i), half(W_, i), MAGIC, FOUR_THIRDS, ALU.subtract, ALU.mult))
                then(v.tensor_scalar(half(WI, i), half(WI, i), EXP_MASK, EXP_MASK, ALU.bitwise_and, ALU.bitwise_xor))
                v.scalar_tensor_tensor(out=probs[0:R, i * NG:(i + 1) * NG].rearrange("p a (h m) -> p (a h) m", m=N),
                                       in0=half(W_, i), scalar=2.0 ** -14, in1=half(W_, i),
                                       op0=ALU.is_ge, op1=ALU.mult).then_inc(p_ready, 1)
            mark(v.tensor_scalar(a_mul, q_y[0], 0.5, None, ALU.mult))
            then(v.memset(stat[:, :, :], 0.0))

            def attended(g, t):
                v.wait_ge(av_psum, 2 * t + g + 1)
                i = 4 * t + 2 * g
                extremes_of(h96, i, ps[h96, i:i + 2, 0:AVI * N], 2)

            attended(0, 0)
            v.wait_ge(pt_psum, 4)
            probs_out(v.tensor_copy, 3).then_inc(pt_ready_v, 1)
            attended(1, 0)
            attended(0, 1)
            attended(1, 1)
            over_all(8, 3)
            scales(q_o, a_mul)
            upper(q_o, 3)
            mark(v.tensor_scalar(rows[:, 2, :], rows[:, 2, :], q_o[0], None, ALU.mult))
            for t in range(2):
                for g in range(2):
                    v.wait_ge(rounded, 7 + 2 * t + g)
                    v.tensor_scalar(
                        o_q[h96, g, 512 * t:512 * t + 512].rearrange("p (w b h) -> p w b h", w=SIDE, b=B // 2),
                        o_v[h96, g, t * T // 2:(t + 1) * T // 2].rearrange("p (b n) -> p b n", n=N)[:, :, 1:N].rearrange(
                            "p b (h w) -> p w b h", w=SIDE), q_o[2][h96], MAGIC, ALU.min, ALU.subtract).then_inc(oq_ready, 1)
            v.tensor_scalar(o_q[h96, :, 1024:T], o_v[h96].rearrange("p g (b n) -> p g b n", n=N)[:, :, :, 0],
                            q_o[2][h96], MAGIC, ALU.min, ALU.subtract).then_inc(oq_ready, 1)
            mark(v.memset(stat[:, :, :], 0.0))

            v.wait_ge(vec, marked())

            def proj_tiles(i):
                return (128 if i < 4 else B), slice(2 * i, 2 * i + (2 if i < 4 else 1))

            def projected(i):
                p, t = proj_tiles(i)
                m = t.stop - t.start
                v.wait_ge(proj_psum, i + 1)
                return mark(v.tensor_tensor(proj[0:p, t, :], ps[0:p, i, 0:m * C].rearrange("p (a c) -> p a c", c=C),
                                            rows[0:p, 2:3, :].to_broadcast([p, m, C]), ALU.mult))

            def biased(i, n):
                p, t = proj_tiles(i)
                v.wait_ge(vec, n)
                m = t.stop - t.start
                return mark(v.tensor_tensor(proj[0:p, t, :], proj[0:p, t, :], rows[0:p, 1:2, :].to_broadcast([p, m, C]), ALU.add))

            def projection_extremes(i, n):
                p, t = proj_tiles(i)
                v.wait_ge(vec, n)
                extremes_of(slice(0, p), i, proj[0:p, t, :].rearrange("p a c -> p (a c)"))

            n = projected(0)
            for i in range(5):
                m = projected(i + 1) if i < 4 else None
                b = biased(i, n)
                if i > 0:
                    projection_extremes(i - 1, before)
                n, before = m, b
            projection_extremes(4, before)
            over_all(5, 4)
            scales(q_p)
            upper(q_p, 4)
            v.wait_ge(rounded, 12)
            then(v.tensor_scalar(proj_v[:, 0:NT - 1], proj_v[:, 0:NT - 1], q_p[2], MAGIC, ALU.min, ALU.subtract))
            then(v.tensor_scalar(proj_v[0:B, NT - 1], proj_v[0:B, NT - 1], q_p[2][0:B], MAGIC, ALU.min, ALU.subtract))
            mark(v.scalar_tensor_tensor(out=pay[:, 0:NT - 1, 0:C], in0=proj_v[:, 0:NT - 1, :], scalar=q_p[0],
                                        in1=pay[:, 0:NT - 1, 0:C], op0=ALU.mult, op1=ALU.add))
            then(v.scalar_tensor_tensor(out=pay[0:B, NT - 1, 0:C], in0=proj_v[0:B, NT - 1, :], scalar=q_p[0][0:B],
                                        in1=pay[0:B, NT - 1, 0:C], op0=ALU.mult, op1=ALU.add))
            for j in range(NT):
                n = mark(v.bn_stats(bn[:, j, :], pay[:, j, 0:C]))
            v.wait_ge(vec, n)
            for j in range(NT):
                n = mark(v.bn_aggr(pay[:, j, COL_MEAN:COL_MEAN + 2], bn[:, j, :]))
            v.wait_ge(vec, n)
            v.tensor_scalar(rstd[:, :], pay[:, :, COL_RSTD], LN_EPS, None, ALU.add).then_inc(var_ready, 1)
            v.wait_ge(rstd_ready, 3)
            for j in range(NT):
                v.tensor_scalar(xn2[:, j, :], pay[:, j, 0:C], pay[:, j, COL_MEAN:COL_MEAN + 1],
                                pay[:, j, COL_RSTD:COL_RSTD + 1], ALU.subtract, ALU.mult).then_inc(xn2_ready, 1)
            for i in range(0, 5, 2):
                v.wait_ge(xn2_psum, i + 1)
                xn2_out(v.tensor_copy, i).then_inc(xn2t_v, 1)

            def all_tiles(f):
                mark(f(slice(0, 128), slice(0, NT - 1)))
                return f(slice(0, B), slice(NT - 1, NT))

            v.wait_ge(lg_psum, 1)
            lgp = ps[:, 7, 0:NT * E].rearrange("p (j e) -> p j e", e=E)
            then(v.memset(lg[:, NT - 1, :], 0.0))
            then(all_tiles(lambda p, t: v.tensor_tensor(
                lg[p, t, :], lgp[p, t, :], bs_row[p].unsqueeze(1).to_broadcast([p.stop, t.stop - t.start, E]), ALU.add)))
            then(v.tensor_reduce(n9[0][:, :], lg[:, :, :], AX.X, ALU.max))

            def per_tile(ap):
                return ap.unsqueeze(2).to_broadcast([128, NT, E])

            v.tensor_tensor(ex[:, :, :], lg[:, :, :], per_tile(n9[0][:, :]), ALU.subtract).then_inc(lg_max, 1)
            then(v.tensor_tensor(hot[:, :, :], lg[:, :, :], per_tile(n9[0][:, :]), ALU.is_lt))
            then(v.scalar_tensor_tensor(out=hot[:, :, :], in0=hot[:, :, :], scalar=float(E), in1=e_idx[:, :, :],
                                        op0=ALU.mult, op1=ALU.add))
            then(v.tensor_reduce(n9[1][:, :], hot[:, :, :], AX.X, ALU.min))
            then(v.tensor_tensor(hot[:, :, :], e_idx[:, :, :], per_tile(n9[1][:, :]), ALU.is_equal))
            then(v.memset(hot[64:128, NT - 1, :], 0.0))
            v.tensor_copy(hot_b[:, :, :], hot[:, :, :]).then_inc(hot_ready, 1)
            v.wait_ge(ex_ready, 1)
            then(v.tensor_reduce(n9[2][:, :], ex[:, :, :], AX.X, ALU.add))
            then(v.reciprocal(pay[:, :, COL_P], n9[2][:, :]))
            v.wait_ge(rank_psum, 1)
            tiles, ends, tmp, starts = e8
            then(v.tensor_scalar(tiles[:, :], ps[:, 1, 0:E], 1.0 / 128, 127.0 / 128 - 0.5 + 1.0 / 256, ALU.mult, ALU.add))
            then(v.tensor_scalar(tiles[:, :], tiles[:, :], MAGIC, MAGIC, ALU.add, ALU.subtract))
            src = tiles
            for i, sh in enumerate((1, 2, 4)):
                dst = (ends, tmp, ends)[i]
                mark(v.tensor_copy(dst[:, 0:sh], src[:, 0:sh]))
                then(v.tensor_tensor(dst[:, sh:E], src[:, sh:E], src[:, 0:E - sh], ALU.add))
                src = dst
            then(v.tensor_tensor(starts[:, :], ends[:, :], tiles[:, :], ALU.subtract))
            then(v.tensor_tensor(te[:, :, :], ends[:, :].unsqueeze(1).to_broadcast([128, SLOT_TILES, E]),
                                 te_idx[:, :].unsqueeze(2).to_broadcast([128, SLOT_TILES, E]), ALU.is_le))
            then(v.tensor_reduce(te_idx[:, :], te[:, :, :], AX.X, ALU.add))
            v.tensor_scalar(tile_expert[:, :], te_idx[:, :], float(E - 1), None, ALU.min).then_inc(table_ready, 1)
            then(v.scalar_tensor_tensor(out=rk[:, :, :], in0=starts[:, :].unsqueeze(1).to_broadcast([128, NT, E]),
                                        scalar=128.0, in1=ps[:, 0, 0:NT * E].rearrange("p (j e) -> p j e", e=E),
                                        op0=ALU.mult, op1=ALU.add))
            then(v.tensor_tensor(rk[:, :, :], rk[:, :, :], hot[:, :, :], ALU.mult))
            then(v.tensor_reduce(n9[1][:, :], rk[:, :, :], AX.X, ALU.add))
            v.tensor_copy(dest[:, :], n9[1][:, :]).then_inc(dest_ready, 1)

            for k in range(2):
                mark(v.memset(xg_t[k][HALF:HALF + 1, 0, :], 1.0))

            def normalise(t, k):
                if not isinstance(t, int) or t >= 2:
                    v.wait_ge(xgt_psum, t - 1)
                v.tensor_scalar(xg_n[k], xg[:, bass.ds(t, 1), 0:C], xg[:, bass.ds(t, 1), COL_MEAN:COL_MEAN + 1],
                                xg[:, bass.ds(t, 1), COL_RSTD:COL_RSTD + 1], ALU.subtract, ALU.mult).then_inc(xg_ready, 1)

            def expert_weights(t, k):
                if not isinstance(t, int) or t >= 2:
                    v.wait_ge(g1_psum, t - 1)
                e = v.value_load(tile_expert[0:1, bass.ds(t, 1)], min_val=0, max_val=E - 1)
                v.tensor_copy(w1_tile[k][0:HALF + 1, 0, :], w1_sb[0:HALF + 1, bass.ds(e, 1), 0, :]).then_inc(w1_tile_ready, 1)
                v.tensor_copy(w1_tile[k][0:HALF, 1, :], w1_sb[0:HALF, bass.ds(e, 1), 1, :]).then_inc(w1_tile_ready, 1)

            def finish(t, k):
                e = v.value_load(tile_expert[0:1, bass.ds(t, 1)], min_val=0, max_val=E - 1)
                v.wait_ge(g2_psum, t + 1)
                v.tensor_tensor(y_b[k], ps[:, 4 + k, 0:C], b2_rows[:, bass.ds(e, 1), :], ALU.add).then_inc(y_b_done, 1)
                if not isinstance(t, int) or t >= 2:
                    v.wait_ge((stored, stored1)[k], 8 * (t - k))
                v.wait_ge(y_b_done, t + 1)
                v.scalar_tensor_tensor(out=y_out[k], in0=y_b[k], scalar=xg[:, bass.ds(t, 1), COL_P:COL_P + 1],
                                       in1=xg[:, bass.ds(t, 1), 0:C], op0=ALU.mult, op1=ALU.add).then_inc(y_done, 1)

            v.wait_ge(table_ready, 1)
            v.wait_ge(w1_in, 48)
            expert_weights(0, 0)
            expert_weights(1, 1)
            v.wait_ge(slots_in0, 16)
            normalise(0, 0)
            normalise(1, 1)
            v.wait_ge(slots_in1, 16)
            v.wait_ge(b2_in, 16)
            normalise(2, 0)
            normalise(3, 1)

            def step(t, k, more=2):
                if more >= 1:
                    expert_weights(t + 2, k)
                finish(t, k)
                if more >= 2:
                    normalise(t + 4, k)

            step(0, 0)
            step(1, 1)
            with v.Fori(1, SLOT_TILES // 2 - 2) as pair:
                step(2 * pair, 0)
                step(2 * pair + 1, 1)
            step(SLOT_TILES - 4, 0, 1)
            step(SLOT_TILES - 3, 1, 1)
            step(SLOT_TILES - 2, 0, 0)
            step(SLOT_TILES - 1, 1, 0)

        @block.scalar
        def _(act):
            mark, _ = tally(act_s)
            h96 = slice(0, HALF)
            act.dma_start(tokw_sb[h96], tok_w.rearrange("(c p) d -> p c d", p=HALF)).then_inc(tokw_in, 16)
            act.dma_start(w_row[h96, 0:6, :], w_qkv.rearrange("(c p) d -> p c d", p=HALF)).then_inc(w_in, 16)
            act.dma_start(w_row[h96, 6:8, :], w_proj.rearrange("(c p) d -> p c d", p=HALF)).then_inc(w_in, 16)
            act.dma_start(b_row[0:6, :], b_qkv.rearrange("(c p) -> c p", p=HALF)).then_inc(bq_in, 16)
            act.dma_start(rows[:, 0, :], tok_b.partition_broadcast(128)).then_inc(small_in, 16)
            act.dma_start(rows[:, 1, :], b_proj.partition_broadcast(128)).then_inc(small_in, 16)
            act.dma_start(bs_row[:, :], bs.partition_broadcast(128)).then_inc(small_in, 16)
            act.dma_start(ws_sb[:, :, :], ws.rearrange("(k p) e -> p k e", p=HALF)).then_inc(small_in, 16)
            act.dma_start(pay[0:B, NT - 1, 0:C], cls_tok.rearrange("a b c -> (a b c)").partition_broadcast(B)).then_inc(small_in, 16)

            def pack(j):
                act.wait_ge(x_in[j // SIDE], 16)
                act.copy(x_c[:, j, :].rearrange("p (r s) -> p r s", s=SEG),
                         x_sb[:, j // SIDE, :, j % SIDE, :]).then_inc(packed_a, 1)

            def patches_out(j):
                act.wait_ge(xt_psum, j + 1)
                if j >= 2:
                    act.wait_ge(embed_psum, j - 1)
                act.copy(x_t[j % 2][h96, 4:8, :], ps[h96, 2 * (j % 2) + 1, :]).then_inc(xt_ready_a, 1)

            pack(1)
            patches_out(0)
            pack(3)
            patches_out(1)
            pack(5)
            patches_out(2)
            pack(7)
            for j in range(3, 7):
                patches_out(j)

            def token_view(q, i):
                tiles, half = XG[i]
                if half is None:
                    return x_part[h96, q].rearrange("p k (b n) -> p k b n", n=N)[:, :, :, 0]
                t = tiles[0] // SIDE
                return x_part[h96, q, half, t * T // 2:(t + 1) * T // 2].rearrange(
                    "p (b n) -> p b n", n=N)[:, :, 1:N].rearrange("p b (h w) -> p w b h", w=SIDE)

            def grouped(ap, i):
                if XG[i][1] is None:
                    return ap[h96, 0:2 * B].rearrange("p (w b) -> p w b", w=2)
                return ap[h96, 0:512].rearrange("p (w b h) -> p w b h", w=SIDE, b=B // 2)

            def highest(i):
                act.wait_ge(xnt_psum, i + 1)
                act.copy(token_view(0, i), grouped(ps[:, 6 + i % 2, :], i)).then_inc(hi_done, 1)

            def middle(i):
                act.wait_ge(res_done, i + 1)
                act.copy(token_view(1, i), grouped(residue[i % 2], i)).then_inc(mid_done, 1)

            def y_out_of(s, c):
                a, b = PIECES[s]
                bank, col = y_bank(c, s)
                act.wait_ge(y_psum, 6 * s + c + 1 if s != 1 else 12)
                act.activation(y_sb[h96, c, a:b], ps[h96, bank, col:col + b - a], ACT.Identity,
                               bias=bq_col[h96, c:c + 1], scale=w_scale[h96, c:c + 1]).then_inc(y_ready, 1)

            highest(0)
            highest(1)
            patches_out(7)
            middle(0)
            middle(1)
            highest(2)
            middle(2)
            act.wait_ge(bq_ready, 1)
            act.wait_ge(embed_psum, 8)
            for c in range(3):
                y_out_of(0, c)
            highest(3)
            highest(4)
            middle(3)
            middle(4)
            for c in range(3, 6):
                y_out_of(0, c)
            for s in (1, 2):
                for c in range(6):
                    y_out_of(s, c)

            def bound(q, which):
                act.wait_ge(bound_in, which)
                act.activation(q[2], q[3], ACT.Identity, bias=magic_c, scale=q[1]).then_inc(bound_done, 1)

            bound(q_y, 1)
            act.wait_ge(y_ready, 18)
            for c in (0, 2, 1, 3, 4, 5):
                act.activation(y_sb[h96, c, :], y_sb[h96, c, :], ACT.Identity, bias=magic_c[h96],
                               scale=q_y[1][h96]).then_inc(rounded, 1)

            act.wait_ge(v_ready, 1)
            vb = kv_t[h96, 3, :].rearrange("p (b n) -> p b n", n=N)
            for h in range(HG):
                ins = act.activation(v_exp_t[h96, 1, :, h, :], vb, ACT.Copy, scale=head_mask[h96, h:h + 1])
                if h < HG - 1:
                    mark(ins)
                else:
                    ins.then_inc(v_exp_t_ready, 1)

            def v_out(n):
                g, b0 = n // 7, (n % 7) * VB
                m = min(VB, B - b0)
                act.wait_ge(v_psum, n + 1)
                act.copy(v_exp[0:M, g, b0:b0 + m, :],
                         bank_b(5 + n % 3)[0:M, 0:m * HALF].rearrange("p (b c) -> p b c", c=HALF)).then_inc(v_exp_ready, 1)

            LH = L // 2
            V_, XI, _, _ = soft
            VI, _, QQ, _ = soft_i
            _, E_, Y0, _ = soft
            sv = ps[0:R, 0:5, 0:4 * M].rearrange("p b (l m) -> p b l m", m=N)
            v3 = V_[0:R].rearrange("p (b l) m -> p b l m", b=5)
            for n in range(3):
                v_out(n)
            bound(q_a, 2)
            act.activation(row_max[0:R], row_max[0:R], ACT.Identity, bias=magic_c[0:R],
                           scale=q_a[1][0:R]).then_inc(attn_scaled, 1)
            act.activation(v3[:, 0:2], sv[:, 0:2], ACT.Identity, bias=magic_c[0:R], scale=q_a[1][0:R])
            act.activation(v3[:, 2], sv[:, 2], ACT.Identity, bias=magic_c[0:R],
                           scale=q_a[1][0:R]).then_inc(attn_scaled, 1)
            act.activation(v3[:, 3:5], sv[:, 3:5], ACT.Identity, bias=magic_c[0:R],
                           scale=q_a[1][0:R]).then_inc(attn_scaled, 1)
            v_out(3)
            for i in range(2):
                act.wait_ge(xi_ready, i + 1)
                act.activation(QQ[0:R, i * LH:(i + 1) * LH], XI[0:R, i * LH:(i + 1) * LH], ACT.Identity,
                               bias=q_bias[0:R], scale=x0_inv[0:R]).then_inc(q_ready, 1)
                act.wait_ge(q_ready, i + 1)
                act.activation(VI[0:R, i * LH:(i + 1) * LH], QQ[0:R, i * LH:(i + 1) * LH], ACT.Identity,
                               bias=exp_c[0:R], scale=-8388608.0).then_inc(power_ready, 1)
                v_out(4 + i)
            for i in range(2):
                for n in range(6 + 4 * i, 10 + 4 * i):
                    v_out(n)
                act.wait_ge(e_ready, i + 1)
                act.wait_ge(act_s, mark(act.activation(Y0[0:R, i * LH:(i + 1) * LH], E_[0:R, i * LH:(i + 1) * LH], ACT.Ln)))
                act.activation(Y0[0:R, i * LH:(i + 1) * LH], Y0[0:R, i * LH:(i + 1) * LH], ACT.Exp,
                               scale=-1.0).then_inc(y0_ready, 1)
            act.wait_ge(pt_psum, 1)
            probs_out(act.copy, 0).then_inc(pt_ready_a, 1)
            act.wait_ge(pt_psum, 2)
            probs_out(act.copy, 1).then_inc(pt_ready_a, 1)
            act.wait_ge(pt_psum, 3)
            probs_out(act.copy, 2).then_inc(pt_ready_a, 1)
            bound(q_o, 3)
            act.wait_ge(av_psum, 4)
            for t in range(2):
                for g in range(2):
                    i = 4 * t + 2 * g
                    act.activation(o_v[h96, g, t * T // 2:(t + 1) * T // 2].rearrange("p (s t) -> p s t", s=2),
                                   ps[h96, i:i + 2, 0:AVI * N], ACT.Identity, bias=magic_c[h96],
                                   scale=q_o[1][h96]).then_inc(rounded, 1)

            bound(q_p, 4)
            act.activation(proj_v[:, 0:NT - 1], proj[:, 0:NT - 1], ACT.Identity, bias=magic_c,
                           scale=q_p[1]).then_inc(rounded, 1)
            act.activation(proj_v[0:B, NT - 1], proj[0:B, NT - 1], ACT.Identity, bias=magic_c[0:B],
                           scale=q_p[1][0:B]).then_inc(rounded, 1)

            for i in range(1, 5, 2):
                act.wait_ge(xn2_psum, i + 1)
                xn2_out(act.copy, i).then_inc(xn2t_a, 1)
            act.wait_ge(lg_max, 1)
            act.activation(ex[:, :, :], ex[:, :, :], ACT.Exp).then_inc(ex_ready, 1)

            def tokens_out(t, k):
                act.wait_ge(xgt_psum, t + 1)
                if not isinstance(t, int) or t >= 2:
                    act.wait_ge(g1_psum, t - 1)
                act.copy(xg_t[k][h96].rearrange("p c t -> p (c t)"), ps[h96, 7, 0:256]).then_inc(xgt_ready, 1)

            def gelu(t, k):
                act.wait_ge(g1_psum, t + 1)
                if not isinstance(t, int) or t >= 2:
                    act.wait_ge(g2_psum, t - 1)
                act.activation(h_t[k].rearrange("p (a f) t -> p a (f t)", a=2), ps[:, 2 * k:2 * k + 2, 0:FH],
                               ACT.Gelu).then_inc(h_ready, 1)

            tokens_out(0, 0)
            tokens_out(1, 1)
            gelu(0, 0)
            tokens_out(2, 0)
            gelu(1, 1)
            tokens_out(3, 1)
            with act.Fori(2, SLOT_TILES - 2, 2) as t:
                gelu(t, 0)
                tokens_out(t + 2, 0)
                gelu(t + 1, 1)
                tokens_out(t + 3, 1)
            gelu(SLOT_TILES - 2, 0)
            gelu(SLOT_TILES - 1, 1)


_INS = ['x', 'cls_tok', 'L0_tok_W', 'L0_tok_b', 'L0_attn_w_qkv', 'L0_attn_b_qkv', 'L0_attn_w_proj', 'L0_attn_b_proj',
        'L0_ffn_Ws', 'L0_ffn_bs', 'L0_ffn_W1', 'L0_ffn_b1', 'L0_ffn_W2', 'L0_ffn_b2']
_OUTS = [((64, 17, 192), 'float32')]


def kernel(**inputs):
    import numpy as _np
    import concourse.bacc as _bacc
    from concourse import mybir as _mybir
    from concourse.bass_utils import run_bass_kernel_spmd as _run

    nc = _bacc.Bacc("TRN2", target_bir_lowering=False, num_devices=1)
    arrays, args = {}, []
    for name in _INS:
        a = _np.ascontiguousarray(inputs[name])
        arrays[f"in_{name}_dram"] = a
        args.append(nc.dram_tensor(f"in_{name}_dram", a.shape, _mybir.dt.from_np(a.dtype), kind="ExternalInput").ap())
    for i, (shape, dtype) in enumerate(_OUTS):
        dt = _mybir.dt.from_np(_np.dtype(dtype))
        args.append(nc.dram_tensor(f"out_{i}_dram", shape, dt, kind="ExternalOutput").ap())
    vit_tower(nc, *args)
    r = _run(nc, [arrays], core_ids=[0])
    return r.results[0]["out_0_dram"]
```

```python
from contextlib import ExitStack

import numpy as np

import concourse.bass as bass
from concourse import mybir

ALU = mybir.AluOpType
ACT = mybir.ActivationFunctionType
AX = mybir.AxisListType
F32 = mybir.dt.float32
BF16 = mybir.dt.bfloat16
I32 = mybir.dt.int32
U32 = mybir.dt.uint32
RMAX = bass.bass_isa.ReduceOp.max

MAGIC = 12582912.0
QEPS = 1.1920928955078125e-07
LN_EPS = 1e-5
INV_255 = float(np.float32(1.0) / np.float32(255.0))
FOUR_THIRDS = float(np.float32(4.0) / np.float32(3.0))
EXP_MASK = 0x7F800000


def tally(sem):
    count = [0]

    def mark(instruction):
        instruction.then_inc(sem, 1)
        count[0] += 1
        return count[0]

    return mark, lambda: count[0]


def vit_tower(nc, x, cls_tok, tok_w, tok_b, w_qkv, b_qkv, w_proj, b_proj, ws, bs, w1, b1, w2, b2, out):
    B, IMG, _, CH = x.shape
    PATCH = 16
    SIDE = IMG // PATCH
    SEG = PATCH * CH
    C = tok_w.shape[1]
    HALF = C // 2
    HEADS, HD = 12, 16
    HG = HEADS // 2
    N = SIDE * SIDE + 1
    T = B * N
    NT = 9
    KC = PATCH * SEG // 128
    E = ws.shape[1]
    F = w1.shape[2]
    FC = F // 128
    FH = F // 2
    GI = 7
    R = GI * N
    NG = -(-B // GI)
    M = HG * N
    L = NG * 2 * HG
    SLOT_TILES = (T + E * 127) // 128
    SLOTS = SLOT_TILES * 128
    BY_PE = 2
    COL_P, COL_ROW, COL_MEAN, COL_RSTD = C, C + 1, C + 2, C + 3
    PAYW = C + 4
    NO_ROW = 4 * T

    with ExitStack() as ctx:
        def sb(name, shape, dt=F32):
            return ctx.enter_context(nc.sbuf_tensor(name, shape, dt))

        def sem(name):
            return ctx.enter_context(nc.semaphore(name))

        slots = nc.dram_tensor("slots", (SLOTS, PAYW), F32, kind="Internal").ap()

        w1_sb = sb("w1_sb", [128, E, 2, F])
        w2_sb = sb("w2_sb", [128, E, FC, C])
        pay = sb("pay", [128, NT, PAYW])
        w_t = sb("w_t", [HALF, 2, 4 * C], BF16)
        ident = sb("ident", [128, 128])
        identb = sb("identb", [128, 128], BF16)
        small = sb("small", [128, 216])
        smalli = sb("smalli", [128, 40], I32)

        RA, RB, RC, RD = 6 * T, 7936, 6 * T, B * HALF
        area_a = sb("area_a", [128, RA + RB])
        area_c = sb("area_c", [128, RC])
        area_d = sb("area_d", [128, RD])

        def part(area, start, shape, dt=F32):
            n = int(np.prod(shape))
            words = n if dt != BF16 else -(-n // 2)
            v = area[:, start:start + words]
            if dt != F32:
                v = v.bitcast(dt)[:, 0:n]
            if len(shape) > 1:
                names = " ".join(f"d{i}" for i in range(len(shape)))
                v = v.rearrange(f"p ({names}) -> p {names}", **{f"d{i}": s for i, s in enumerate(shape) if i})
            return v

        x_sb = part(area_a, 0, [2, PATCH, SIDE, SEG])
        x_c = part(area_c, 0, [8, PATCH * SEG])
        x_t = [part(area_a, RA + 1024 * i, [KC, 128]) for i in range(2)]
        y_sb = part(area_a, 0, [6, T])
        xn = part(area_d, 0, [NT, C])
        residue = [part(area_d, NT * C + 512 * i, [512]) for i in range(2)]
        qmask = part(area_a, RA, [2, B, R], BF16)
        w_row = part(area_d, 0, [8, C])
        w_v = part(area_d, 8 * C, [8, C])
        w_int = part(area_d, 16 * C, [8, C], BF16)
        tokw_sb = part(area_d, 20 * C, [KC, C])
        b_row = part(area_d, 28 * C, [HALF])
        x_part = part(area_c, 0, [3, 2, T], BF16)
        kv_t = part(area_d, 0, [4, T], BF16)
        k_exp = part(area_c, 0, [2, B, HG, N], BF16)
        v_exp_t = part(area_a, 0, [2, B, HG, N], BF16)
        v_exp = part(area_d, 0, [2, B, HALF], BF16)
        SW = L * N
        assert SW * 3 <= RC and SW <= B * M // 2 * 40 // 64
        soft, soft_i = ([part(area_c if i < 3 else area_a, SW * (i % 3), [L, N], dt) for i in range(4)]
                        for dt in (F32, I32))
        probs = part(area_a, RA, [NG * 2, M], BF16)
        probs_t = part(area_a, RA + SW // 2, [NG * 2, R], BF16)
        o_q = part(area_c, 0, [2, T], BF16)
        o_v = part(area_a, 0, [2, T])
        proj_t = part(area_a, 2 * T, [2, T])
        qi_t = part(area_c, T, [2, NT * 128], BF16)
        h0_t = part(area_c, RC // 2, [NT, 2, 128])
        xg = part(area_a, 0, [SLOT_TILES, PAYW])
        o = SLOT_TILES * PAYW
        xg_n = [part(area_a, o + C * i, [C]) for i in range(2)]
        o += 2 * C
        xg_t = [part(area_a, o + 256 * i, [2, 128]) for i in range(2)]
        o += 512
        w1_tile = [part(area_a, o + 2 * F * i, [2, F]) for i in range(2)]
        o += 4 * F
        h_t = [part(area_a, o + F * i, [FC, 128]) for i in range(2)]
        o += 2 * F
        y_b = [part(area_a, o + C * i, [C]) for i in range(2)]
        o += 2 * C
        y_out = [part(area_a, o + C * i, [C]) for i in range(2)]
        o += 2 * C
        slot_row = part(area_a, o, [SLOT_TILES], U32)
        o += SLOT_TILES
        slot_idx = part(area_a, o, [128])
        o += 128
        to_slot = [part(area_a, o + NT * 128 * i, [NT, 128]) for i in range(BY_PE)]
        o += BY_PE * NT * 128
        assert o <= RA + RB
        b2_rows = part(area_c, 2304, [E, C])
        fill = part(area_c, 2304 + E * C, [PAYW])
        head_mask = small[:, 0:6]
        o = 6

        def cols(n):
            nonlocal o
            v = small[:, o:o + n]
            o += n
            return v

        w_max, w_min, w_scale, w_inv, w_him = (cols(8) for _ in range(5))
        bq_col = cols(8)
        colsum = cols(E)
        proj_scale = cols(2)
        magic_c = cols(1)
        exp_c = cols(1)
        stat = cols(2 * 19).rearrange("p (s c) -> p s c", s=2)
        gin = cols(2)
        gout = cols(2)
        q_y, q_a, q_o, q_p = ([cols(1) for _ in range(4)] for _ in range(4))
        a_mul = cols(1)
        pol = cols(3)
        pol_t, pol_f, pol_g = cols(3), cols(3), cols(3)
        x0_30, x0_inv, q_bias, x0_pos = cols(1), cols(1), cols(1), cols(1)
        assert o <= 216
        tokb_row = sb("tokb_row", [128, C])
        ones_f = sb("ones_f", [HALF, 128])
        ws_part = sb("ws_part", [HALF, 2, E, 3], BF16)
        ws_rest = sb("ws_rest", [HALF, 2, E])
        lg0 = sb("lg0", [128, NT, E])
        bs_row = sb("bs_row", [128, E])
        ws_sb = sb("ws_sb", [HALF, 2, E])
        row_max = sb("row_max", [128, L])
        row_sum = sb("row_sum", [128, L])
        bn = sb("bn", [128, NT, 6])
        mv = sb("mv", [128, NT, 2])
        rstd = sb("rstd", [128, NT])
        pow_e = sb("pow_e", [128, NT])
        lg, ex, hot, rk = (part(area_a, 8000 + NT * E * i, [NT, E]) for i in range(4))
        hot_b = part(area_a, 8000 + NT * E * 4, [NT, E], BF16)
        te = part(area_a, 8000 + NT * E * 5, [SLOT_TILES, E])
        e_idx = sb("e_idx", [128, NT, E])
        before, before_sum = (sb(n, [128, E, E]) for n in ("before", "before_sum"))
        tri = sb("tri", [128, 128], BF16)
        ones_b = sb("ones_b", [128, 128], BF16)
        n9 = [sb(f"n9_{i}", [128, NT]) for i in range(3)]
        e8 = [sb(f"e8_{i}", [128, E]) for i in range(4)]
        dest = sb("dest", [128, NT], U32)
        te_idx = sb("te_idx", [128, SLOT_TILES])
        tile_expert = sb("tile_expert", [128, SLOT_TILES], I32)

        ps = ctx.enter_context(nc.psum_tensor("ps", [128, 8, 512], F32))

        def bank_b(b):
            return ps[:, b, :].bitcast(BF16)

        x_in = [sem(f"x_in{i}") for i in range(2)]
        w_in, tokw_in, tokb_in, small_in, w1_in, w2_in, b2_in = (sem(n) for n in ("w_in", "tokw_in", "tokb_in", "small_in", "w1_in", "w2_in", "b2_in"))
        consts = sem("consts")
        vec, act_s, pool_s = sem("vec"), sem("act_s"), sem("pool_s")
        w_inv_ready, w_rounded, w_int_ready, w_t_psum, w_t_ready, vectors_psum = (sem(n) for n in (
            "w_inv_ready", "w_rounded", "w_int_ready", "w_t_psum", "w_t_ready", "vectors_psum"))
        h0_psum, h0_ready, lg0_psum, lg0_ready = (sem(n) for n in ("h0_psum", "h0_ready", "lg0_psum", "lg0_ready"))
        packed_v, packed_a, bq_in, bq_ready = (sem(n) for n in ("packed_v", "packed_a", "bq_in", "bq_ready"))
        xt_psum, xt_ready_v, xt_ready_a, embed_psum, embed_done = (sem(n) for n in (
            "xt_psum", "xt_ready_v", "xt_ready_a", "embed_psum", "embed_done"))
        var_ready, rstd_ready, xn_ready, xnt_psum, hi_done, res_done, mid_done, lo_done = (sem(n) for n in (
            "var_ready", "rstd_ready", "xn_ready", "xnt_psum", "hi_done", "res_done", "mid_done", "lo_done"))
        y_psum, y_ready = sem("y_psum"), sem("y_ready")
        stat_ready, all_max = sem("stat_ready"), sem("all_max")
        bound_in, bound_done, y_rounded, o_rounded, proj_rounded = (sem(n) for n in (
            "bound_in", "bound_done", "y_rounded", "o_rounded", "proj_rounded"))
        qmask_zero, k_ready, k_exp_ready, k_exp_ready_a = (sem(n) for n in ("qmask_zero", "k_ready", "k_exp_ready", "k_exp_ready_a"))
        v_ready, s_psum, v_exp_t_ready, v_exp_t_ready_a, v_psum, v_exp_ready = (sem(n) for n in (
            "v_ready", "s_psum", "v_exp_t_ready", "v_exp_t_ready_a", "v_psum", "v_exp_ready"))
        attn_scaled, xi_ready, q_ready, e_ready, y0_ready, power_ready, p_ready, pt_psum, pt_ready_v, pt_ready_a, av_psum = (sem(n) for n in (
            "attn_scaled", "xi_ready", "q_ready", "e_ready", "y0_ready", "power_ready", "p_ready", "pt_psum", "pt_ready_v", "pt_ready_a", "av_psum"))
        oq_ready, proj_scale_ready, proj_psum, proj_ready, qi_ready, qi_psum, h2_ready = (sem(n) for n in (
            "oq_ready", "proj_scale_ready", "proj_psum", "proj_ready", "qi_ready", "qi_psum", "h2_ready"))
        lg_max, ex_ready, hot_ready, rank_psum, dest_ready, table_ready = (sem(n) for n in (
            "lg_max", "ex_ready", "hot_ready", "rank_psum", "dest_ready", "table_ready"))
        filled, scattered, slots_in0, slots_in1 = (sem(n) for n in ("filled", "scattered", "slots_in0", "slots_in1"))
        slot_idx_ready, to_slot_ready, xg0_psum, xg0_ready, rows_ready, xg_ready, xgt_psum, xgt_ready, w1_tile_ready, g1_psum, h_ready, g2_psum, y_b_done, y_done, stored, stored1 = (sem(n) for n in (
            "slot_idx_ready", "to_slot_ready", "xg0_psum", "xg0_ready", "rows_ready", "xg_ready", "xgt_psum", "xgt_ready", "w1_tile_ready", "g1_psum", "h_ready", "g2_psum", "y_b_done", "y_done", "stored", "stored1"))

        block = ctx.enter_context(nc.Block())

        XG = [(range(0, 4), 0), (range(0, 4), 1), (range(8, 9), None), (range(4, 8), 0), (range(4, 8), 1)]
        XG_BANK = (6, 7, 0, 7, 6)
        XG_A = 3
        PIECES = [(0, 512), (1024, T), (512, 1024)]

        def y_bank(c, s):
            a, b = PIECES[s]
            return (c, 0) if s != 1 else (6, c * (b - a))
        LN1_TILES = [0, 1, 2, 3, 8, 4, 5, 6, 7]
        LN1_COLS = [(0, 5), (5, 9)]
        LN2_TILES = [(0, 6), (6, 9)]
        VB = 10
        AVI = 16
        PT = [(range(0, 5), 5), (range(5, 10), 6), (range(10, 16), 7), (range(16, 20), 5)]
        P_PARTS = [(0, 5), (5, 8), (8, 10)]

        def av_bank(g, b):
            return b // (B // 2) * 4 + 2 * g + b % (B // 2) // AVI

        GH = 4
        CONSTS = 20
        P_FILL = 1
        W_TBANK = 6
        V_PACKS, A_PACKS = (0, 2), (1, 3, 4, 5, 6, 7)
        X_SPLIT = 4
        WARM_BANK = 7

        PROJ = [(0, 512, 0), (512, 1024, 2), (1024, T, 4)]
        QI = [(range(4, 8), 5), (range(0, 4), 6), (range(8, 9), 4)]
        LG0_BANK = 5
        H0_BANK = (7, 6, 7, 6, 7)

        def probs_out(copy, n):
            blocks, bank = PT[n]
            return copy(probs_t[0:M, blocks[0]:blocks[-1] + 1, :],
                        bank_b(bank)[0:M, 0:len(blocks) * 128].rearrange("p (a r) -> p a r", r=128)[:, :, 0:R])

        K_HEADS, V_HEADS = 4, (3, 4)

        def spread(scaled, blocks, rows_t, row, g, b0, b1, heads, done, mark):
            for h in heads:
                ins = scaled(blocks[0:HALF, g, b0:b1, h, :],
                                           rows_t[0:HALF, row, b0 * N:b1 * N].rearrange("p (b n) -> p b n", n=N),
                                           head_mask[0:HALF, h:h + 1], None, ALU.mult)
                if h == heads[-1]:
                    ins.then_inc(done, 1)
                else:
                    mark(ins)

        @block.sync
        def _(sp):
            xr = x.rearrange("(t b) (h r) w c -> t (b h) (r w c)", t=2, r=PATCH)
            def load_images(t):
                sp.dma_start(area_a[:, t * PATCH * IMG * CH:(t + 1) * PATCH * IMG * CH], xr[t]).then_inc(x_in[t], 16)

            load_images(0)
            sp.dma_start(w_row[0:HALF, 0:6, :], w_qkv.rearrange("(c p) d -> p c d", p=HALF)).then_inc(w_in, 16)
            sp.dma_start(w_row[0:HALF, 6:8, :], w_proj.rearrange("(c p) d -> p c d", p=HALF)).then_inc(w_in, 16)
            load_images(1)
            for t in range(2):
                sp.wait_ge(x_in[t], 16)
            sp.wait_ge(tokw_in, 16)
            sp.wait_ge(w_in, 32)
            sp.dma_start(w1_sb[0:HALF, :, 0, :], w1[:, 0:HALF, :].rearrange("e d f -> d e f")).then_inc(w1_in, 16)
            sp.dma_start(w1_sb[0:HALF, :, 1, :], w1[:, HALF:C, :].rearrange("e d f -> d e f")).then_inc(w1_in, 16)
            sp.dma_start(w1_sb[HALF:HALF + 1, :, 0, :], b1.unsqueeze(0)).then_inc(w1_in, 16)
            for c in range(FC):
                sp.dma_start(w2_sb[:, :, c, :], w2[:, c * 128:(c + 1) * 128, :].rearrange("e p d -> p e d")).then_inc(w2_in, 16)
            sp.wait_ge(pool_s, P_FILL)
            sp.dma_start(slots.rearrange("(t p) c -> p t c", p=128),
                         fill.unsqueeze(1).to_broadcast([128, SLOT_TILES, PAYW])).then_inc(filled, 16)
            sp.dma_start(b2_rows.rearrange("p e c -> p (e c)"),
                         b2.rearrange("e c -> (e c)").partition_broadcast(128)).then_inc(b2_in, 16)
            sp.wait_ge(scattered, 16 * NT)
            sl = slots.rearrange("(t p) c -> p t c", p=128)
            sp.dma_start(xg[:, BY_PE:BY_PE + 2, :], sl[:, BY_PE:BY_PE + 2, :]).then_inc(slots_in0, 16)
            sp.dma_start(xg[:, BY_PE + 2:SLOT_TILES, :], sl[:, BY_PE + 2:SLOT_TILES, :]).then_inc(slots_in1, 16)

        @block.gpsimd
        def _(pool):
            mark, _ = tally(consts)
            mark(pool.memset(ident[:, :], 0.0))
            mark(pool.memset(identb[:, :], 0.0))
            mark(pool.memset(head_mask, 1.0))
            mark(pool.memset(tri[:, :], 1.0))
            mark(pool.memset(ones_b[:, :], 1.0))
            mark(pool.memset(magic_c, MAGIC))
            mark(pool.memset(exp_c, 157.0 * 2.0 ** 23))
            mark(pool.memset(pow_e[:, :], -0.5))
            mark(pool.memset(gin, 0.0))
            n = mark(pool.memset(ones_f[:, :], 1.0))
            pool.wait_ge(consts, n)
            mark(pool.affine_select(out=ident[:, :], in_=ident[:, :], compare_op=ALU.not_equal, fill=1.0,
                                    base=0, pattern=[[-1, 128]], channel_multiplier=1))
            mark(pool.affine_select(out=identb[:, :], in_=identb[:, :], compare_op=ALU.not_equal, fill=1.0,
                                    base=0, pattern=[[-1, 128]], channel_multiplier=1))
            mark(pool.affine_select(out=tri[:, :], in_=tri[:, :], compare_op=ALU.is_gt, fill=0.0,
                                    base=0, pattern=[[1, 128]], channel_multiplier=-1))
            n = mark(pool.affine_select(out=head_mask, in_=head_mask, compare_op=ALU.is_ge, fill=0.0,
                                        base=0, pattern=[[-HD, HG]], channel_multiplier=1))
            pool.wait_ge(consts, n)
            mark(pool.affine_select(out=head_mask, in_=head_mask, compare_op=ALU.is_ge, fill=0.0,
                                    base=HD - 1, pattern=[[HD, HG]], channel_multiplier=-1))
            mark(pool.iota(e_idx[:, :, :], [[0, NT], [1, E]], base=0, channel_multiplier=0,
                           allow_small_or_imprecise_dtypes=True))
            mark(pool.iota(te_idx[:, :], [[1, SLOT_TILES]], base=0, channel_multiplier=0,
                           allow_small_or_imprecise_dtypes=True))
            mark(pool.iota(smalli[:, 0:1], [[0, 1]], base=0, channel_multiplier=1))
            mark(pool.iota(smalli[:, 1:1 + NT - 1], [[N * B // 2, 2], [1, SIDE]], base=1, channel_multiplier=SIDE))
            assert mark(pool.iota(smalli[:, NT:NT + 1], [[0, 1]], base=0, channel_multiplier=N)) == CONSTS

            for i, (a, b) in enumerate(LN1_COLS):
                pool.wait_ge(var_ready, i + 1)
                pool.tensor_tensor(rstd[:, a:b], mv[:, a:b, 1], pow_e[:, a:b], ALU.pow).then_inc(rstd_ready, 1)
            pool.wait_ge(embed_psum, 8)
            pool.memset(part(area_a, RA, [RB]), 0.0).then_inc(qmask_zero, 1)
            for i in range(3):
                pool.wait_ge(stat_ready, i + 1)
                pool.partition_all_reduce(gout, gin, 128, RMAX).then_inc(all_max, 1)
            pool.wait_ge(p_ready, len(P_PARTS))
            pool.memset(fill, 0.0).then_inc(pool_s, 1)
            pool.iota(slot_idx, [[1, 128]], base=0, channel_multiplier=0,
                      allow_small_or_imprecise_dtypes=True).then_inc(slot_idx_ready, 1)
            pool.wait_ge(stat_ready, 4)
            pool.partition_all_reduce(gout, gin, 128, RMAX).then_inc(all_max, 1)
            for i, (a, b) in enumerate(LN2_TILES):
                pool.wait_ge(var_ready, 3 + i)
                pool.tensor_tensor(pay[:, a:b, COL_RSTD], rstd[:, a:b], pow_e[:, a:b], ALU.pow).then_inc(rstd_ready, 1)
            pool.wait_ge(dest_ready, 1)
            pool.wait_ge(filled, 16)
            for j in range(NT):
                n = 128 if j < NT - 1 else B
                pool.indirect_dma_start(out=slots, out_offset=bass.IndirectOffsetOnAxis(ap=dest[0:n, j:j + 1], axis=0),
                                        in_=pay[0:n, j, :], in_offset=None, bounds_check=SLOTS - 1,
                                        oob_is_err=False).then_inc(scattered, 16)
            out_rows = out.rearrange("b n c -> (b n) c")

            def store(t, k):
                pool.wait_ge(y_done, t + 1)
                if t in (0, BY_PE):
                    pool.wait_ge(rows_ready, 1 + t // BY_PE)
                pool.indirect_dma_start(out=out_rows, out_offset=bass.IndirectOffsetOnAxis(ap=slot_row[:, t:t + 1], axis=0),
                                        in_=y_out[k], in_offset=None, bounds_check=T - 1,
                                        oob_is_err=False).then_inc((stored, stored1)[k], 16)

            for t in range(SLOT_TILES):
                store(t, t % 2)
            pool.wait_ge(stored, 16 * SLOT_TILES // 2)
            pool.wait_ge(stored1, 16 * SLOT_TILES // 2)

        @block.tensor
        def _(pe):
            pe.wait_ge(consts, CONSTS)

            def warm(n):
                for _ in range(n):
                    pe.matmul(ps[:, WARM_BANK, 0:128], ones_b[:, :], ones_b[:, :], start=True, stop=True)

            warm(36)
            def turn_weights(k):
                pe.wait_ge(w_int_ready, 8)
                for c in range(8):
                    mm = pe.transpose(bank_b(W_TBANK + k)[0:HALF, c * HALF:(c + 1) * HALF],
                                      w_int[0:HALF, c, k * HALF:(k + 1) * HALF], identb[0:HALF, 0:HALF])
                mm.then_inc(w_t_psum, 1)

            def turn_vectors():
                pe.wait_ge(w_t_ready, 1)
                pe.wait_ge(bq_in, 32)
                pe.wait_ge(small_in, 16 * 3)
                pe.transpose(ps[0:HALF, W_TBANK, 0:8], b_row[0:8, :], ident[0:8, 0:8])
                for k in range(2):
                    mm = pe.matmul(ps[:, W_TBANK, 8:8 + E], ones_f[:, :], ws_sb[:, k, :], start=k == 0, stop=k == 1)
                mm.then_inc(vectors_psum, 1)

            def turn_patches(j):
                if j in V_PACKS:
                    pe.wait_ge(packed_v, V_PACKS.index(j) + 1)
                else:
                    pe.wait_ge(packed_a, A_PACKS.index(j) + 1)
                if j >= 2:
                    pe.wait_ge(xt_ready_v, j - 1)
                    pe.wait_ge(xt_ready_a, j - 1)
                for k in range(KC):
                    mm = pe.transpose(ps[:, 2 * (j % 2) + k // 4, (k % 4) * 128:(k % 4 + 1) * 128],
                                      x_c[:, j, k * 128:(k + 1) * 128], ident[:, :])
                mm.then_inc(xt_psum, 1)

            def embed(j):
                pe.wait_ge(xt_ready_v, j + 1)
                pe.wait_ge(xt_ready_a, j + 1)
                if j == 0:
                    pe.wait_ge(tokw_in, 16)
                if j >= 2:
                    pe.wait_ge(embed_done, j - 1)
                for k in range(KC):
                    mm = pe.matmul(ps[:, 4 + j % 2, 0:C], x_t[j % 2][:, k, :], tokw_sb[:, k, :],
                                   start=k == 0, stop=k == KC - 1)
                mm.then_inc(embed_psum, 1)

            def turn_normalised(i):
                tiles, half = XG[i]
                pe.wait_ge(xn_ready, 5 if i < XG_A else NT)
                if i == 0:
                    pe.wait_ge(w_t_ready, 2)
                    pe.wait_ge(bq_ready, 2)
                if i >= XG_A:
                    pe.wait_ge(res_done, i - 1)
                n = 0
                for k in ([half] if half is not None else [0, 1]):
                    for j in tiles:
                        w = 128 if j < NT - 1 else B
                        mm = pe.transpose(ps[0:HALF, XG_BANK[i], n:n + w], xn[0:w, j, k * HALF:(k + 1) * HALF],
                                          ident[0:w, 0:w])
                        n += w
                mm.then_inc(xnt_psum, 1)

            turn_patches(0)
            turn_patches(1)
            embed(0)
            turn_patches(2)
            embed(1)
            turn_patches(3)
            embed(2)
            turn_patches(4)
            embed(3)
            turn_patches(5)
            embed(4)
            turn_patches(6)
            embed(5)
            turn_patches(7)
            embed(6)
            turn_weights(0)
            turn_weights(1)
            turn_vectors()
            turn_normalised(0)
            turn_normalised(1)
            turn_normalised(2)
            embed(7)

            def y_of(s, c):
                a, b = PIECES[s]
                bank, col = y_bank(c, s)
                if s == 0 and c >= 4:
                    pe.wait_ge(embed_done, c + 3)
                if s == 2:
                    pe.wait_ge(y_ready, c + 1)
                for n, (k, q) in enumerate([(k, q) for q in range(3) for k in range(2)]):
                    mm = pe.matmul(ps[0:HALF, bank, col:col + b - a], w_t[:, k, c * HALF:(c + 1) * HALF],
                                   x_part[0:HALF, q, k, a:b], start=n == 0, stop=n == 5)
                mm.then_inc(y_psum, 1)

            pe.wait_ge(lo_done, XG_A)
            for c in range(3):
                y_of(0, c)
            turn_normalised(3)
            turn_normalised(4)
            for c in range(3, 6):
                y_of(0, c)
            pe.wait_ge(lo_done, 5)
            for s in (1, 2):
                for c in range(6):
                    y_of(s, c)

            for i in range(6):
                if i == 1:
                    pe.wait_ge(y_ready, 12)
                if i >= 2:
                    pe.wait_ge(h0_ready, i - 1)
                for n in range(4 * i, min(4 * i + 4, 2 * NT)):
                    mm = pe.transpose(ps[0:HALF, H0_BANK[i], (n % 4) * 128:(n % 4 + 1) * 128],
                                      pay[:, n // 2, n % 2 * HALF:(n % 2 + 1) * HALF], ident[:, :])
                if i < 5:
                    mm.then_inc(h0_psum, 1)
                if i == 1:
                    pe.wait_ge(y_ready, 18)
                if i >= 1:
                    pe.wait_ge(h0_ready, i)
                    for j in range(2 * i - 2, min(2 * i, NT)):
                        for k in range(2):
                            mm = pe.matmul(ps[:, LG0_BANK, j * E:(j + 1) * E], h0_t[0:HALF, j, k, :], ws_sb[:, k, :],
                                           start=k == 0, stop=k == 1)
            mm.then_inc(lg0_psum, 1)

            for g in range(2):
                for G in range(NG):
                    if (g, G) in ((0, 0), (0, GH), (1, 0)):
                        pe.wait_ge(k_exp_ready, 1 + 2 * g + (G == GH))
                    if (g, G) == (1, 0):
                        pe.wait_ge(k_exp_ready_a, 1)
                    images = range(GI * G, min(GI * G + GI, B))
                    for b in images:
                        mm = pe.matmul(ps[0:R, G // 2, (G % 2) * 2 * M + g * M:(G % 2) * 2 * M + (g + 1) * M],
                                       qmask[0:HALF, g, b, :], k_exp[0:HALF, g, b, :, :],
                                       start=b == images[0], stop=b == images[-1])
                    if g == 1 and G % 2 == 1:
                        mm.then_inc(s_psum, 1)

            n = 0
            pe.wait_ge(lg0_ready, 1)
            pe.wait_ge(v_exp_t_ready, 2)
            for g in range(2):
                pe.wait_ge(v_exp_t_ready_a, g + 1)
                for b0 in range(0, B, VB):
                    if n >= 3:
                        pe.wait_ge(v_exp_ready, n - 2)
                    for b in range(b0, min(b0 + VB, B)):
                        mm = pe.transpose(bank_b(5 + n % 3)[0:M, (b - b0) * HALF:(b - b0 + 1) * HALF],
                                          v_exp_t[0:HALF, g, b, :, :], identb[0:HALF, 0:HALF])
                    mm.then_inc(v_psum, 1)
                    n += 1
            NV = n

            def turn_probs(n):
                blocks, bank = PT[n]
                for i in blocks:
                    mm = pe.transpose(bank_b(bank)[0:M, (i - blocks[0]) * 128:(i - blocks[0]) * 128 + R],
                                      probs[0:R, i, :], identb[0:R, 0:R])
                mm.then_inc(pt_psum, 1)

            def attend(g, b0, b1):
                for b in range(b0, b1):
                    mm = pe.matmul(ps[0:HALF, av_bank(g, b), (b % AVI) * N:(b % AVI + 1) * N],
                                   v_exp[0:M, g, b, :], probs_t[0:M, 2 * (b // GI) + g, (b % GI) * N:(b % GI + 1) * N],
                                   start=True, stop=True)
                return mm

            pe.wait_ge(v_exp_ready, NV)
            pe.wait_ge(p_ready, 1)
            turn_probs(0)
            turn_probs(1)
            pe.wait_ge(pt_ready_a, 2)
            attend(0, 0, B // 2).then_inc(av_psum, 1)
            pe.wait_ge(p_ready, 2)
            turn_probs(2)
            attend(1, 0, B // 2).then_inc(av_psum, 1)
            part1, part2 = (P_PARTS[i][1] * GI for i in range(2))
            for g in range(2):
                attend(g, B // 2, part1)
            pe.wait_ge(pt_ready_a, 3)
            for g in range(2):
                attend(g, part1, 3 * AVI)
            pe.wait_ge(p_ready, 3)
            turn_probs(3)
            attend(1, 3 * AVI, part2)
            pe.wait_ge(pt_ready_v, 1)
            attend(0, 3 * AVI, part2)
            for g in range(2):
                attend(g, part2, B).then_inc(av_psum, 1)

            for i, (a, b, bank) in enumerate(PROJ):
                pe.wait_ge(oq_ready, (2, 4, 5)[i])
                for m in range(2):
                    for g in range(2):
                        mm = pe.matmul(ps[0:HALF, bank + m, 0:b - a], w_t[:, g, 3 * C + m * HALF:3 * C + (m + 1) * HALF],
                                       o_q[0:HALF, g, a:b], start=g == 0, stop=g == 1)
                    mm.then_inc(proj_psum, 1)
            for i, (tiles, bank) in enumerate(QI):
                pe.wait_ge(qi_ready, i + 1)
                for j in tiles:
                    for k in range(2):
                        pe.transpose(bank_b(bank)[:, (j % 4) * C + k * HALF:(j % 4) * C + (k + 1) * HALF],
                                     qi_t[0:HALF, k, j * 128:(j + 1) * 128], identb[0:HALF, 0:HALF])
                    for k in range(2):
                        mm = pe.matmul(ps[:, 7, j * 3 * E:(j + 1) * 3 * E], qi_t[0:HALF, k, j * 128:(j + 1) * 128],
                                       ws_part[:, k].rearrange("p e q -> p (e q)"), start=k == 0, stop=k == 1)
                mm.then_inc(qi_psum, 1)
            pe.wait_ge(hot_ready, 1)
            pe.matmul(ps[:, 0, 0:NT * E], tri[:, :], hot_b[:, :, :], start=True, stop=False, skip_group_check=True)
            for j in range(NT - 1):
                pe.matmul(ps[:, 0, (j + 1) * E:NT * E], ones_b[:, :],
                          hot_b[:, j:j + 1, :].to_broadcast([128, NT - 1 - j, E]), start=False, stop=j == NT - 2,
                          skip_group_check=True)
            for j in range(NT):
                mm = pe.matmul(ps[:, 1, 0:E], ones_b[:, :], hot_b[:, j, :], start=j == 0, stop=j == NT - 1)
            mm.then_inc(rank_psum, 1)

            warm(28)
            def fill_slots(i, tiles):
                for j in tiles:
                    w = 128 if j < NT - 1 else B
                    pe.wait_ge(to_slot_ready, NT * i + j + 1)
                    mm = pe.matmul(ps[:, 2 + i, 0:PAYW], to_slot[i][0:w, j, :], pay[0:w, j, :], start=j == 0, stop=j == NT - 1)
                if tiles[-1] == NT - 1:
                    mm.then_inc(xg0_psum, 1)

            fill_slots(0, range(NT))
            fill_slots(1, range(4))
            pe.wait_ge(w2_in, 16 * FC)

            def turn_tokens(t, k):
                pe.wait_ge(xg_ready, t + 1)
                if not isinstance(t, int) or t >= 1:
                    pe.wait_ge(xgt_ready, t)
                for c in range(2):
                    mm = pe.transpose(ps[0:HALF, 7, c * 128:(c + 1) * 128], xg_n[k][:, c * HALF:(c + 1) * HALF],
                                      ident[:, :])
                mm.then_inc(xgt_psum, 1)

            def first_product(t, k):
                pe.wait_ge(xgt_ready, t + 1)
                pe.wait_ge(w1_tile_ready, 2 * t + 2)
                if not isinstance(t, int) or t >= 2:
                    pe.wait_ge(h_ready, t - 1)
                for f in range(FC):
                    for c in range(2):
                        p = HALF + 1 if c == 0 else HALF
                        mm = pe.matmul(ps[:, 2 * k + f // 3, (f % 3) * 128:(f % 3 + 1) * 128],
                                       w1_tile[k][0:p, c, f * 128:(f + 1) * 128], xg_t[k][0:p, c, :],
                                       start=c == 0, stop=c == 1)
                mm.then_inc(g1_psum, 1)

            def second_product(t, k):
                e = pe.value_load(tile_expert[0:1, bass.ds(t, 1)], min_val=0, max_val=E - 1)
                pe.wait_ge(h_ready, t + 1)
                if not isinstance(t, int) or t >= 2:
                    pe.wait_ge(y_done, t - 1)
                for f in range(FC):
                    mm = pe.matmul(ps[:, 4 + k, 0:C], h_t[k][:, f, :], w2_sb[:, bass.ds(e, 1), f, :],
                                   start=f == 0, stop=f == FC - 1)
                mm.then_inc(g2_psum, 1)

            turn_tokens(0, 0)
            fill_slots(1, range(4, NT))
            pe.wait_ge(table_ready, 1)
            first_product(0, 0)
            turn_tokens(1, 1)
            first_product(1, 1)
            second_product(0, 0)
            turn_tokens(2, 0)

            def step(t, k, more=2):
                if more >= 2:
                    turn_tokens(t + 2, k)
                if more >= 1:
                    first_product(t + 1, 1 - k)
                second_product(t, k)

            step(1, 1)
            with pe.Fori(2, SLOT_TILES - 2, 2) as t:
                step(t, 0)
                step(t + 1, 1)
            step(SLOT_TILES - 2, 0, 1)
            step(SLOT_TILES - 1, 1, 0)

        @block.vector
        def _(v):
            mark, marked = tally(vec)

            def then(instruction):
                v.wait_ge(vec, mark(instruction))

            mark(v.memset(pay[B:128, NT - 1, :], 0.0))
            mark(v.memset(stat[:, :, :], 0.0))
            wr = w_row[0:HALF]
            h96 = slice(0, HALF)

            def pack(j):
                v.wait_ge(x_in[j // SIDE], 16)
                v.tensor_copy(x_c[:, j, :].rearrange("p (r s) -> p r s", s=SEG),
                              x_sb[:, j // SIDE, :, j % SIDE, :]).then_inc(packed_v, 1)

            def patches_out(j):
                v.wait_ge(xt_psum, j + 1)
                if j >= 2:
                    v.wait_ge(embed_psum, j - 1)
                v.tensor_copy(x_t[j % 2][:, X_SPLIT:KC, :].rearrange("p k t -> p (k t)"),
                              ps[:, 2 * (j % 2) + 1, 0:(KC - X_SPLIT) * 128]).then_inc(xt_ready_v, 1)

            def embedded(j):
                v.wait_ge(embed_psum, j + 1)
                v.tensor_tensor(pay[:, j, 0:C], ps[:, 4 + j % 2, 0:C], tokb_row[:, :], ALU.add).then_inc(embed_done, 1)
                v.wait_ge(embed_done, j + 1)
                mark(v.bn_stats(bn[:, LN1_TILES.index(j), :], pay[:, j, 0:C]))

            def weight_scales():
                mark(v.tensor_scalar(w_max[h96], w_max[h96], 0.0, None, ALU.max))
                then(v.tensor_scalar(w_min[h96], w_min[h96], 0.0, None, ALU.min))
                then(v.tensor_tensor(w_scale[h96], w_max[h96], w_min[h96], ALU.subtract))
                then(v.tensor_scalar(w_scale[h96], w_scale[h96], INV_255, QEPS, ALU.mult, ALU.max))
                v.reciprocal(w_inv[h96], w_scale[h96]).then_inc(w_inv_ready, 1)
                v.wait_ge(w_inv_ready, 1)
                then(v.tensor_tensor(w_him[h96], w_min[h96], w_inv[h96], ALU.mult))
                then(v.tensor_scalar(w_him[h96], w_him[h96], MAGIC, 255.0, ALU.add, ALU.add))

            def weight_integers(chunks):
                v.wait_ge(w_rounded, 8)
                for c in chunks:
                    v.tensor_scalar(w_int[h96, c], w_v[h96, c], w_him[h96, c:c + 1], MAGIC, ALU.min,
                                    ALU.subtract).then_inc(w_int_ready, 1)

            def weights_out(k):
                v.wait_ge(w_t_psum, k + 1)
                v.tensor_copy(w_t[:, k, :], bank_b(W_TBANK + k)[h96, 0:8 * HALF]).then_inc(w_t_ready, 1)

            def part_variance(i):
                a, b = LN1_COLS[i]
                for n in range(a, b):
                    last = mark(v.bn_aggr(mv[:, n, :], bn[:, n, :]))
                v.wait_ge(vec, last)
                v.tensor_scalar(mv[:, a:b, 1], mv[:, a:b, 1], LN_EPS, None, ALU.add).then_inc(var_ready, 1)

            def part_rows(i):
                a, b = LN1_COLS[i]
                v.wait_ge(rstd_ready, i + 1)
                for n in range(a, b):
                    j = LN1_TILES[n]
                    v.tensor_scalar(xn[:, j, :], pay[:, j, 0:C], mv[:, n, 0:1], rstd[:, n:n + 1], ALU.subtract,
                                    ALU.mult).then_inc(xn_ready, 1)

            pack(0)
            pack(2)
            patches_out(0)
            patches_out(1)
            v.wait_ge(tokb_in, 16)
            embedded(0)
            patches_out(2)
            v.wait_ge(w_in, 32)
            mark(v.tensor_reduce(w_max[h96], wr, AX.X, ALU.max))
            embedded(1)
            patches_out(3)
            then(v.tensor_reduce(w_min[h96], wr, AX.X, ALU.min))
            embedded(2)
            patches_out(4)
            weight_scales()
            embedded(3)
            v.wait_ge(small_in, 16 * 3)
            last = mark(v.bn_stats(bn[:, 4, :], pay[:, 8, 0:C]))
            patches_out(5)
            v.wait_ge(vec, last)
            part_variance(0)
            embedded(4)
            patches_out(6)
            weight_integers(range(8))
            embedded(5)
            v.wait_ge(w_int_ready, 8)
            part_rows(0)
            v.wait_ge(consts, CONSTS)
            patches_out(7)
            weights_out(0)
            weights_out(1)
            v.wait_ge(vectors_psum, 1)
            v.tensor_copy(bq_col[h96], ps[h96, W_TBANK, 0:8]).then_inc(bq_ready, 1)
            v.tensor_copy(colsum, ps[:, W_TBANK, 8:8 + E]).then_inc(bq_ready, 1)

            def token_view(q, k, i):
                tiles, half = XG[i]
                if half is None:
                    return x_part[h96, q].rearrange("p k (b n) -> p k b n", n=N)[:, :, :, 0]
                t = tiles[0] // SIDE
                return x_part[h96, q, half, t * T // 2:(t + 1) * T // 2].rearrange(
                    "p (b n) -> p b n", n=N)[:, :, 1:N].rearrange("p b (h w) -> p w b h", w=SIDE)

            def split(i):
                tiles, half = XG[i]
                n = 512 if half is not None else 2 * B
                shape = dict(w=SIDE, b=B // 2) if half is not None else dict(w=2)
                pat = "p (w b h) -> p w b h" if half is not None else "p (w b) -> p w b"
                return n, (lambda ap: ap[h96, 0:n].rearrange(pat, **shape))

            def residue_of(i):
                n, view = split(i)
                v.wait_ge(hi_done, i + 1)
                if i >= 2:
                    v.wait_ge(lo_done, i - 1)
                v.tensor_tensor(view(residue[i % 2]), view(ps[:, XG_BANK[i], :]), token_view(0, None, i),
                                ALU.subtract).then_inc(res_done, 1)

            def lowest(i):
                n, view = split(i)
                v.wait_ge(mid_done, i + 1)
                v.tensor_tensor(token_view(2, None, i), view(residue[i % 2]), token_view(1, None, i),
                                ALU.subtract).then_inc(lo_done, 1)

            def extremes_of(p, i, values, n=1):
                mark(v.tensor_reduce(stat[p, 0, 1 + i:1 + i + n], values, AX.X, ALU.max))
                mark(v.tensor_reduce(stat[p, 1, 1 + i:1 + i + n], values, AX.X, ALU.min, negate=True))

            def y_extremes(s, c):
                v.wait_ge(y_ready, 6 * s + c + 1)
                extremes_of(h96, 6 * s + c, y_sb[h96, c, PIECES[s][0]:PIECES[s][1]])

            residue_of(0)
            residue_of(1)
            lowest(0)
            lowest(1)
            residue_of(2)
            lowest(2)
            embedded(6)
            then(v.tensor_scalar(smalli[:, 20:21], smalli[:, 0:1], 2, None, ALU.arith_shift_right))
            then(v.tensor_copy(n9[0][:, 0:1], smalli[:, 20:21]))
            mark(v.tensor_scalar(pay[:, 0:NT - 1, COL_ROW], smalli[:, 1:NT], n9[0][:, 0:1], float(-NO_ROW), ALU.add, ALU.add))
            mark(v.tensor_scalar(pay[0:B, NT - 1, COL_ROW:COL_ROW + 1], smalli[0:B, NT:NT + 1], float(-NO_ROW), None, ALU.add))
            embedded(7)
            v.wait_ge(vec, marked())
            part_variance(1)
            y_extremes(0, 0)
            part_rows(1)
            y_extremes(0, 1)
            residue_of(3)
            residue_of(4)
            lowest(3)
            lowest(4)

            for c in range(2, 6):
                y_extremes(0, c)
            v.wait_ge(y_ready, 12)
            extremes_of(h96, 6, y_sb[h96, :, PIECES[1][0]:PIECES[1][1]], 6)
            for c in range(6):
                y_extremes(2, c)

            def over_all(count, which, meanwhile=None):
                v.wait_ge(vec, marked())
                v.tensor_reduce(gin, stat[:, :, 0:count + 1], AX.X, ALU.max).then_inc(stat_ready, 1)
                if meanwhile:
                    meanwhile()
                v.wait_ge(all_max, which)

            def scales(q, mul=1.0):
                mark(v.tensor_scalar(q[3], gout[:, 1:2], -1.0, None, ALU.mult))
                then(v.tensor_scalar(q[0], gout[:, 0:1], gout[:, 1:2], mul, ALU.add, ALU.mult))
                then(v.tensor_scalar(q[0], q[0], INV_255, QEPS, ALU.mult, ALU.max))
                if isinstance(mul, float):
                    v.reciprocal(q[1], q[0]).then_inc(bound_in, 1)
                else:
                    then(v.reciprocal(q[1], q[0]))
                    v.tensor_scalar(q[1], q[1], mul, None, ALU.mult).then_inc(bound_in, 1)

            def upper(q, which):
                v.wait_ge(bound_done, which)
                then(v.tensor_scalar(q[2], q[2], 255.0, None, ALU.add))

            over_all(18, 1)
            scales(q_y)
            upper(q_y, 1)
            then(v.tensor_scalar(a_mul, q_y[0], q_y[0], HD ** -0.5, ALU.mult, ALU.mult))
            then(v.memset(stat[:, :, :], 0.0))
            v.wait_ge(qmask_zero, 1)

            def queries(g, G0, G1):
                full = min(G1, NG - 1)
                for i in range(GI):
                    last = mark(v.tensor_scalar(
                        qmask[h96, g, GI * G0:GI * full, :].rearrange("p (G i) r -> p G i r", i=GI)[:, :, i, i * N:(i + 1) * N],
                        y_sb[h96, g, R * G0:R * full].rearrange("p (G r) -> p G r", r=R)[:, :, i * N:(i + 1) * N],
                        q_y[2][h96], MAGIC, ALU.min, ALU.subtract))
                if G1 == NG:
                    last = mark(v.tensor_scalar(qmask[h96, g, B - 1, 0:N], y_sb[h96, g, T - N:T], q_y[2][h96], MAGIC,
                                                ALU.min, ALU.subtract))

            def keys(g, b0, b1):
                return mark(v.tensor_scalar(kv_t[h96, g, b0 * N:b1 * N], y_sb[h96, 2 + g, b0 * N:b1 * N], q_y[2][h96],
                                            MAGIC, ALU.min, ALU.subtract))

            def key_blocks(g, b0, b1, heads, keys_at):
                v.wait_ge(vec, keys_at)
                spread(v.tensor_scalar, k_exp, kv_t, g, g, b0, b1, heads, k_exp_ready, mark)

            v.wait_ge(y_rounded, 1)
            queries(0, 0, GH)
            v.wait_ge(y_rounded, 2)
            key_blocks(0, 0, GH * GI, range(HG), keys(0, 0, GH * GI))
            v.wait_ge(y_rounded, 3)
            queries(0, GH, NG)
            v.wait_ge(y_rounded, 4)
            key_blocks(0, GH * GI, B, range(HG), keys(0, GH * GI, B))
            v.wait_ge(y_rounded, 5)
            v.wait_ge(lg0_psum, 1)
            v.tensor_scalar(kv_t[h96, 1, :], y_sb[h96, 3, :], q_y[2][h96], MAGIC, ALU.min, ALU.subtract).then_inc(k_ready, 1)
            v.wait_ge(y_rounded, 6)
            queries(1, 0, NG)
            v.wait_ge(k_ready, 1)
            spread(v.tensor_scalar, k_exp, kv_t, 1, 1, 0, B, range(K_HEADS), k_exp_ready, mark)
            v.wait_ge(y_rounded, 8)
            v.tensor_scalar(kv_t[h96, 2:4, :], y_sb[h96, 4:6, :], q_y[2][h96], MAGIC, ALU.min,
                            ALU.subtract).then_inc(v_ready, 1)
            v.wait_ge(v_ready, 1)
            spread(v.tensor_scalar, v_exp_t, kv_t, 2, 0, 0, B, range(V_HEADS[0]), v_exp_t_ready, mark)

            rm = row_max[0:R].rearrange("p (b l) -> p b l", b=5)
            for i in range(5):
                v.wait_ge(s_psum, i + 1)
                n = mark(v.tensor_reduce(rm[:, i], ps[0:R, i, 0:4 * M].rearrange("p (l m) -> p l m", m=N), AX.X, ALU.max))
                mark(v.tensor_reduce(stat[0:R, 1, 1 + i:2 + i], ps[0:R, i, 0:4 * M], AX.X, ALU.min, negate=True))
            v.wait_ge(vec, n)
            mark(v.tensor_reduce(stat[0:R, 0, 1:2], row_max[0:R], AX.X, ALU.max))
            over_all(5, 2, lambda: spread(v.tensor_scalar, v_exp_t, kv_t, 2, 0, 0, B, range(*V_HEADS), v_exp_t_ready, mark))
            scales(q_a, a_mul)
            c0 = np.float32(0.35815147)
            then(v.reciprocal(x0_pos, q_a[0]))
            mark(v.tensor_scalar(pol[:, 0:1], x0_pos, float(np.float32(-0.6931)), None, ALU.mult))
            mark(v.tensor_scalar(pol[:, 1:2], x0_pos, float(np.float32(0.96963238) / c0), None, ALU.mult))
            then(v.tensor_scalar(pol[:, 2:3], x0_pos, x0_pos, float(np.float32(1.0) / c0), ALU.mult, ALU.mult))
            then(v.tensor_scalar(pol_t, pol, 16777216.0, None, ALU.min))
            then(v.tensor_copy(smalli[:, 24:27], pol_t))
            then(v.tensor_copy(pol_f, smalli[:, 24:27]))
            then(v.tensor_tensor(pol_g, pol_f, pol_t, ALU.is_gt))
            then(v.tensor_tensor(pol_f, pol_f, pol_g, ALU.subtract))
            mark(v.tensor_scalar(pol_g, pol, 8388608.0, None, ALU.is_ge))
            then(v.tensor_tensor(pol_t, pol, pol_f, ALU.subtract))
            then(v.tensor_tensor(pol_t, pol_t, pol_g, ALU.mult))
            then(v.tensor_tensor(pol, pol_f, pol_t, ALU.add))
            mark(v.tensor_scalar(x0_30, pol[:, 0:1], 30.0, None, ALU.mult))
            mark(v.tensor_scalar(x0_pos, pol[:, 0:1], -1.0, None, ALU.mult))
            then(v.reciprocal(x0_inv, pol[:, 0:1]))
            then(v.tensor_scalar(q_bias, x0_inv, -0.5, -0.5, ALU.mult, ALU.add))
            upper(q_a, 2)
            v.wait_ge(attn_scaled, 1)
            then(v.tensor_scalar(row_max[0:R], row_max[0:R], q_a[2][0:R], None, ALU.min))
            LH = L // 2
            V_, XI, _, W_ = soft
            VI, _, QQ, WI = soft_i
            _, E_, Y0, _ = soft

            def half(ap, i):
                return ap[0:R, i * LH:(i + 1) * LH, :]

            def bc(ap, i):
                return ap[0:R, i * LH:(i + 1) * LH].unsqueeze(2).to_broadcast([R, LH, N])

            for i in range(2):
                v.wait_ge(attn_scaled, i + 2)
                then(v.scalar_tensor_tensor(out=half(V_, i), in0=half(V_, i), scalar=q_a[2][0:R], in1=bc(row_max, i),
                                            op0=ALU.min, op1=ALU.subtract))
                v.tensor_scalar(half(XI, i), half(V_, i), x0_30[0:R], None, ALU.max).then_inc(xi_ready, 1)
            for i in range(2):
                v.wait_ge(q_ready, i + 1)
                then(v.scalar_tensor_tensor(out=half(XI, i), in0=half(QQ, i), scalar=x0_pos[0:R], in1=half(XI, i),
                                            op0=ALU.mult, op1=ALU.add))
                if i == 0:
                    v.wait_ge(v_psum, 40 // VB)
                then(v.scalar_tensor_tensor(out=half(W_, i), in0=half(XI, i), scalar=pol[0:R, 1:2], in1=half(XI, i),
                                            op0=ALU.add, op1=ALU.mult))
                v.wait_ge(power_ready, i + 1)
                v.scalar_tensor_tensor(out=half(E_, i), in0=half(W_, i), scalar=pol[0:R, 2:3], in1=half(V_, i),
                                       op0=ALU.add, op1=ALU.mult).then_inc(e_ready, 1)
            v.wait_ge(e_ready, 2)
            for i in range(2):
                n = mark(v.tensor_reduce(row_sum[0:R, i * LH:(i + 1) * LH], half(E_, i), AX.X, ALU.add))
            v.wait_ge(vec, n)
            then(v.tensor_scalar(row_sum[0:R], row_sum[0:R], -1.0, None, ALU.mult))
            mark(v.tensor_tensor(before[:, :, :], e_idx[:, 0, :].unsqueeze(1).to_broadcast([128, E, E]),
                                 e_idx[:, 0, :].unsqueeze(2).to_broadcast([128, E, E]), ALU.is_lt))
            hi, mid, lo = (ws_part[:, :, :, q] for q in range(3))
            then(v.tensor_copy(hi, ws_sb[:, :, :]))
            then(v.tensor_tensor(ws_rest[:, :, :], ws_sb[:, :, :], hi, ALU.subtract))
            then(v.tensor_copy(mid, ws_rest[:, :, :]))
            mark(v.tensor_tensor(lo, ws_rest[:, :, :], mid, ALU.subtract))
            for G0, G1 in P_PARTS:
                l = slice(2 * HG * G0, 2 * HG * G1)
                w, wi, e, y0 = (ap[0:R, l, :] for ap in (W_, WI, E_, Y0))
                v.wait_ge(y0_ready, -(-l.stop // LH))
                then(v.tensor_tensor(w, e, y0, ALU.mult))
                then(v.scalar_tensor_tensor(out=w, in0=w, scalar=2.0, in1=y0, op0=ALU.subtract, op1=ALU.mult))
                then(v.tensor_tensor(w, w, row_sum[0:R, l].unsqueeze(2).to_broadcast([R, l.stop - l.start, N]), ALU.mult))
                then(v.tensor_scalar(w, w, 1048576.0, MAGIC, ALU.min, ALU.add))
                then(v.tensor_scalar(w, w, MAGIC, FOUR_THIRDS, ALU.subtract, ALU.mult))
                then(v.tensor_scalar(wi, wi, EXP_MASK, EXP_MASK, ALU.bitwise_and, ALU.bitwise_xor))
                v.scalar_tensor_tensor(out=probs[0:R, 2 * G0:2 * G1].rearrange("p a (h m) -> p (a h) m", m=N),
                                       in0=w, scalar=2.0 ** -14, in1=w, op0=ALU.is_ge, op1=ALU.mult).then_inc(p_ready, 1)
            mark(v.tensor_scalar(a_mul, q_y[0], 0.5, None, ALU.mult))
            then(v.memset(stat[:, :, :], 0.0))

            def attended(g, t):
                v.wait_ge(av_psum, 2 * t + g + 1)
                i = 4 * t + 2 * g
                extremes_of(h96, i, ps[h96, i:i + 2, 0:AVI * N], 2)

            attended(0, 0)
            v.wait_ge(pt_psum, 4)
            probs_out(v.tensor_copy, 3).then_inc(pt_ready_v, 1)
            attended(1, 0)
            attended(0, 1)
            attended(1, 1)
            over_all(8, 3)
            scales(q_o, a_mul)
            upper(q_o, 3)
            v.tensor_scalar(proj_scale[h96], w_scale[h96, 6:8], q_o[0][h96], None, ALU.mult).then_inc(proj_scale_ready, 1)
            then(v.memset(qi_t[h96, :, T:NT * 128], 0.0))
            for t in range(2):
                for g in range(2):
                    v.wait_ge(o_rounded, 2 * t + g + 1)
                    v.tensor_scalar(
                        o_q[h96, g, 512 * t:512 * t + 512].rearrange("p (w b h) -> p w b h", w=SIDE, b=B // 2),
                        o_v[h96, g, t * T // 2:(t + 1) * T // 2].rearrange("p (b n) -> p b n", n=N)[:, :, 1:N].rearrange(
                            "p b (h w) -> p w b h", w=SIDE), q_o[2][h96], MAGIC, ALU.min, ALU.subtract).then_inc(oq_ready, 1)
            v.tensor_scalar(o_q[h96, :, 1024:T], o_v[h96].rearrange("p g (b n) -> p g b n", n=N)[:, :, :, 0],
                            q_o[2][h96], MAGIC, ALU.min, ALU.subtract).then_inc(oq_ready, 1)
            mark(v.memset(stat[:, :, :], 0.0))

            v.wait_ge(vec, marked())
            for i, (a, b, _) in enumerate(PROJ):
                if i < 2:
                    for m in range(2):
                        v.wait_ge(proj_ready, 2 * i + m + 1)
                        extremes_of(h96, 2 * i + m, proj_t[h96, m, a:b])
                else:
                    v.wait_ge(proj_ready, 6)
                    extremes_of(h96, 4, proj_t[h96, :, a:b], 2)
            over_all(6, 4)
            scales(q_p)
            v.wait_ge(bound_in, 4)
            a, b, _ = PROJ[1]
            mark(v.tensor_scalar(proj_t[h96, :, a:b], proj_t[h96, :, a:b], q_p[1][h96], MAGIC, ALU.mult, ALU.add))
            upper(q_p, 4)
            for i, n in ((1, None), (0, 1), (2, 2)):
                a, b, _ = PROJ[i]
                if n is not None:
                    v.wait_ge(proj_rounded, n)
                v.tensor_scalar(qi_t[h96, :, a:b], proj_t[h96, :, a:b], q_p[2][h96], MAGIC, ALU.min,
                                ALU.subtract).then_inc(qi_ready, 1)
            for i, (tiles, bank) in enumerate(QI):
                v.wait_ge(qi_psum, i + 1)
                t = slice(tiles[0], tiles[-1] + 1)
                v.scalar_tensor_tensor(out=pay[:, t, 0:C],
                                       in0=bank_b(bank)[:, 0:len(tiles) * C].rearrange("p (a c) -> p a c", c=C),
                                       scalar=q_p[0], in1=pay[:, t, 0:C], op0=ALU.mult, op1=ALU.add).then_inc(h2_ready, 1)
            for i, (a, b) in enumerate(LN2_TILES):
                v.wait_ge(h2_ready, 3)
                for j in range(a, b):
                    n = mark(v.bn_stats(bn[:, j, :], pay[:, j, 0:C]))
                v.wait_ge(vec, n)
                for j in range(a, b):
                    n = mark(v.bn_aggr(pay[:, j, COL_MEAN:COL_MEAN + 2], bn[:, j, :]))
                v.wait_ge(vec, n)
                v.tensor_scalar(rstd[:, a:b], pay[:, a:b, COL_RSTD], LN_EPS, None, ALU.add).then_inc(var_ready, 1)

            def per_tile(ap):
                return ap.unsqueeze(2).to_broadcast([128, NT, E])

            def per_expert(ap):
                return ap.unsqueeze(1).to_broadcast([128, NT, E])

            mark(v.tensor_tensor(ex[:, :, :], per_expert(colsum), per_tile(pay[:, :, COL_MEAN]), ALU.mult))
            then(v.tensor_reduce(lg[:, :, :], ps[:, 7, 0:NT * E * 3].rearrange("p (j e q) -> p j e q", e=E, q=3), AX.X, ALU.add))
            v.wait_ge(lg0_ready, 1)
            then(v.scalar_tensor_tensor(out=lg[:, :, :], in0=lg[:, :, :], scalar=q_p[0], in1=lg0[:, :, :],
                                        op0=ALU.mult, op1=ALU.add))
            then(v.tensor_tensor(lg[:, :, :], lg[:, :, :], ex[:, :, :], ALU.subtract))
            v.wait_ge(rstd_ready, 4)
            then(v.tensor_tensor(lg[:, :, :], lg[:, :, :], per_tile(pay[:, :, COL_RSTD]), ALU.mult))
            then(v.tensor_tensor(lg[:, :, :], lg[:, :, :], per_expert(bs_row[:, :]), ALU.add))
            then(v.tensor_reduce(n9[0][:, :], lg[:, :, :], AX.X, ALU.max))

            v.tensor_tensor(ex[:, :, :], lg[:, :, :], per_tile(n9[0][:, :]), ALU.subtract).then_inc(lg_max, 1)
            then(v.tensor_tensor(hot[:, :, :], lg[:, :, :], per_tile(n9[0][:, :]), ALU.is_lt))
            then(v.scalar_tensor_tensor(out=hot[:, :, :], in0=hot[:, :, :], scalar=float(E), in1=e_idx[:, :, :],
                                        op0=ALU.mult, op1=ALU.add))
            then(v.tensor_reduce(n9[1][:, :], hot[:, :, :], AX.X, ALU.min))
            then(v.tensor_tensor(hot_b[:, :, :], e_idx[:, :, :], per_tile(n9[1][:, :]), ALU.is_equal))
            v.memset(hot_b[64:128, NT - 1, :], 0.0).then_inc(hot_ready, 1)
            v.wait_ge(hot_ready, 1)
            v.wait_ge(ex_ready, 1)
            then(v.tensor_reduce(n9[2][:, :], ex[:, :, :], AX.X, ALU.add))
            then(v.reciprocal(pay[:, :, COL_P], n9[2][:, :]))
            v.wait_ge(rank_psum, 1)
            tiles, ends, starts, _ = e8
            then(v.tensor_scalar(tiles[:, :], ps[:, 1, 0:E], 1.0 / 128, 127.0 / 128 - 0.5 + 1.0 / 256, ALU.mult, ALU.add))
            then(v.tensor_scalar(tiles[:, :], tiles[:, :], MAGIC, MAGIC, ALU.add, ALU.subtract))
            then(v.tensor_tensor(before_sum[:, :, :], before[:, :, :], tiles[:, :].unsqueeze(1).to_broadcast([128, E, E]), ALU.mult))
            then(v.tensor_reduce(starts[:, :], before_sum[:, :, :], AX.X, ALU.add))
            then(v.scalar_tensor_tensor(out=rk[:, :, :], in0=starts[:, :].unsqueeze(1).to_broadcast([128, NT, E]),
                                        scalar=128.0, in1=ps[:, 0, 0:NT * E].rearrange("p (j e) -> p j e", e=E),
                                        op0=ALU.mult, op1=ALU.add))
            then(v.tensor_tensor(rk[:, :, :], rk[:, :, :], hot_b[:, :, :], ALU.mult))
            then(v.tensor_reduce(n9[1][:, :], rk[:, :, :], AX.X, ALU.add))
            v.tensor_copy(dest[:, :], n9[1][:, :]).then_inc(dest_ready, 1)
            v.wait_ge(slot_idx_ready, 1)
            for i in range(BY_PE):
                for j in range(NT):
                    v.tensor_scalar(to_slot[i][:, j, :], slot_idx, 128.0 * i, n9[1][:, j:j + 1], ALU.add,
                                    ALU.is_equal).then_inc(to_slot_ready, 1)
            then(v.tensor_tensor(ends[:, :], starts[:, :], tiles[:, :], ALU.add))
            then(v.tensor_tensor(te[:, :, :], ends[:, :].unsqueeze(1).to_broadcast([128, SLOT_TILES, E]),
                                 te_idx[:, :].unsqueeze(2).to_broadcast([128, SLOT_TILES, E]), ALU.is_le))
            then(v.tensor_reduce(te_idx[:, :], te[:, :, :], AX.X, ALU.add))
            v.tensor_scalar(tile_expert[:, :], te_idx[:, :], float(E - 1), None, ALU.min).then_inc(table_ready, 1)

            for k in range(2):
                mark(v.memset(xg_t[k][HALF:HALF + 1, 0, :], 1.0))

            def normalise(t, k):
                if not isinstance(t, int) or t >= 2:
                    v.wait_ge(xgt_psum, t - 1)
                v.tensor_scalar(xg_n[k], xg[:, bass.ds(t, 1), 0:C], xg[:, bass.ds(t, 1), COL_MEAN:COL_MEAN + 1],
                                xg[:, bass.ds(t, 1), COL_RSTD:COL_RSTD + 1], ALU.subtract, ALU.mult).then_inc(xg_ready, 1)

            def expert_weights(t, k):
                if not isinstance(t, int) or t >= 2:
                    v.wait_ge(g1_psum, t - 1)
                e = v.value_load(tile_expert[0:1, bass.ds(t, 1)], min_val=0, max_val=E - 1)
                v.tensor_copy(w1_tile[k][0:HALF + 1, 0, :], w1_sb[0:HALF + 1, bass.ds(e, 1), 0, :]).then_inc(w1_tile_ready, 1)
                v.tensor_copy(w1_tile[k][0:HALF, 1, :], w1_sb[0:HALF, bass.ds(e, 1), 1, :]).then_inc(w1_tile_ready, 1)

            def finish(t, k):
                e = v.value_load(tile_expert[0:1, bass.ds(t, 1)], min_val=0, max_val=E - 1)
                v.wait_ge(g2_psum, t + 1)
                v.tensor_tensor(y_b[k], ps[:, 4 + k, 0:C], b2_rows[:, bass.ds(e, 1), :], ALU.add).then_inc(y_b_done, 1)
                if not isinstance(t, int) or t >= 2:
                    v.wait_ge((stored, stored1)[k], 8 * (t - k))
                v.wait_ge(y_b_done, t + 1)
                v.scalar_tensor_tensor(out=y_out[k], in0=y_b[k], scalar=xg[:, bass.ds(t, 1), COL_P:COL_P + 1],
                                       in1=xg[:, bass.ds(t, 1), 0:C], op0=ALU.mult, op1=ALU.add).then_inc(y_done, 1)

            def slot_rows(t0, t1):
                v.tensor_scalar(slot_row[:, t0:t1].bitcast(I32), xg[:, t0:t1, COL_ROW], float(NO_ROW), None,
                                ALU.add).then_inc(rows_ready, 1)

            v.wait_ge(table_ready, 1)
            v.wait_ge(w1_in, 48)
            v.wait_ge(xg0_ready, 1)
            normalise(0, 0)
            expert_weights(0, 0)
            v.wait_ge(xg0_ready, 2)
            normalise(1, 1)
            expert_weights(1, 1)
            slot_rows(0, BY_PE)
            v.wait_ge(b2_in, 16)

            def step(t, k, more=2):
                if more >= 1:
                    expert_weights(t + 2, k)
                finish(t, k)
                if more >= 2:
                    normalise(t + 4, k)

            expert_weights(2, 0)
            v.wait_ge(slots_in0, 16)
            normalise(2, 0)
            expert_weights(3, 1)
            finish(0, 0)
            normalise(3, 1)
            v.wait_ge(slots_in1, 16)
            normalise(4, 0)
            slot_rows(BY_PE, SLOT_TILES)
            finish(1, 1)
            normalise(5, 1)
            with v.Fori(1, SLOT_TILES // 2 - 2) as pair:
                step(2 * pair, 0)
                step(2 * pair + 1, 1)
            step(SLOT_TILES - 4, 0, 1)
            step(SLOT_TILES - 3, 1, 1)
            step(SLOT_TILES - 2, 0, 0)
            step(SLOT_TILES - 1, 1, 0)

        @block.scalar
        def _(act):
            mark, _ = tally(act_s)
            h96 = slice(0, HALF)
            act.dma_start(tokw_sb, tok_w.rearrange("(c p) d -> p c d", p=128)).then_inc(tokw_in, 16)
            act.dma_start(tokb_row[:, :], tok_b.partition_broadcast(128)).then_inc(tokb_in, 16)
            act.dma_start(b_row[0:6, :], b_qkv.rearrange("(c p) -> c p", p=HALF)).then_inc(bq_in, 16)
            act.dma_start(b_row[6:8, :], b_proj.rearrange("(c p) -> c p", p=HALF)).then_inc(bq_in, 16)
            act.dma_start(bs_row[:, :], bs.partition_broadcast(128)).then_inc(small_in, 16)
            act.dma_start(ws_sb[:, :, :], ws.rearrange("(k p) e -> p k e", p=HALF)).then_inc(small_in, 16)
            act.dma_start(pay[0:B, NT - 1, 0:C], cls_tok.rearrange("a b c -> (a b c)").partition_broadcast(B)).then_inc(small_in, 16)

            def pack(j):
                act.wait_ge(x_in[j // SIDE], 16)
                act.copy(x_c[:, j, :].rearrange("p (r s) -> p r s", s=SEG),
                         x_sb[:, j // SIDE, :, j % SIDE, :]).then_inc(packed_a, 1)

            def patches_out(j):
                act.wait_ge(xt_psum, j + 1)
                if j >= 2:
                    act.wait_ge(embed_psum, j - 1)
                act.copy(x_t[j % 2][:, 0:X_SPLIT, :].rearrange("p k t -> p (k t)"),
                         ps[:, 2 * (j % 2), 0:X_SPLIT * 128]).then_inc(xt_ready_a, 1)

            pack(1)
            patches_out(0)
            pack(3)
            patches_out(1)
            patches_out(2)
            pack(4)
            patches_out(3)
            pack(5)
            pack(6)
            patches_out(4)
            pack(7)
            act.wait_ge(consts, CONSTS)
            act.wait_ge(w_inv_ready, 1)
            for c in range(8):
                act.activation(w_v[h96, c], w_row[h96, c], ACT.Identity, bias=magic_c[h96],
                               scale=w_inv[h96, c:c + 1]).then_inc(w_rounded, 1)
                if c % 4 == 1:
                    patches_out(5 + c // 4)
            patches_out(7)

            def token_view(q, i):
                tiles, half = XG[i]
                if half is None:
                    return x_part[h96, q].rearrange("p k (b n) -> p k b n", n=N)[:, :, :, 0]
                t = tiles[0] // SIDE
                return x_part[h96, q, half, t * T // 2:(t + 1) * T // 2].rearrange(
                    "p (b n) -> p b n", n=N)[:, :, 1:N].rearrange("p b (h w) -> p w b h", w=SIDE)

            def grouped(ap, i):
                if XG[i][1] is None:
                    return ap[h96, 0:2 * B].rearrange("p (w b) -> p w b", w=2)
                return ap[h96, 0:512].rearrange("p (w b h) -> p w b h", w=SIDE, b=B // 2)

            def highest(i):
                act.wait_ge(xnt_psum, i + 1)
                act.copy(token_view(0, i), grouped(ps[:, XG_BANK[i], :], i)).then_inc(hi_done, 1)

            def middle(i):
                act.wait_ge(res_done, i + 1)
                act.copy(token_view(1, i), grouped(residue[i % 2], i)).then_inc(mid_done, 1)

            def y_out_of(s, c):
                a, b = PIECES[s]
                bank, col = y_bank(c, s)
                act.wait_ge(y_psum, 6 * s + c + 1 if s != 1 else 12)
                act.activation(y_sb[h96, c, a:b], ps[h96, bank, col:col + b - a], ACT.Identity,
                               bias=bq_col[h96, c:c + 1], scale=w_scale[h96, c:c + 1]).then_inc(y_ready, 1)

            highest(0)
            highest(1)
            middle(0)
            highest(2)
            middle(1)
            middle(2)
            act.wait_ge(bq_ready, 1)
            act.wait_ge(embed_psum, 8)
            for c in range(3):
                y_out_of(0, c)
            highest(3)
            highest(4)
            middle(3)
            middle(4)
            for c in range(3, 6):
                y_out_of(0, c)
            for s in (1, 2):
                for c in range(6):
                    y_out_of(s, c)

            def bound(q, which):
                act.wait_ge(bound_in, which)
                act.activation(q[2], q[3], ACT.Identity, bias=magic_c, scale=q[1]).then_inc(bound_done, 1)

            def h0_out(i):
                m = min(4, 2 * NT - 4 * i) * 128
                act.wait_ge(h0_psum, i + 1)
                act.copy(h0_t[h96].rearrange("p j k t -> p (j k t)")[:, 512 * i:512 * i + m],
                         ps[h96, H0_BANK[i], 0:m]).then_inc(h0_ready, 1)

            for i in range(4):
                h0_out(i)

            bound(q_y, 1)
            act.wait_ge(y_ready, 18)
            part = GH * GI * N
            for n, (c, a, b) in enumerate(((0, 0, part), (2, 0, part), (0, part, T), (2, part, T), (3, 0, T), (1, 0, T),
                                           (4, 0, T), (5, 0, T))):
                if n == 2:
                    h0_out(4)
                act.activation(y_sb[h96, c, a:b], y_sb[h96, c, a:b], ACT.Identity, bias=magic_c[h96],
                               scale=q_y[1][h96]).then_inc(y_rounded, 1)

            act.wait_ge(lg0_psum, 1)
            act.copy(lg0[:, :, :],
                     ps[:, LG0_BANK, 0:NT * E].rearrange("p (j e) -> p j e", e=E)).then_inc(lg0_ready, 1)

            def scaled(out, in_, scale, _, op):
                return act.activation(out, in_, ACT.Copy, scale=scale)

            act.wait_ge(k_ready, 1)
            spread(scaled, k_exp, kv_t, 1, 1, 0, B, range(K_HEADS, HG), k_exp_ready_a, mark)
            act.wait_ge(v_ready, 1)
            spread(scaled, v_exp_t, kv_t, 2, 0, 0, B, range(V_HEADS[1], HG), v_exp_t_ready_a, mark)
            spread(scaled, v_exp_t, kv_t, 3, 1, 0, B, range(HG), v_exp_t_ready_a, mark)

            def v_out(n):
                g, b0 = n // 7, (n % 7) * VB
                m = min(VB, B - b0)
                act.wait_ge(v_psum, n + 1)
                act.copy(v_exp[0:M, g, b0:b0 + m, :],
                         bank_b(5 + n % 3)[0:M, 0:m * HALF].rearrange("p (b c) -> p b c", c=HALF)).then_inc(v_exp_ready, 1)

            LH = L // 2
            V_, XI, _, _ = soft
            VI, _, QQ, _ = soft_i
            _, E_, Y0, _ = soft
            sv = ps[0:R, 0:5, 0:4 * M].rearrange("p b (l m) -> p b l m", m=N)
            v3 = V_[0:R].rearrange("p (b l) m -> p b l m", b=5)
            bound(q_a, 2)
            act.activation(row_max[0:R], row_max[0:R], ACT.Identity, bias=magic_c[0:R],
                           scale=q_a[1][0:R]).then_inc(attn_scaled, 1)
            act.activation(v3[:, 0:2], sv[:, 0:2], ACT.Identity, bias=magic_c[0:R], scale=q_a[1][0:R])
            act.activation(v3[:, 2], sv[:, 2], ACT.Identity, bias=magic_c[0:R],
                           scale=q_a[1][0:R]).then_inc(attn_scaled, 1)
            act.activation(v3[:, 3:5], sv[:, 3:5], ACT.Identity, bias=magic_c[0:R],
                           scale=q_a[1][0:R]).then_inc(attn_scaled, 1)
            v_out(0)
            v_out(1)
            for i in range(2):
                act.wait_ge(xi_ready, i + 1)
                act.activation(QQ[0:R, i * LH:(i + 1) * LH], XI[0:R, i * LH:(i + 1) * LH], ACT.Identity,
                               bias=q_bias[0:R], scale=x0_inv[0:R]).then_inc(q_ready, 1)
                act.wait_ge(q_ready, i + 1)
                act.activation(VI[0:R, i * LH:(i + 1) * LH], QQ[0:R, i * LH:(i + 1) * LH], ACT.Identity,
                               bias=exp_c[0:R], scale=-8388608.0).then_inc(power_ready, 1)
                if i == 0:
                    v_out(2)
            for i in range(2):
                if i == 1:
                    v_out(3)
                    v_out(4)
                act.wait_ge(e_ready, i + 1)
                n = mark(act.activation(Y0[0:R, i * LH:(i + 1) * LH], E_[0:R, i * LH:(i + 1) * LH], ACT.Ln))
            act.wait_ge(act_s, n)
            for i in range(2):
                act.activation(Y0[0:R, i * LH:(i + 1) * LH], Y0[0:R, i * LH:(i + 1) * LH], ACT.Exp,
                               scale=-1.0).then_inc(y0_ready, 1)
            for n in range(5, 14):
                v_out(n)
            act.wait_ge(pt_psum, 1)
            probs_out(act.copy, 0).then_inc(pt_ready_a, 1)
            act.wait_ge(pt_psum, 2)
            probs_out(act.copy, 1).then_inc(pt_ready_a, 1)
            act.wait_ge(pt_psum, 3)
            probs_out(act.copy, 2).then_inc(pt_ready_a, 1)
            bound(q_o, 3)
            act.wait_ge(av_psum, 4)
            for t in range(2):
                for g in range(2):
                    i = 4 * t + 2 * g
                    act.activation(o_v[h96, g, t * T // 2:(t + 1) * T // 2].rearrange("p (s t) -> p s t", s=2),
                                   ps[h96, i:i + 2, 0:AVI * N], ACT.Identity, bias=magic_c[h96],
                                   scale=q_o[1][h96]).then_inc(o_rounded, 1)

            act.wait_ge(proj_scale_ready, 1)
            for i, (a, b, bank) in enumerate(PROJ):
                for m in range(2):
                    act.wait_ge(proj_psum, 2 * i + m + 1)
                    act.activation(proj_t[h96, m, a:b], ps[h96, bank + m, 0:b - a], ACT.Identity,
                                   bias=bq_col[h96, 6 + m:7 + m], scale=proj_scale[h96, m:m + 1]).then_inc(proj_ready, 1)
            bound(q_p, 4)
            act.wait_ge(proj_ready, 6)
            for a, b, _ in PROJ[0::2]:
                act.activation(proj_t[h96, :, a:b], proj_t[h96, :, a:b], ACT.Identity, bias=magic_c[h96],
                               scale=q_p[1][h96]).then_inc(proj_rounded, 1)

            act.wait_ge(lg_max, 1)
            act.activation(ex[:, :, :], ex[:, :, :], ACT.Exp).then_inc(ex_ready, 1)

            def tokens_out(t, k):
                act.wait_ge(xgt_psum, t + 1)
                if not isinstance(t, int) or t >= 2:
                    act.wait_ge(g1_psum, t - 1)
                act.copy(xg_t[k][h96].rearrange("p c t -> p (c t)"), ps[h96, 7, 0:256]).then_inc(xgt_ready, 1)

            def gelu(t, k):
                act.wait_ge(g1_psum, t + 1)
                if not isinstance(t, int) or t >= 2:
                    act.wait_ge(g2_psum, t - 1)
                act.activation(h_t[k].rearrange("p (a f) t -> p a (f t)", a=2), ps[:, 2 * k:2 * k + 2, 0:FH],
                               ACT.Gelu).then_inc(h_ready, 1)

            for t in range(BY_PE):
                act.wait_ge(xg0_psum, t + 1)
                act.copy(xg[:, t, :], ps[:, 2 + t, 0:PAYW]).then_inc(xg0_ready, 1)
            tokens_out(0, 0)
            tokens_out(1, 1)
            gelu(0, 0)
            gelu(1, 1)
            tokens_out(2, 0)
            tokens_out(3, 1)
            with act.Fori(2, SLOT_TILES - 2, 2) as t:
                gelu(t, 0)
                tokens_out(t + 2, 0)
                gelu(t + 1, 1)
                tokens_out(t + 3, 1)
            gelu(SLOT_TILES - 2, 0)
            gelu(SLOT_TILES - 1, 1)


_INS = ['x', 'cls_tok', 'L0_tok_W', 'L0_tok_b', 'L0_attn_w_qkv', 'L0_attn_b_qkv', 'L0_attn_w_proj', 'L0_attn_b_proj',
        'L0_ffn_Ws', 'L0_ffn_bs', 'L0_ffn_W1', 'L0_ffn_b1', 'L0_ffn_W2', 'L0_ffn_b2']
_OUTS = [((64, 17, 192), 'float32')]


def kernel(**inputs):
    import numpy as _np
    import concourse.bacc as _bacc
    from concourse import mybir as _mybir
    from concourse.bass_utils import run_bass_kernel_spmd as _run

    nc = _bacc.Bacc("TRN2", target_bir_lowering=False, num_devices=1)
    arrays, args = {}, []
    for name in _INS:
        a = _np.ascontiguousarray(inputs[name])
        arrays[f"in_{name}_dram"] = a
        args.append(nc.dram_tensor(f"in_{name}_dram", a.shape, _mybir.dt.from_np(a.dtype), kind="ExternalInput").ap())
    for i, (shape, dtype) in enumerate(_OUTS):
        dt = _mybir.dt.from_np(_np.dtype(dtype))
        args.append(nc.dram_tensor(f"out_{i}_dram", shape, dt, kind="ExternalOutput").ap())
    vit_tower(nc, *args)
    r = _run(nc, [arrays], core_ids=[0])
    return r.results[0]["out_0_dram"]
```
